# Optimizing a Trainium2 kernel written in Bass

```python
import numpy as np
import jax
import jax.numpy as jnp

def _softmax(x, axis=-1):
    return jax.nn.softmax(x, axis=axis)

def _gelu(x):
    return jax.nn.gelu(x, approximate=True)

def _silu(x):
    return jax.nn.silu(x)

def _sigmoid(x):
    return jax.nn.sigmoid(x)

def _layernorm(x, axis=-1, eps=1e-05):
    m = jnp.mean(x, axis=axis, keepdims=True)
    v = jnp.var(x, axis=axis, keepdims=True)
    return (x - m) / jnp.sqrt(v + eps)

def _scatter_add(tgt, idx, src, axis=0):
    return tgt.at[idx].add(src)

def _segment_sum(src, seg, n):
    return jax.ops.segment_sum(src, seg, n)
kernel_name = 'mk_seq_postln_d4_jaxref_r8_6b11e8'

def setup_inputs(seed: int=0):
    np.random.seed(seed)
    _w = jnp.asarray

    def _L0_attn_setup():
        import jax, jax.numpy as jnp
        import numpy as np
        import math
        CTX_LEN = 96
        N_EMBD = 128

        def _depthwise_causal_conv(z, w, T, C):
            return jax.lax.conv_general_dilated(z, w, window_strides=(1,), padding=[(T - 1, 0)], feature_group_count=C, dimension_numbers=('NCH', 'OIH', 'NCH'))
        key = jax.random.key(seed)
        ks = jax.random.split(key, 8)
        B, T, C = (8, CTX_LEN, N_EMBD)
        x = jax.random.normal(ks[0], (B, T, C), dtype=jnp.float32)
        time_decay = jax.random.normal(ks[1], (C, 1), dtype=jnp.float32) * 0.1
        time_first = jnp.full((C, 1), math.log(0.3), dtype=jnp.float32)
        time_mix = jax.random.uniform(ks[2], (1, 1, C), dtype=jnp.float32)
        s = 0.02
        Wk = jax.random.normal(ks[3], (C, C), dtype=jnp.float32) * s
        Wv = jax.random.normal(ks[4], (C, C), dtype=jnp.float32) * s
        Wr = jax.random.normal(ks[5], (C, C), dtype=jnp.float32) * s
        Wo = jax.random.normal(ks[6], (C, C), dtype=jnp.float32) * s
        return {'x': x, 'time_decay': time_decay, 'time_first': time_first, 'time_mix': time_mix, 'Wk': Wk, 'Wv': Wv, 'Wr': Wr, 'Wo': Wo}
    _L0_attn_in = _L0_attn_setup()

    def _L0_ffn_setup():
        import jax, jax.numpy as jnp
        import numpy as np
        NUM_OPS, B, T, D = (8, 8, 64, 128)
        key = jax.random.key(seed)
        k1, k2, k3, k4 = jax.random.split(key, 4)
        x = jax.random.normal(k1, (B, T, D), dtype=jnp.float32)
        W = jax.random.normal(k2, (NUM_OPS, D, D), dtype=jnp.float32) * 0.02
        b = jnp.zeros((NUM_OPS, D), dtype=jnp.float32)
        logits = 0.001 * jax.random.normal(k3, (NUM_OPS,), dtype=jnp.float32)
        u = jax.random.uniform(k4, (NUM_OPS,), dtype=jnp.float32, minval=1e-06, maxval=1.0 - 1e-06)
        return {'x': x, 'W': W, 'b': b, 'logits': logits, 'u': u}
    _L0_ffn_in = _L0_ffn_setup()

    def _L1_attn_setup():
        import jax, jax.numpy as jnp
        import numpy as np
        import math
        B, S, E, H = (2, 256, 128, 16)
        D = E // H
        key = jax.random.key(seed)
        ks = jax.random.split(key, 5)
        scale_p = 1.0 / math.sqrt(D)
        return {'x': jax.random.normal(ks[0], (B, S, E), dtype=jnp.float32), 'Wq': jax.random.normal(ks[1], (D, D), dtype=jnp.float32) * scale_p, 'Wk': jax.random.normal(ks[2], (D, D), dtype=jnp.float32) * scale_p, 'Wv': jax.random.normal(ks[3], (D, D), dtype=jnp.float32) * scale_p, 'W_out': jax.random.normal(ks[4], (E, E), dtype=jnp.float32) * (1.0 / math.sqrt(E)), 'b_out': jnp.zeros((E,), dtype=jnp.float32)}
    _L1_attn_in = _L1_attn_setup()

    def _L1_ffn_setup():
        import jax, jax.numpy as jnp
        import numpy as np
        from jax import lax
        D = 128
        H = 176
        E = 8
        K = 2
        ROUTER_SCALE = 1.0

        def _expert(x, w1, b1, w3, b3, w2, b2):
            h = jax.nn.silu((x @ w1 + b1) * (x @ w3 + b3))
            return h @ w2 + b2
        key = jax.random.key(seed)
        ks = jax.random.split(key, 16)
        s = 0.02
        inp = {'x': jax.random.normal(ks[0], (2, 256, D), dtype=jnp.float32), 'gate_w': jax.random.normal(ks[1], (E, D), dtype=jnp.float32) * s, 'gate_b': jax.random.normal(ks[2], (E,), dtype=jnp.float32) * s, 'w1': jax.random.normal(ks[3], (E, D, H), dtype=jnp.float32) * s, 'b1': jax.random.normal(ks[4], (E, H), dtype=jnp.float32) * s, 'w3': jax.random.normal(ks[5], (E, D, H), dtype=jnp.float32) * s, 'b3': jax.random.normal(ks[6], (E, H), dtype=jnp.float32) * s, 'w2': jax.random.normal(ks[7], (E, H, D), dtype=jnp.float32) * s, 'b2': jax.random.normal(ks[8], (E, D), dtype=jnp.float32) * s, 'sw1': jax.random.normal(ks[9], (D, H), dtype=jnp.float32) * s, 'sb1': jax.random.normal(ks[10], (H,), dtype=jnp.float32) * s, 'sw3': jax.random.normal(ks[11], (D, H), dtype=jnp.float32) * s, 'sb3': jax.random.normal(ks[12], (H,), dtype=jnp.float32) * s, 'sw2': jax.random.normal(ks[13], (H, D), dtype=jnp.float32) * s, 'sb2': jax.random.normal(ks[14], (D,), dtype=jnp.float32) * s}
        return inp
    _L1_ffn_in = _L1_ffn_setup()

    def _L2_attn_setup():
        import jax, jax.numpy as jnp
        import numpy as np
        import math
        D_MODEL = 128
        NUM_HEADS = 16
        THETA = 10000.0

        def _rope(x, theta):
            n, d_k = (x.shape[-2], x.shape[-1])
            powers = jnp.arange(0, d_k, 2, dtype=jnp.float32) / d_k
            freqs = 1.0 / theta ** powers
            t = jnp.arange(n, dtype=jnp.float32)
            angles = jnp.outer(t, freqs)
            cos = jnp.cos(angles).astype(x.dtype)
            sin = jnp.sin(angles).astype(x.dtype)
            x_even = x[..., 0::2]
            x_odd = x[..., 1::2]
            rot_even = x_even * cos - x_odd * sin
            rot_odd = x_even * sin + x_odd * cos
            return jnp.stack([rot_even, rot_odd], axis=-1).reshape(x.shape)
        key = jax.random.key(seed)
        ks = jax.random.split(key, 5)
        B, N, D = (2, 256, D_MODEL)
        std = math.sqrt(2.0 / (D + D))
        x = jax.random.normal(ks[0], (B, N, D), dtype=jnp.float32)
        wq = jax.random.normal(ks[1], (D, D), dtype=jnp.float32) * std
        wk = jax.random.normal(ks[2], (D, D), dtype=jnp.float32) * std
        wv = jax.random.normal(ks[3], (D, D), dtype=jnp.float32) * std
        wo = jax.random.normal(ks[4], (D, D), dtype=jnp.float32) * std
        return {'x': x, 'wq': wq, 'wk': wk, 'wv': wv, 'wo': wo}
    _L2_attn_in = _L2_attn_setup()

    def _L2_ffn_setup():
        import jax, jax.numpy as jnp
        import numpy as np
        HID = 128
        NH = 16
        NKV = 4
        HD = HID // NH
        E = 8
        TOPK = 2
        FFN = 256
        EPS = 1e-05
        THETA = 10000.0

        def _rmsnorm(x, w):
            var = jnp.mean(x * x, axis=-1, keepdims=True)
            return x * jax.lax.rsqrt(var + EPS) * w

        def _rope_tables(S):
            inv_freq = 1.0 / THETA ** (jnp.arange(0, HD, 2, dtype=jnp.float32) / HD)
            freqs = jnp.arange(S, dtype=jnp.float32)[:, None] * inv_freq[None, :]
            emb = jnp.concatenate([freqs, freqs], axis=-1)
            return (jnp.cos(emb), jnp.sin(emb))

        def _apply_rope(t, cos, sin):
            t1, t2 = jnp.split(t, 2, axis=-1)
            rot = jnp.concatenate([-t2, t1], axis=-1)
            return t * cos[None, :, None, :] + rot * sin[None, :, None, :]
        key = jax.random.key(seed)
        ks = jax.random.split(key, 6)
        B, S = (1, 256)
        x = jax.random.normal(ks[0], (B, S, HID), dtype=jnp.float32)
        wqkv = jax.random.normal(ks[1], ((NH + 2 * NKV) * HD, HID), dtype=jnp.float32) * 0.02
        wo = jax.random.normal(ks[2], (HID, NH * HD), dtype=jnp.float32) * 0.02
        gate_w = jax.random.normal(ks[3], (E, HID), dtype=jnp.float32) * 0.02
        w13 = jax.random.normal(ks[4], (E, 2 * FFN, HID), dtype=jnp.float32) * 0.02
        w2 = jax.random.normal(ks[5], (E, HID, FFN), dtype=jnp.float32) * 0.02
        return {'x': x, 'ln1_w': jnp.ones((HID,), jnp.float32), 'ln2_w': jnp.ones((HID,), jnp.float32), 'wqkv': wqkv, 'wo': wo, 'gate_w': gate_w, 'w13': w13, 'w2': w2}
    _L2_ffn_in = _L2_ffn_setup()

    def _L3_attn_setup():
        import math
        import jax, jax.numpy as jnp
        import numpy as np
        D_MODEL = 128
        NUM_HEADS = 16
        NUM_KV_HEADS = 4
        D_HEAD = D_MODEL // NUM_HEADS
        SEQ = 512
        BATCH = 1
        key = jax.random.key(seed)
        ks = jax.random.split(key, 9)
        s = 0.02
        dkv = NUM_KV_HEADS * D_HEAD
        inp = {'qkv': jax.random.normal(ks[0], (BATCH, SEQ, D_MODEL), jnp.float32), 'Wq': jax.random.normal(ks[1], (D_MODEL, D_MODEL), jnp.float32) * s, 'bq': jnp.zeros((D_MODEL,), jnp.float32), 'Wk': jax.random.normal(ks[2], (D_MODEL, dkv), jnp.float32) * s, 'bk': jnp.zeros((dkv,), jnp.float32), 'Wv': jax.random.normal(ks[3], (D_MODEL, dkv), jnp.float32) * s, 'bv': jnp.zeros((dkv,), jnp.float32), 'Wo': jax.random.normal(ks[4], (D_MODEL, D_MODEL), jnp.float32) * s, 'bo': jnp.zeros((D_MODEL,), jnp.float32), 'slopes': jnp.exp2(-jnp.linspace(0.0, 7.0, NUM_HEADS)).astype(jnp.float32)}
        return inp
    _L3_attn_in = _L3_attn_setup()

    def _L3_ffn_setup():
        import jax, jax.numpy as jnp
        import numpy as np
        LN_EPS = 1e-05

        def layer_norm(x, g, b):
            mu = jnp.mean(x, axis=-1, keepdims=True)
            var = jnp.mean(jnp.square(x - mu), axis=-1, keepdims=True)
            return (x - mu) * jax.lax.rsqrt(var + LN_EPS) * g + b

        def ternary_quant(w):
            scale = 1.0 / jnp.clip(jnp.mean(jnp.abs(w)), 1e-05)
            wq = jnp.clip(jnp.round(w * scale), -1.0, 1.0) / scale
            return w + jax.lax.stop_gradient(wq - w)
        key = jax.random.key(seed)
        ks = jax.random.split(key, 3)
        dim, hidden = (128, 512)
        B, S = (8, 128)
        x = jax.random.normal(ks[0], (B, S, dim), dtype=jnp.float32)
        w1 = jax.random.normal(ks[1], (hidden, dim), dtype=jnp.float32) * 0.02
        w2 = jax.random.normal(ks[2], (dim, hidden), dtype=jnp.float32) * 0.02
        return {'x': x, 'ln1_g': jnp.ones((dim,), jnp.float32), 'ln1_b': jnp.zeros((dim,), jnp.float32), 'w1': w1, 'b1': jnp.zeros((hidden,), jnp.float32), 'ln2_g': jnp.ones((hidden,), jnp.float32), 'ln2_b': jnp.zeros((hidden,), jnp.float32), 'w2': w2, 'b2': jnp.zeros((dim,), jnp.float32)}
    _L3_ffn_in = _L3_ffn_setup()
    _d = {'L0_attn_x': _L0_attn_in['x'], 'L0_attn_time_decay': _L0_attn_in['time_decay'], 'L0_attn_time_first': _L0_attn_in['time_first'], 'L0_attn_time_mix': _L0_attn_in['time_mix'], 'L0_attn_Wk': _L0_attn_in['Wk'], 'L0_attn_Wv': _L0_attn_in['Wv'], 'L0_attn_Wr': _L0_attn_in['Wr'], 'L0_attn_Wo': _L0_attn_in['Wo'], 'L0_ffn_W': _L0_ffn_in['W'], 'L0_ffn_b': _L0_ffn_in['b'], 'L0_ffn_logits': _L0_ffn_in['logits'], 'L0_ffn_u': _L0_ffn_in['u'], 'L1_attn_Wq': _L1_attn_in['Wq'], 'L1_attn_Wk': _L1_attn_in['Wk'], 'L1_attn_Wv': _L1_attn_in['Wv'], 'L1_attn_W_out': _L1_attn_in['W_out'], 'L1_attn_b_out': _L1_attn_in['b_out'], 'L1_ffn_gate_w': _L1_ffn_in['gate_w'], 'L1_ffn_gate_b': _L1_ffn_in['gate_b'], 'L1_ffn_w1': _L1_ffn_in['w1'], 'L1_ffn_b1': _L1_ffn_in['b1'], 'L1_ffn_w3': _L1_ffn_in['w3'], 'L1_ffn_b3': _L1_ffn_in['b3'], 'L1_ffn_w2': _L1_ffn_in['w2'], 'L1_ffn_b2': _L1_ffn_in['b2'], 'L1_ffn_sw1': _L1_ffn_in['sw1'], 'L1_ffn_sb1': _L1_ffn_in['sb1'], 'L1_ffn_sw3': _L1_ffn_in['sw3'], 'L1_ffn_sb3': _L1_ffn_in['sb3'], 'L1_ffn_sw2': _L1_ffn_in['sw2'], 'L1_ffn_sb2': _L1_ffn_in['sb2'], 'L2_attn_wq': _L2_attn_in['wq'], 'L2_attn_wk': _L2_attn_in['wk'], 'L2_attn_wv': _L2_attn_in['wv'], 'L2_attn_wo': _L2_attn_in['wo'], 'L2_ffn_ln1_w': _L2_ffn_in['ln1_w'], 'L2_ffn_ln2_w': _L2_ffn_in['ln2_w'], 'L2_ffn_wqkv': _L2_ffn_in['wqkv'], 'L2_ffn_wo': _L2_ffn_in['wo'], 'L2_ffn_gate_w': _L2_ffn_in['gate_w'], 'L2_ffn_w13': _L2_ffn_in['w13'], 'L2_ffn_w2': _L2_ffn_in['w2'], 'L3_attn_Wq': _L3_attn_in['Wq'], 'L3_attn_bq': _L3_attn_in['bq'], 'L3_attn_Wk': _L3_attn_in['Wk'], 'L3_attn_bk': _L3_attn_in['bk'], 'L3_attn_Wv': _L3_attn_in['Wv'], 'L3_attn_bv': _L3_attn_in['bv'], 'L3_attn_Wo': _L3_attn_in['Wo'], 'L3_attn_bo': _L3_attn_in['bo'], 'L3_attn_slopes': _L3_attn_in['slopes'], 'L3_ffn_ln1_g': _L3_ffn_in['ln1_g'], 'L3_ffn_ln1_b': _L3_ffn_in['ln1_b'], 'L3_ffn_w1': _L3_ffn_in['w1'], 'L3_ffn_b1': _L3_ffn_in['b1'], 'L3_ffn_ln2_g': _L3_ffn_in['ln2_g'], 'L3_ffn_ln2_b': _L3_ffn_in['ln2_b'], 'L3_ffn_w2': _L3_ffn_in['w2'], 'L3_ffn_b2': _L3_ffn_in['b2']}
    _x0 = _d['L0_attn_x']
    _d['L0_attn_x'] = jax.random.normal(jax.random.fold_in(jax.random.key(seed), 1), (4, 512, 128), dtype=_x0.dtype)
    del _x0
    return _d

def reference(L0_attn_x, L0_attn_time_decay, L0_attn_time_first, L0_attn_time_mix, L0_attn_Wk, L0_attn_Wv, L0_attn_Wr, L0_attn_Wo, L0_ffn_W, L0_ffn_b, L0_ffn_logits, L0_ffn_u, L1_attn_Wq, L1_attn_Wk, L1_attn_Wv, L1_attn_W_out, L1_attn_b_out, L1_ffn_gate_w, L1_ffn_gate_b, L1_ffn_w1, L1_ffn_b1, L1_ffn_w3, L1_ffn_b3, L1_ffn_w2, L1_ffn_b2, L1_ffn_sw1, L1_ffn_sb1, L1_ffn_sw3, L1_ffn_sb3, L1_ffn_sw2, L1_ffn_sb2, L2_attn_wq, L2_attn_wk, L2_attn_wv, L2_attn_wo, L2_ffn_ln1_w, L2_ffn_ln2_w, L2_ffn_wqkv, L2_ffn_wo, L2_ffn_gate_w, L2_ffn_w13, L2_ffn_w2, L3_attn_Wq, L3_attn_bq, L3_attn_Wk, L3_attn_bk, L3_attn_Wv, L3_attn_bv, L3_attn_Wo, L3_attn_bo, L3_attn_slopes, L3_ffn_ln1_g, L3_ffn_ln1_b, L3_ffn_w1, L3_ffn_b1, L3_ffn_ln2_g, L3_ffn_ln2_b, L3_ffn_w2, L3_ffn_b2):

    def _L0_attn_ref(x, time_decay, time_first, time_mix, Wk, Wv, Wr, Wo):
        import jax, jax.numpy as jnp
        import numpy as np
        import math
        CTX_LEN = 96
        N_EMBD = 128

        def _depthwise_causal_conv(z, w, T, C):
            return jax.lax.conv_general_dilated(z, w, window_strides=(1,), padding=[(T - 1, 0)], feature_group_count=C, dimension_numbers=('NCH', 'OIH', 'NCH'))
        B, T, C = x.shape
        xs = jnp.pad(x, ((0, 0), (1, 0), (0, 0)))[:, :-1]
        xm = x * time_mix + xs * (1.0 - time_mix)
        k = jnp.einsum('btc,dc->bdt', xm, Wk)
        v = jnp.einsum('btc,dc->bdt', xm, Wv)
        r = jnp.einsum('btc,dc->btd', xm, Wr)
        k = jnp.exp(jnp.minimum(k, 60.0))
        kv = k * v
        time_curve = (jnp.arange(T - 1, dtype=jnp.float32) - (T - 2))[None, :]
        time_w = jnp.concatenate([jnp.exp(time_decay) * time_curve, time_first], axis=-1)
        w = jnp.exp(time_w)[:, None, :]
        wkv = _depthwise_causal_conv(kv, w, T, C)
        wk = _depthwise_causal_conv(k, w, T, C) + 1e-09
        rwkv = jax.nn.sigmoid(r) * jnp.swapaxes(wkv / wk, 1, 2)
        return jnp.einsum('btc,dc->btd', rwkv, Wo)

    def _L0_ffn_ref(x, W, b, logits, u):
        import jax, jax.numpy as jnp
        import numpy as np
        NUM_OPS, B, T, D = (8, 8, 64, 128)
        gumbel = -jnp.log(-jnp.log(u))
        idx = jnp.argmax(jax.nn.log_softmax(logits) + gumbel)
        out = jnp.einsum('btd,de->bte', x, W[idx]) + b[idx]
        return out

    def _L1_attn_ref(x, Wq, Wk, Wv, W_out, b_out):
        import jax, jax.numpy as jnp
        import numpy as np
        import math
        B, S, E, H = (2, 256, 128, 16)
        D = E // H
        b, s, e = x.shape
        xh = x.reshape(b, s, H, D)
        q = jnp.einsum('bshd,ed->bshe', xh, Wq)
        k = jnp.einsum('bshd,ed->bshe', xh, Wk)
        v = jnp.einsum('bshd,ed->bshe', xh, Wv)
        energy = jnp.einsum('bqhd,bkhd->bhqk', q, k) / jnp.sqrt(jnp.float32(e))
        attn = jax.nn.softmax(energy, axis=-1)
        out = jnp.einsum('bhqk,bkhd->bqhd', attn, v).reshape(b, s, e)
        return out @ W_out.T + b_out

    def _L1_ffn_ref(x, gate_w, gate_b, w1, b1, w3, b3, w2, b2, sw1, sb1, sw3, sb3, sw2, sb2):
        import jax, jax.numpy as jnp
        import numpy as np
        from jax import lax
        D = 128
        H = 176
        E = 8
        K = 2
        ROUTER_SCALE = 1.0

        def _expert(x, w1, b1, w3, b3, w2, b2):
            h = jax.nn.silu((x @ w1 + b1) * (x @ w3 + b3))
            return h @ w2 + b2
        shape = x.shape
        xf = x.reshape(-1, D)
        T = xf.shape[0]
        scores = jax.nn.softmax(xf @ gate_w.T, axis=-1)
        biased = scores + gate_b
        _, idx = lax.top_k(biased, K)
        w = jnp.take_along_axis(scores, idx, axis=-1) * ROUTER_SCALE
        rw = jnp.zeros((T, E), dtype=xf.dtype).at[jnp.arange(T)[:, None], idx].add(w)
        h = jax.nn.silu((jnp.einsum('td,edh->teh', xf, w1) + b1) * (jnp.einsum('td,edh->teh', xf, w3) + b3))
        oe = jnp.einsum('teh,ehd->ted', h, w2) + b2
        y = jnp.einsum('te,ted->td', rw, oe)
        z = _expert(xf, sw1, sb1, sw3, sb3, sw2, sb2)
        return (y + z).reshape(shape)

    def _L2_attn_ref(x, wq, wk, wv, wo):
        import jax, jax.numpy as jnp
        import numpy as np
        import math
        D_MODEL = 128
        NUM_HEADS = 16
        THETA = 10000.0

        def _rope(x, theta):
            n, d_k = (x.shape[-2], x.shape[-1])
            powers = jnp.arange(0, d_k, 2, dtype=jnp.float32) / d_k
            freqs = 1.0 / theta ** powers
            t = jnp.arange(n, dtype=jnp.float32)
            angles = jnp.outer(t, freqs)
            cos = jnp.cos(angles).astype(x.dtype)
            sin = jnp.sin(angles).astype(x.dtype)
            x_even = x[..., 0::2]
            x_odd = x[..., 1::2]
            rot_even = x_even * cos - x_odd * sin
            rot_odd = x_even * sin + x_odd * cos
            return jnp.stack([rot_even, rot_odd], axis=-1).reshape(x.shape)
        B, N, D = x.shape
        H = NUM_HEADS
        d_k = D // H

        def split_heads(t):
            return t.reshape(B, N, H, d_k).transpose(0, 2, 1, 3)
        Q = split_heads(x @ wq.T)
        K = split_heads(x @ wk.T)
        V = split_heads(x @ wv.T)
        Q = _rope(Q, THETA)
        K = _rope(K, THETA)
        scale = 1.0 / math.sqrt(d_k)
        scores = jnp.einsum('bhqd,bhkd->bhqk', Q, K) * scale
        causal_mask = jnp.triu(jnp.ones((N, N), dtype=bool), k=1)
        scores = jnp.where(causal_mask, -jnp.inf, scores)
        attn = jax.nn.softmax(scores, axis=-1)
        out = jnp.einsum('bhqk,bhkd->bhqd', attn, V)
        out = out.transpose(0, 2, 1, 3).reshape(B, N, D)
        return out @ wo.T

    def _L2_ffn_ref(x, ln1_w, ln2_w, wqkv, wo, gate_w, w13, w2):
        import jax, jax.numpy as jnp
        import numpy as np
        HID = 128
        NH = 16
        NKV = 4
        HD = HID // NH
        E = 8
        TOPK = 2
        FFN = 256
        EPS = 1e-05
        THETA = 10000.0

        def _rmsnorm(x, w):
            var = jnp.mean(x * x, axis=-1, keepdims=True)
            return x * jax.lax.rsqrt(var + EPS) * w

        def _rope_tables(S):
            inv_freq = 1.0 / THETA ** (jnp.arange(0, HD, 2, dtype=jnp.float32) / HD)
            freqs = jnp.arange(S, dtype=jnp.float32)[:, None] * inv_freq[None, :]
            emb = jnp.concatenate([freqs, freqs], axis=-1)
            return (jnp.cos(emb), jnp.sin(emb))

        def _apply_rope(t, cos, sin):
            t1, t2 = jnp.split(t, 2, axis=-1)
            rot = jnp.concatenate([-t2, t1], axis=-1)
            return t * cos[None, :, None, :] + rot * sin[None, :, None, :]
        B, S, _ = x.shape
        h = _rmsnorm(x, ln1_w)
        qkv = jnp.einsum('bsh,oh->bso', h, wqkv)
        q = qkv[..., :NH * HD].reshape(B, S, NH, HD)
        k = qkv[..., NH * HD:(NH + NKV) * HD].reshape(B, S, NKV, HD)
        v = qkv[..., (NH + NKV) * HD:].reshape(B, S, NKV, HD)
        cos, sin = _rope_tables(S)
        q = _apply_rope(q, cos, sin)
        k = _apply_rope(k, cos, sin)
        groups = NH // NKV
        k = jnp.repeat(k, groups, axis=2)
        v = jnp.repeat(v, groups, axis=2)
        scale = HD ** (-0.5)
        scores = jnp.einsum('bqhd,bkhd->bhqk', q, k) * scale
        causal = jnp.tril(jnp.ones((S, S), dtype=bool))
        scores = jnp.where(causal[None, None], scores, jnp.finfo(scores.dtype).min)
        probs = jax.nn.softmax(scores, axis=-1)
        attn = jnp.einsum('bhqk,bkhd->bqhd', probs, v).reshape(B, S, NH * HD)
        x = x + jnp.einsum('bso,ho->bsh', attn, wo)
        h = _rmsnorm(x, ln2_w).reshape(-1, HID)
        T = h.shape[0]
        logits = jnp.einsum('th,eh->te', h, gate_w)
        rprobs = jax.nn.softmax(logits.astype(jnp.float32), axis=-1)
        topw, topi = jax.lax.top_k(rprobs, TOPK)
        topw = topw / jnp.sum(topw, axis=-1, keepdims=True)
        wfull = jnp.zeros((T, E), jnp.float32).at[jnp.arange(T)[:, None], topi].set(topw)
        wfull = wfull.astype(h.dtype)
        out = jnp.zeros((T, HID), h.dtype)
        for e in range(E):
            w1 = w13[e, :FFN]
            w3 = w13[e, FFN:]
            g = jax.nn.silu(h @ w1.T) * (h @ w3.T)
            out = out + jnp.einsum('tf,hf->th', g, w2[e]) * wfull[:, e:e + 1]
        return x + out.reshape(B, S, HID)

    def _L3_attn_ref(qkv, Wq, bq, Wk, bk, Wv, bv, Wo, bo, slopes):
        import math
        import jax, jax.numpy as jnp
        import numpy as np
        D_MODEL = 128
        NUM_HEADS = 16
        NUM_KV_HEADS = 4
        D_HEAD = D_MODEL // NUM_HEADS
        SEQ = 512
        BATCH = 1
        B, S, D = qkv.shape
        H, KVH, dh = (NUM_HEADS, NUM_KV_HEADS, D_HEAD)
        G = H // KVH
        scale = 1.0 / math.sqrt(dh)
        q = (qkv @ Wq + bq).reshape(B, S, H, dh).transpose(0, 2, 1, 3)
        k = (qkv @ Wk + bk).reshape(B, S, KVH, dh).transpose(0, 2, 1, 3)
        v = (qkv @ Wv + bv).reshape(B, S, KVH, dh).transpose(0, 2, 1, 3)
        qg = q.reshape(B, KVH, G, S, dh)
        scores = jnp.einsum('bhgqd,bhkd->bhgqk', qg, k) * scale
        rel = jnp.arange(S, dtype=jnp.float32)[None, :] - jnp.arange(S, dtype=jnp.float32)[:, None]
        bias = slopes.reshape(KVH, G, 1, 1) * rel
        causal = jnp.tril(jnp.ones((S, S), dtype=bool))
        bias = jnp.where(causal, bias, -jnp.inf)
        attn = jax.nn.softmax(scores + bias[None], axis=-1)
        out = jnp.einsum('bhgqk,bhkd->bhgqd', attn, v)
        out = out.reshape(B, H, S, dh).transpose(0, 2, 1, 3).reshape(B, S, D)
        return out @ Wo + bo

    def _L3_ffn_ref(x, ln1_g, ln1_b, w1, b1, ln2_g, ln2_b, w2, b2):
        import jax, jax.numpy as jnp
        import numpy as np
        LN_EPS = 1e-05

        def layer_norm(x, g, b):
            mu = jnp.mean(x, axis=-1, keepdims=True)
            var = jnp.mean(jnp.square(x - mu), axis=-1, keepdims=True)
            return (x - mu) * jax.lax.rsqrt(var + LN_EPS) * g + b

        def ternary_quant(w):
            scale = 1.0 / jnp.clip(jnp.mean(jnp.abs(w)), 1e-05)
            wq = jnp.clip(jnp.round(w * scale), -1.0, 1.0) / scale
            return w + jax.lax.stop_gradient(wq - w)
        h = layer_norm(x, ln1_g, ln1_b)
        h = jnp.einsum('bsd,hd->bsh', h, ternary_quant(w1)) + b1
        h = jax.nn.gelu(h, approximate=False)
        h = layer_norm(h, ln2_g, ln2_b)
        out = jnp.einsum('bsh,dh->bsd', h, ternary_quant(w2)) + b2
        return out
    x = L0_attn_x
    x = _layernorm(x + _L0_attn_ref(x, L0_attn_time_decay, L0_attn_time_first, L0_attn_time_mix, L0_attn_Wk, L0_attn_Wv, L0_attn_Wr, L0_attn_Wo), axis=-1)
    x = _layernorm(x + _L0_ffn_ref(x, L0_ffn_W, L0_ffn_b, L0_ffn_logits, L0_ffn_u), axis=-1)
    x = _layernorm(x + _L1_attn_ref(x, L1_attn_Wq, L1_attn_Wk, L1_attn_Wv, L1_attn_W_out, L1_attn_b_out), axis=-1)
    x = _layernorm(x + _L1_ffn_ref(x, L1_ffn_gate_w, L1_ffn_gate_b, L1_ffn_w1, L1_ffn_b1, L1_ffn_w3, L1_ffn_b3, L1_ffn_w2, L1_ffn_b2, L1_ffn_sw1, L1_ffn_sb1, L1_ffn_sw3, L1_ffn_sb3, L1_ffn_sw2, L1_ffn_sb2), axis=-1)
    x = _layernorm(x + _L2_attn_ref(x, L2_attn_wq, L2_attn_wk, L2_attn_wv, L2_attn_wo), axis=-1)
    x = _layernorm(x + _L2_ffn_ref(x, L2_ffn_ln1_w, L2_ffn_ln2_w, L2_ffn_wqkv, L2_ffn_wo, L2_ffn_gate_w, L2_ffn_w13, L2_ffn_w2), axis=-1)
    x = _layernorm(x + _L3_attn_ref(x, L3_attn_Wq, L3_attn_bq, L3_attn_Wk, L3_attn_bk, L3_attn_Wv, L3_attn_bv, L3_attn_Wo, L3_attn_bo, L3_attn_slopes), axis=-1)
    x = _layernorm(x + _L3_ffn_ref(x, L3_ffn_ln1_g, L3_ffn_ln1_b, L3_ffn_w1, L3_ffn_b1, L3_ffn_ln2_g, L3_ffn_ln2_b, L3_ffn_w2, L3_ffn_b2), axis=-1)
    return x

_drawn_inputs = setup_inputs


def setup_inputs(seed=0):
    import zlib

    import numpy as np

    out = dict(_drawn_inputs(seed))
    spreads = {'L0_attn_time_first': (-1.2039728164672852, 0.6),
     'L0_ffn_b': (0.0, 0.1),
     'L1_attn_b_out': (0.0, 0.1),
     'L2_ffn_ln1_w': (1.0, 0.6),
     'L2_ffn_ln2_w': (1.0, 0.6),
     'L3_attn_bq': (0.0, 0.8),
     'L3_attn_bk': (0.0, 0.8),
     'L3_attn_bv': (0.0, 0.397),
     'L3_attn_bo': (0.0, 0.1),
     'L3_ffn_ln1_g': (1.0, 0.2),
     'L3_ffn_ln1_b': (0.0, 0.303),
     'L3_ffn_b1': (0.0, 0.1),
     'L3_ffn_ln2_g': (1.0, 0.2),
     'L3_ffn_ln2_b': (0.0, 0.274),
     'L3_ffn_b2': (0.0, 0.1)}
    factors = {'L0_attn_time_decay': 8.0,
     'L0_attn_time_mix': 8.0,
     'L0_attn_Wk': 8.0,
     'L0_attn_Wv': 3.965,
     'L0_attn_Wr': 8.0,
     'L0_attn_Wo': 3.963,
     'L1_ffn_gate_w': 8.0,
     'L1_ffn_gate_b': 8.0,
     'L1_ffn_w1': 8.0,
     'L1_ffn_b1': 8.0,
     'L1_ffn_w3': 8.0,
     'L1_ffn_b3': 8.0,
     'L1_ffn_w2': 8.0,
     'L1_ffn_b2': 8.0,
     'L1_ffn_sw1': 8.0,
     'L1_ffn_sb1': 8.0,
     'L1_ffn_sw3': 8.0,
     'L1_ffn_sb3': 8.0,
     'L1_ffn_sw2': 8.0,
     'L2_ffn_wqkv': 8.0,
     'L2_ffn_wo': 7.996,
     'L2_ffn_gate_w': 8.0,
     'L2_ffn_w13': 8.0,
     'L2_ffn_w2': 8.0,
     'L3_attn_Wq': 8.0,
     'L3_attn_Wk': 8.0,
     'L3_attn_Wv': 2.709,
     'L3_attn_slopes': 4.254}
    for name, (base, spread) in spreads.items():
        noise = np.random.default_rng([zlib.crc32(name.encode()), seed]).standard_normal(out[name].shape)
        drawn = base * np.exp(spread * noise) if base else spread * noise
        out[name] = jnp.asarray(drawn.astype(out[name].dtype))
    for name, factor in factors.items():
        out[name] = (out[name] * factor).astype(out[name].dtype)
    return out
```

```python
from contextlib import ExitStack

import numpy as np

import concourse.bass as bass
from concourse import mybir

F32 = mybir.dt.float32
BF16 = mybir.dt.bfloat16
ALU = mybir.AluOpType
ACT = mybir.ActivationFunctionType
AX_X = mybir.AxisListType.X
AX_XY = mybir.AxisListType.XY

P = 128
NB = 4
T = 512
NT = T // P
H = 16
HD = P // H
GH = 4
NG = H // GH
PARTS = 3
STACK = HD * PARTS * PARTS
ALIBI = 2 * PARTS
ROWS_SHIFT = P - PARTS
VW = 32
E = 8
NGATE = 9
MASKED = -1.0e30
LN_EPS = 1e-5

(L0_MIX, L0_LINEAR, L1_ATTN, L1_MOE, L2_ATTN, L2_GQA, L2_MOE, L3_ATTN, L3_FFN) = range(9)
LAST = L3_FFN
NORMS = {L0_MIX: ("ln",), L0_LINEAR: ("ln",), L1_ATTN: ("ln",), L1_MOE: ("ln",), L2_ATTN: ("ln", "rms"),
         L2_GQA: ("rms",), L2_MOE: ("ln",), L3_ATTN: ("ln", "ln"), L3_FFN: ("ln",)}
NORM_BASE = [sum(NB * len(NORMS[q]) for q in range(p)) for p in range(9)]

LAYERS = [
    dict(phase=L1_ATTN, kv=H, scale=P ** -0.5, causal=False, rope=None, alibi=False),
    dict(phase=L2_ATTN, kv=H, scale=HD ** -0.5, causal=True, rope=0, alibi=False),
    dict(phase=L2_GQA, kv=NG, scale=HD ** -0.5, causal=True, rope=1, alibi=False),
    dict(phase=L3_ATTN, kv=NG, scale=1.0, causal=True, rope=None, alibi=True),
]
PREP_USES = [5 if c["rope"] is not None else 3 for c in LAYERS]
PREP_BASE = [sum(NB * n for n in PREP_USES[:i]) for i in range(4)]
UNITS = NB * NG

MOE_CHUNKS = {L1_MOE: 13, L2_MOE: 16}
MOE_BASE = {L1_MOE: 0, L2_MOE: NB * 13}

W_COLS, _at = {}, 0
for _n, _w in [("l0_k", P), ("l0_v", P), ("l0_r", P), ("l0_o", P), ("l1_out", P),
               ("l2_q", P), ("l2_qs", P), ("l2_k", P), ("l2_ks", P), ("l2_v", P), ("l2_o", P),
               ("g_q", P), ("g_qs", P), ("g_k", 32), ("g_ks", 32), ("g_v", 32), ("g_o", P),
               ("l3_q", P), ("l3_k", 32), ("l3_v", 32), ("l3_o", P), ("l1_gate", E), ("l2_gate", E)]:
    W_COLS[_n] = (_at, _at + _w)
    _at += _w
W_TOTAL = _at
C_COLS, _at = {}, 0
for _n, _w in [("decay", 1), ("first", 1), ("mix", 1), ("ln1_w", 1), ("ln2_w", 1), ("bq", 1), ("bk", 1),
               ("f_ln1_g", 1), ("f_ln1_b", 1), ("f_ln2_g", 4), ("f_ln2_b", 4), ("m_b1", 13), ("m_b3", 13)]:
    C_COLS[_n] = (_at, _at + _w)
    _at += _w
C_TOTAL = _at
R_COLS, _at = {}, 0
for _n, _w in [("logits", E), ("u", E), ("l0_b", E * P), ("gate_b", E), ("b_out", P), ("bv", 32), ("bo", P),
               ("f_b1", T), ("f_b2", P)]:
    R_COLS[_n] = (_at, _at + _w)
    _at += _w
R_TOTAL = _at


def post_index(p, b):
    return b * 2 + p if p <= L0_LINEAR else b + NB * p


def norm_index(p, b):
    return b * 2 + p if p <= L0_LINEAR else b * len(NORMS[p]) + NORM_BASE[p]


def for_blocks(eng, body):
    body(0)
    with eng.Fori(1, NB) as b:
        body(b)


def at_least(eng, sem, count):
    if isinstance(count, int) and count <= 0:
        return
    eng.wait_ge(sem, count)


def build(nc, d):
    ctx = ExitStack()
    with ctx:
        def sb(name, shape, dt=F32):
            return ctx.enter_context(nc.sbuf_tensor(name, shape, dt))

        def sem(name):
            return ctx.enter_context(nc.semaphore(name))

        bank = [ctx.enter_context(nc.psum_tensor(f"bank{i}", [P, T], F32)) for i in range(8)]
        X = sb("X", [P, NB * T])
        X1buf = sb("X1", [P, NB * (T + 1)])
        X1 = X1buf[:, 0:NB * T]
        XTP = X1buf[:, :].rearrange("p (b t) -> p b t", b=NB)
        XT = sb("XT", [P, NB * T])
        XTS = sb("XTS", [P, T])
        WC = sb("WC", [P, W_TOTAL])
        CC = sb("CC", [P, C_TOTAL])
        RC = sb("RC", [P, R_TOTAL])
        ident = sb("ident", [P, P])
        identb = sb("identb", [P, P], BF16)
        maskb = sb("maskb", [P, P], BF16)
        WQKV1 = sb("WQKV1", [P, 3, P])
        WSEL = sb("WSEL", [P, P])
        BSEL = sb("BSEL", [P, P])
        tables = sb("tables", [P, 2, 2, T])
        MW1 = sb("MW1", [P, 16 * P])
        MW3 = sb("MW3", [P, 16 * P])
        MW2 = sb("MW2", [P, 16, P])
        MB2 = sb("MB2", [NGATE, P])
        SEL = sb("SEL", [P, 16, P], BF16)
        RWT = sb("RWT", [P, NB * T], BF16)
        RW9 = sb("RW9", [NGATE, NB * T])
        RWB = sb("RWB", [NGATE, T])
        FW1 = sb("FW1", [P, T])
        FW2 = sb("FW2", [P, 4, P])
        QS = sb("QS", [P, H, T], BF16)
        KS = sb("KS", [P, H, T], BF16)
        PQ = sb("PQ", [P, PARTS, T], BF16)
        PK = sb("PK", [P, PARTS, T], BF16)
        QF = sb("QF", [P, T])
        KF = sb("KF", [P, T])
        RA = sb("RA", [P, 2, T])
        SA = sb("RB", [P, 2, T + 1])
        RB = SA[:, :, 0:T]
        W0 = RA[:, :, :].rearrange("p a (n d) -> p (a n) d", d=P)
        VST = sb("VST", [P, NT, P])
        VA = sb("VA", [P, NT, H, VW])
        PT = [sb(f"PT{i}", [P, GH, T]) for i in range(2)]
        M = [sb(f"M{i}", [P, NT * GH]) for i in range(2)]
        MR = sb("MR", [P, NT * GH])
        MS = [sb(f"MS{i}", [P, NT, PARTS, GH], BF16) for i in range(2)]
        MSB = [sb(f"MSB{i}", [PARTS * GH, T], BF16) for i in range(2)]
        OT = sb("OT", [P, T])
        OR = sb("OR", [P, NT * GH])
        AO = sb("AO", [P, NT, P])
        AOT = sb("AOT", [P, T])
        slope = sb("slope", [H, 1])
        slope_r = sb("slope_r", [H, 1])
        slope_p = sb("slope_p", [H, PARTS], BF16)
        slope_w = sb("slope_w", [H, PARTS, T], BF16)
        YB = sb("YB", [P, NT, P])
        N1 = sb("N1", [P, NT, P])
        N2 = sb("N2", [P, NT, P])
        ST = sb("ST", [P, NT, 6])
        MV = sb("MV", [P, NT, 2])
        MS2 = sb("MS2", [P, NT])
        VE = sb("VE", [P, NT])
        RSTD = sb("RSTD", [P, NT])
        neg_half = sb("neg_half", [P, NT])
        zcol = sb("zcol", [P, 1])
        bqs = sb("bqs", [P, 1])
        GL = sb("GL", [P, NB * NT, E])
        GE = sb("GE", [P, NB * NT, E])
        GB = sb("GB", [P, NB * NT, E])
        GR = sb("GR", [P, NB * NT, E])
        GO = sb("GO", [P, NB * NT, E])
        GM = sb("GM", [P, NB * NT])
        GW = sb("GW", [P, NB * NT, NGATE])
        GWR = sb("GWR", [P, NB * NT, NGATE])
        GWP = sb("GWP", [P, NB * NT, PARTS, NGATE], BF16)
        rev = sb("rev", [P, E])
        sel0 = sb("sel0", [P, 12, E])
        A1 = [PT[0][:, 0, :], PT[0][:, 1, :]]
        U1 = [PT[0][:, 2, :], PT[0][:, 3, :]]
        S1 = [PT[1][:, 0, :], PT[1][:, 1, :]]
        H1 = [PT[1][:, 2, :], PT[1][:, 3, :]]
        XM0, XM, KM, KE = (PT[0][:, i, :] for i in range(4))
        SG, KV, RWKV = (PT[1][:, i, :] for i in range(3))
        cols0 = sb("cols0", [P, 4])
        HG = PT[0]
        HT2 = PT[1]
        FST = sb("FST", [P, NT, 6])
        qa = sb("qa", [P, 2, 8])
        ones = sb("ones", [P, P])
        qt0 = YB[:, :, :].rearrange("p a b -> p (a b)")

        ld_x, ld_0, ld_w, ld_1, ld_m1, ld_m2, ld_f = (sem("load_" + n) for n in
                                                      ("x", "l0", "weights", "l1", "moe1", "moe2", "ffn"))
        pool_const = sem("pool_const")
        pool_passed, pe_passed = sem("pool_passed"), sem("pe_passed")
        y_ready, y_added, var_ready, rstd_ready, normed, x_saved, xt_ready, xt_evac, out_done = (sem(n) for n in (
            "pe_y", "dve_y_added", "dve_var", "pool_rstd", "dve_normed", "pool_x_saved", "pe_xt", "act_xt", "dma_out"))
        z_sem, z2_sem, sel_ready, xm0_ready, xm_ready, kvr_ready, km_ready, ke_ready, rwkv_ready, y0_done = (sem(n) for n in (
            "act_z", "dve_z", "dve_sel", "pool_xm0", "dve_xm", "pe_kvr", "dve_km", "act_ke", "dve_rwkv", "pe_l0_done"))
        c0a, c0b, sg_ready = sem("act_cols0"), sem("dve_cols0"), sem("act_sigmoid")
        (proj_ready, prep_evac, parts_ready, parts_stored, v_placed, s_ready, max_done, m_split, mt_ready, m_evac,
         st_ready, exp_done, pv_done, o_evac, ot_ready, o_normed, ao_ready, ao_evac, xts_ready, alibi_rows) = (sem(n) for n in (
             "pe_proj", "prep_evac", "pool_parts", "dma_parts", "pool_v", "pe_scores", "dve_max", "dve_shift",
             "pe_shift", "act_shift", "pe_scores_t", "act_exp", "pe_pv", "act_o", "pe_o_t", "dve_o", "pe_ao", "act_ao",
             "pool_xts", "dma_alibi"))
        slope_ready = sem("dve_slope")
        stack_landed = [sem(f"dma_stack{g}") for g in range(NG)]
        shift_landed = [sem(f"dma_shift{i}") for i in range(2)]
        (lg_ready, gm_ready, ge_ready, gw_ready, gt_ready, gt_evac, rwb_ready, ab_ready, a_evac, u_ready, s1_ready,
         h_ready, yc_done) = (sem(n) for n in (
             "pe_logits", "dve_gmax", "act_gexp", "dve_gates", "pe_gates_t", "act_gates_t", "pool_rwb", "pe_ab", "act_a", "dve_u",
             "act_silu", "dve_h", "pe_chunk"))
        (qs_ready, qm_ready, fu_ready, fb_ready, fg_ready, fv_ready, fr_ready, fn_ready, ft_ready, ft_evac) = (sem(n) for n in (
            "dve_absum", "pe_absum", "pe_up", "dve_up", "act_gelu", "dve_fvar", "pool_frstd", "dve_fnorm", "pe_ft", "act_ft"))

        scr_q = nc.dram_tensor("scr_q", [H * STACK * T], BF16, kind="Internal").ap().tensor
        scr_k = nc.dram_tensor("scr_k", [H * STACK * T], BF16, kind="Internal").ap().tensor

        def wc(name):
            return WC[:, W_COLS[name][0]:W_COLS[name][1]]

        def cc(name, i=0, rows=P):
            return CC[0:rows, C_COLS[name][0] + i:C_COLS[name][0] + i + 1]

        def rc(name):
            return RC[:, R_COLS[name][0]:R_COLS[name][1]]

        def blk(t, b):
            return t[:, b * T:(b + 1) * T] if isinstance(b, int) else t[:, bass.ds(b * T, T)]

        def tiles(ap, n=NT):
            return ap.rearrange("p (a b) -> p a b", a=n)

        Y = bank[6]
        block = ctx.enter_context(nc.Block())

        NEXT_BIAS = {L0_MIX: lambda: BSEL[:, :], L0_LINEAR: lambda: rc("b_out"), L2_MOE: lambda: rc("bo"),
                     L3_ATTN: lambda: rc("f_b2")}

        def attn_weights(L):
            return [(WQKV1[:, 0, :], None, WQKV1[:, 1, :], None, WQKV1[:, 2, :], wc("l1_out")),
                    (wc("l2_q"), wc("l2_qs"), wc("l2_k"), wc("l2_ks"), wc("l2_v"), wc("l2_o")),
                    (wc("g_q"), wc("g_qs"), wc("g_k"), wc("g_ks"), wc("g_v"), wc("g_o")),
                    (wc("l3_q"), None, wc("l3_k"), None, wc("l3_v"), wc("l3_o"))][L]

        def prep_uses(L):
            return ["q", "qs", "k", "ks", "v"] if LAYERS[L]["rope"] is not None else ["q", "k", "v"]

        def prep_places(L):
            if LAYERS[L]["rope"] is not None:
                return {(0, 0): 0, (0, 2): 1, (1, 0): 2, (1, 2): 3, (2, 0): 4}
            return {(0, 0): 0, (0, 2): 1, (2, 0): 2}

        def U(L, b, g):
            return (b + NB * L) * NG + g

        def half(L, b, g):
            return (b + NB * L) * 2 + g // 2

        def sequence(L, unit, Fori):
            unit(0, 0, ahead=(0, 2))
            with Fori(0, NB - 1) as b:
                unit(b, 1, ahead=(b, 3), prep=b + 1)
                unit(b, 2, ahead=(b + 1, 0))
                unit(b, 3, ahead=(b + 1, 1))
                unit(b + 1, 0, ahead=(b + 1, 2), end=b)
            unit(NB - 1, 1, ahead=(NB - 1, 3))
            unit(NB - 1, 2)
            unit(NB - 1, 3)

        def q_from(L, t):
            return t * P if LAYERS[L]["causal"] else 0

        def k_to(L, t):
            return (t + 1) * P if LAYERS[L]["causal"] else T

        def kv_slot(L, g, j):
            return g if LAYERS[L]["kv"] == NG else g * GH + j

        @block.sync
        def _(sp):
            sp.dma_start(XTP[:, :, 1:T + 1], d["xT"].rearrange("c (b t) -> c b t", b=NB)).then_inc(ld_x, 16)
            sp.dma_start(CC[:, :], d["cols"]).then_inc(ld_0, 16)
            sp.dma_start(WC[:, :], d["wpack"]).then_inc(ld_w, 16)
            sp.dma_start(RC[:, :], d["rows"].partition_broadcast(P)).then_inc(ld_0, 16)
            sp.dma_start(W0[:, :, :], d["L0_ffn_W"].rearrange("n d e -> d n e")).then_inc(ld_0, 16)
            sp.dma_start(tiles(X[:, :], NB * NT), d["L0_attn_x"].rearrange("b (t p) c -> p (b t) c", p=P)).then_inc(ld_x, 16)
            sp.dma_start(ident[:, :], d["ident"]).then_inc(ld_x, 16)
            sp.dma_start(identb[:, :], d["identb"]).then_inc(ld_1, 16)
            sp.dma_start(maskb[:, :], d["maskb"]).then_inc(ld_1, 16)
            sp.wait_ge(pool_const, 1)
            for i, n in enumerate(("l1_wq", "l1_wk", "l1_wv")):
                for h in range(H):
                    sp.dma_start(WQKV1[h * HD:(h + 1) * HD, i, h * HD:(h + 1) * HD], d[n]).then_inc(ld_1, 16)
            for i in range(2):
                for k in range(2):
                    sp.dma_start(tables[:, i, k, :], d["tables"][i, k]).then_inc(ld_1, 16)
            sp.dma_start(SEL[:, :, :], d["sel"][0]).then_inc(ld_m1, 16)
            sp.dma_start(MW1[:, 0:13 * P], d["m1_w1"]).then_inc(ld_m1, 16)
            sp.dma_start(MW3[:, 0:13 * P], d["m1_w3"]).then_inc(ld_m1, 16)
            sp.dma_start(MW2[:, 0:13, :], d["m1_w2"]).then_inc(ld_m1, 16)
            sp.dma_start(MB2[:, :], d["m1_b2"]).then_inc(ld_m1, 16)
            sp.dma_start(FW1[:, :], d["f_w1"]).then_inc(ld_f, 16)
            sp.dma_start(FW2[:, :, :], d["f_w2"]).then_inc(ld_f, 16)
            sp.dma_start(slope[:, :], d["slopes"]).then_inc(ld_f, 16)

            def store_parts(L, b):
                B = b + NB * L
                nk = LAYERS[L]["kv"] * HD
                for g in range(NG):
                    at_least(sp, stack_landed[g], B * 32)
                at_least(sp, parts_ready, B * 2 + 1)
                for j in range(PARTS):
                    sp.dma_start(bass.AP(tensor=scr_q, offset=j * T, ap=[[9 * T, P], [3 * T, 3], [1, T]]),
                                 PQ[:, :, :]).then_inc(parts_stored, 16)
                at_least(sp, parts_ready, B * 2 + 2)
                for i in range(PARTS):
                    sp.dma_start(bass.AP(tensor=scr_k, offset=3 * i * T, ap=[[9 * T, nk], [T, 3], [1, T]]),
                                 PK[0:nk, :, :]).then_inc(parts_stored, 16)
                at_least(sp, parts_stored, (B + 1) * 96)

            def load_stack(L, b, g):
                u = U(L, b, g)
                at_least(sp, st_ready, (u - 3) * 16)
                sp.dma_start(QS[0:STACK, g * GH:(g + 1) * GH, :],
                             bass.AP(tensor=scr_q, offset=g * GH * STACK * T, ap=[[T, STACK], [STACK * T, GH], [1, T]])
                             ).then_inc(stack_landed[g], 16)
                n = GH if LAYERS[L]["kv"] == H else 1
                sp.dma_start(KS[0:STACK, g * n:(g + 1) * n, :],
                             bass.AP(tensor=scr_k, offset=g * n * STACK * T, ap=[[T, STACK], [STACK * T, n], [1, T]])
                             ).then_inc(stack_landed[g], 16)

            def load_shift(L, b, g):
                at_least(sp, m_evac, U(L, b, g) + 1)
                for i in range(PARTS):
                    sp.dma_start(QS[ROWS_SHIFT + i:ROWS_SHIFT + i + 1, g * GH:(g + 1) * GH, :],
                                 MSB[g % 2][i * GH:(i + 1) * GH, :]).then_inc(shift_landed[g % 2], 16)

            def attention_sp(L):
                if LAYERS[L]["alibi"]:
                    sp.wait_ge(slope_ready, 1)
                    at_least(sp, st_ready, 16 * U(L, 0, 0))
                    for i in range(PARTS):
                        for k in range(2):
                            r = STACK + 2 * i + k
                            sp.dma_start(QS[r:r + 1, :, :], slope_w[:, i, :]).then_inc(alibi_rows, 16)
                    sp.dma_start(KS[STACK:STACK + ALIBI, 0:NG, :], d["kpos"]).then_inc(alibi_rows, 16)
                store_parts(L, 0)
                for g in range(NG):
                    load_stack(L, 0, g)
                load_shift(L, 0, 0)

                def unit(b, g, ahead=None, prep=None, end=None):
                    if g == 2 and ahead is not None:
                        load_stack(L, b + 1, 1)
                    if g == 3 and ahead is not None:
                        load_stack(L, b + 1, 2)
                    if end is not None:
                        load_stack(L, b, 3)
                    if not (g == 3 and ahead is None):
                        load_shift(L, b + (g + 1) // NG, (g + 1) % NG)
                    if prep is not None:
                        store_parts(L, prep)
                        load_stack(L, prep, 0)
                sequence(L, unit, sp.Fori)

            attention_sp(0)
            attention_sp(1)
            sp.wait_ge(xt_evac, 4 * (L1_MOE + 1))
            sp.dma_start(SEL[:, :, :], d["sel"][1]).then_inc(ld_m2, 16)
            sp.dma_start(MW1[:, :], d["m2_w1"]).then_inc(ld_m2, 16)
            sp.dma_start(MW3[:, :], d["m2_w3"]).then_inc(ld_m2, 16)
            sp.dma_start(MW2[:, :, :], d["m2_w2"]).then_inc(ld_m2, 16)
            attention_sp(2)
            attention_sp(3)
            with sp.Fori(0, NB) as b:
                sp.wait_ge(normed, b + 4 * LAST + 1)
                sp.dma_start(d["out"][bass.ds(b, 1)].rearrange("a (t p) c -> p (a t) c", p=P), N1[:, :, :]).then_inc(out_done, 16)
            sp.wait_ge(out_done, 16 * NB)

        @block.gpsimd
        def _(pool):
            g = nc.gpsimd

            def wait(sem, count):
                at_least(pool, sem, count)
                if not isinstance(count, int):
                    pool.sem_inc(pool_passed, 1)
            g.memset(WQKV1[:, :, :], 0.0).then_inc(pool_const, 1)
            g.memset(XTP[:, :, 0:1], 0.0)
            g.memset(SA[:, :, 0:1], 0.0)
            g.memset(neg_half[:, :], -0.5)
            g.iota(rev[:, :], pattern=[[-1, E]], base=E, channel_multiplier=0, allow_small_or_imprecise_dtypes=True)
            g.memset(ones[:, :], 1.0).then_inc(pool_const, 1)
            g.memset(QS[:, :, :], 0.0)
            g.memset(KS[:, :, :], 0.0).then_inc(pool_const, 1)
            g.memset(VA[:, :, :, :], 0.0)
            pool.drain()
            g.memset(VA[:, :, :, HD:HD + 1], 1.0)
            pool.drain()
            g.affine_select(out=KS[96:P, :, :], in_=KS[96:P, :, :], compare_op=ALU.is_gt, fill=1.0,
                            base=ROWS_SHIFT - 96, pattern=[[0, H * T]], channel_multiplier=-1).then_inc(pool_const, 1)
            pool.drain()
            g.memset(RWT[:, :], 0.0).then_inc(pool_const, 1)

            def rstd(idx, eps):
                wait(var_ready, idx + 1)
                g.tensor_scalar(VE[:, :], MS2[:, :], eps, 1.0, ALU.add, ALU.mult)
                pool.drain()
                g.tensor_tensor(RSTD[:, :], VE[:, :], neg_half[:, :], ALU.pow).then_inc(rstd_ready, 1)

            def post(p, b):
                pi = post_index(p, b)
                n0 = norm_index(p, b)
                if p == L2_GQA:
                    wait(var_ready, n0 + 1)
                    g.tensor_copy(blk(X1, b), YB[:, :, :].rearrange("p a b -> p (a b)")).then_inc(x_saved, 1)
                    rstd(n0, LN_EPS)
                    return
                rstd(n0, LN_EPS)
                if p == LAST:
                    return
                wait(normed, pi + 1) if len(NORMS[p]) == 1 else wait(var_ready, n0 + 2)
                if p in NEXT_BIAS:
                    if p == L0_MIX:
                        wait(sel_ready, 1)
                    bias = NEXT_BIAS[p]()
                    g.tensor_tensor(tiles(blk(X, b)), N1[:, :, :], bias.rearrange("p (a b) -> p a b", a=1).to_broadcast([P, NT, P]),
                                    ALU.add).then_inc(x_saved, 1)
                else:
                    g.tensor_copy(blk(X, b), N1[:, :, :].rearrange("p a b -> p (a b)")).then_inc(x_saved, 1)
                if len(NORMS[p]) == 2:
                    rstd(n0 + 1, LN_EPS)

            wait(ld_x, 48)
            wait(c0b, 1)

            def layer0_pool(b):
                wait(kvr_ready, b)
                xs = XTP[:, b, 0:T] if isinstance(b, int) else XTP[:, bass.ds(b, 1), 0:T].rearrange("p a b -> p (a b)")
                g.tensor_tensor(XM0, xs, cols0[:, 0:1].to_broadcast([P, T]), ALU.mult).then_inc(xm0_ready, 1)
                post(L0_MIX, b)
                post(L0_LINEAR, b)
            for_blocks(pool, layer0_pool)

            def split(src, tmp, parts, n):
                g.tensor_copy(parts[0:n, 0, :], src)
                pool.drain()
                g.tensor_tensor(tmp, src, parts[0:n, 0, :], ALU.subtract)
                pool.drain()
                g.tensor_copy(parts[0:n, 1, :], tmp)
                pool.drain()
                g.tensor_tensor(parts[0:n, 2, :], tmp, parts[0:n, 1, :], ALU.subtract).then_inc(parts_ready, 1)

            def prep_pool(L, b):
                B = b + NB * L
                c = LAYERS[L]
                base = b * PREP_USES[L] + PREP_BASE[L]
                nk = c["kv"] * HD
                wait(xt_evac, post_index(c["phase"] - 1, b) + 1)
                if L:
                    wait(proj_ready, base)
                else:
                    wait(proj_ready, base)
                g.tensor_copy(XTS[:, :], blk(XT, b)).then_inc(xts_ready, 1)
                wait(parts_stored, B * 96)
                for i, (f, parts, n) in enumerate(((QF, PQ, P), (KF, PK, nk))):
                    if c["rope"] is not None:
                        wait(prep_evac, base + 2 * i + 2)
                        g.tensor_tensor(f[0:n, :], RA[0:n, i, :], RB[0:n, i, :], ALU.add)
                        pool.drain()
                    else:
                        wait(prep_evac, base + i + 1)
                    split(f[0:n, :], RA[0:n, i, :], parts, n)

            def place_v(L, b, gg):
                c = LAYERS[L]
                n = GH if c["kv"] == H else 1
                wait(prep_evac, (b + 1) * PREP_USES[L] + PREP_BASE[L])
                wait(pv_done, (U(L, b, gg) - 3) * NT)
                g.tensor_copy(VA[:, :, gg * n:(gg + 1) * n, 0:HD],
                              VST[:, :, gg * n * HD:(gg + 1) * n * HD].rearrange("p t (h e) -> p t h e", e=HD)
                              ).then_inc(v_placed, 1)

            def attention_pool(L):
                p = LAYERS[L]["phase"]
                prep_pool(L, 0)
                for gg in range(NG):
                    place_v(L, 0, gg)

                def unit(b, gg, ahead=None, prep=None, end=None):
                    if prep is not None:
                        prep_pool(L, prep)
                    if gg == 2 and ahead is not None:
                        place_v(L, b + 1, 0)
                        place_v(L, b + 1, 1)
                    if gg == 3 and ahead is not None:
                        place_v(L, b + 1, 2)
                    if end is not None:
                        place_v(L, b, 3)
                        post(p, end)
                sequence(L, unit, pool.Fori)
                post(p, NB - 1)

            def moe_pool(p):
                if p == L1_MOE:
                    def body(b):
                        wait(gt_evac, b * 2 + 2)
                        wait(y_ready, b + NB * p)
                        g.tensor_copy(RWB[:, :], blk(RW9, b)).then_inc(rwb_ready, 1)
                        post(p, b)
                    for_blocks(pool, body)
                else:
                    with pool.Fori(0, NB) as b:
                        post(p, b)

            attention_pool(0)
            moe_pool(L1_MOE)
            attention_pool(1)
            attention_pool(2)
            moe_pool(L2_MOE)
            attention_pool(3)

            def ffn_pool(b):
                wait(xt_evac, b + NB * LAST - NB + 1)
                wait(fu_ready, b * NT)
                g.tensor_copy(XTS[:, :], blk(XT, b)).then_inc(xts_ready, 1)
                wait(fv_ready, b + 1)
                g.tensor_scalar(VE[:, :], MS2[:, :], LN_EPS, 1.0, ALU.add, ALU.mult)
                pool.drain()
                g.tensor_tensor(RSTD[:, :], VE[:, :], neg_half[:, :], ALU.pow).then_inc(fr_ready, 1)
                post(LAST, b)
            for_blocks(pool, ffn_pool)

        @block.scalar
        def _(act):
            a = nc.scalar

            def xt_out(p, b):
                act.wait_ge(xt_ready, post_index(p, b) + 1)
                dst = XTS[:, :] if p == L0_MIX else blk(XT, b)
                src = (bank[6] if p in (L1_ATTN, L2_ATTN, L2_GQA, L3_ATTN) else bank[7])[:, :]
                if p == L2_ATTN:
                    i = a.activation(dst, src, ACT.Copy, scale=cc("ln1_w"))
                elif p == L2_GQA:
                    i = a.activation(dst, src, ACT.Copy, scale=cc("ln2_w"))
                elif p == L3_ATTN:
                    i = a.activation(dst, src, ACT.Identity, scale=cc("f_ln1_g"), bias=cc("f_ln1_b"))
                else:
                    i = a.activation(dst, src, ACT.Copy)
                i.then_inc(xt_evac, 1)

            act.wait_ge(ld_0, 48)
            a.activation(sel0[:, 0, :], rc("u"), ACT.Ln)
            act.drain()
            a.activation(sel0[:, 1, :], sel0[:, 0, :], ACT.Ln, scale=-1.0).then_inc(z_sem, 1)
            act.wait_ge(z2_sem, 1)
            a.activation(sel0[:, 3, :], sel0[:, 2, :], ACT.Exp, accum_out=sel0[:, 4, 0:1])
            act.drain()
            a.activation(sel0[:, 4, 1:2], sel0[:, 4, 0:1], ACT.Ln).then_inc(z_sem, 1)
            a.activation(cols0[:, 1:2], cc("decay"), ACT.Exp)
            act.drain()
            a.activation(cols0[:, 2:3], cols0[:, 1:2], ACT.Exp, scale=-1.0)
            a.activation(cols0[:, 3:4], cc("first"), ACT.Exp).then_inc(c0a, 1)

            def layer0_act(b):
                act.wait_ge(km_ready, b + 1)
                a.activation(KE, KM, ACT.Exp).then_inc(ke_ready, 1)
                a.activation(SG, bank[2][:, :], ACT.Sigmoid).then_inc(sg_ready, 1)
                xt_out(L0_MIX, b)
                xt_out(L0_LINEAR, b)
            for_blocks(act, layer0_act)

            def prep_act(L, b, i):
                c = LAYERS[L]
                B = b + NB * L
                base = b * PREP_USES[L] + PREP_BASE[L]
                what = prep_uses(L)[i]
                nk = c["kv"] * HD
                if what == "v":
                    act.wait_ge(proj_ready, base + i + 1)
                    at_least(act, v_placed, B * NG)
                    if c["alibi"]:
                        return
                    a.activation(VST[:, :, 0:nk], tiles(bank[6][:, :])[:, :, 0:nk], ACT.Copy).then_inc(prep_evac, 1)
                elif c["rope"] is None:
                    n, f = (P, QF) if what == "q" else (nk, KF)
                    act.wait_ge(proj_ready, base + i + 1)
                    at_least(act, parts_ready, B * 2 - (1 if what == "q" else 0))
                    if c["alibi"] and what == "q":
                        r = a.activation(f[0:n, :], bank[6][0:n, :], ACT.Identity, scale=HD ** -0.5, bias=bqs[:, :])
                    elif c["alibi"]:
                        r = a.activation(f[0:n, :], bank[6][0:n, :], ACT.Identity, bias=cc("bk", rows=n))
                    else:
                        r = a.activation(f[0:n, :], bank[6][0:n, :], ACT.Copy)
                    r.then_inc(prep_evac, 1)

            def m_out(L, b, g):
                w = U(L, b, g)
                act.wait_ge(mt_ready, w + 1)
                at_least(act, shift_landed[g % 2], half(L, b, g) * 48)
                a.activation(MSB[g % 2][:, :], bank[7][0:PARTS * GH, 0:T // 2].bitcast(BF16), ACT.Copy).then_inc(m_evac, 1)

            def o_out(L, u, g):
                act.wait_ge(pv_done, (u + 1) * NT)
                a.activation(OT[:, :], bank[4 + g % 2][:, :], ACT.Copy).then_inc(o_evac, 1)

            def ao_out(L, b):
                B = b + NB * L
                act.wait_ge(ao_ready, B + 1)
                at_least(act, y_ready, b + NB * LAYERS[L]["phase"])
                a.activation(AOT[:, :], bank[6][:, :], ACT.Copy).then_inc(ao_evac, 1)

            def attention_act(L):
                c = LAYERS[L]
                p = c["phase"]
                for i in range(PREP_USES[L]):
                    prep_act(L, 0, i)
                m_out(L, 0, 0)
                places = prep_places(L)

                def unit(b, g, ahead=None, prep=None, end=None):
                    u = U(L, b, g)
                    for kt in range(NT):
                        q0 = q_from(L, kt)
                        at_least(act, pv_done, u * NT + kt - 1)
                        for j in range(GH):
                            n = u * 16 + kt * GH + j
                            act.wait_ge(st_ready, n + 1)
                            a.activation(PT[kt % 2][:, j, q0:T], bank[2 + j % 2][:, 0:T - q0], ACT.Exp,
                                         scale=c["scale"]).then_inc(exp_done, 1)
                            if prep is not None and j % 2 and (kt, j - 1) in places:
                                prep_act(L, prep, places[(kt, j - 1)])
                            if kt == 0 and j == 3 and not (isinstance(b, int) and b == 0 and g == 0):
                                o_out(L, u - 1, g - 1)
                            if kt == 1 and j == 0 and not (g == 3 and ahead is None):
                                m_out(L, b + (g + 1) // NG, (g + 1) % NG)
                            if end is not None and kt == 2 and j == 1:
                                ao_out(L, end)
                            if end is not None and kt == 3 and j == 3:
                                xt_out(p, end)
                sequence(L, unit, act.Fori)
                o_out(L, U(L, NB - 1, NG - 1), NG - 1)
                ao_out(L, NB - 1)
                xt_out(p, NB - 1)

            def moe_act(p):
                act.wait_ge(gm_ready, 1 if p == L1_MOE else 2)
                a.activation(GE[:, :, :], GL[:, :, :], ACT.Exp).then_inc(ge_ready, 1)
                gi = 0 if p == L1_MOE else 1
                for b in range(NB):
                    act.wait_ge(gt_ready, (gi * NB + b) * 2 + 1)
                    a.activation(blk(RW9, b), bank[6][0:NGATE, :], ACT.Copy).then_inc(gt_evac, 1)
                    act.wait_ge(gt_ready, (gi * NB + b) * 2 + 2)
                    a.activation(blk(RWT, b)[0:PARTS * NGATE, :], bank[7][0:PARTS * NGATE, 0:T // 2].bitcast(BF16), ACT.Copy).then_inc(gt_evac, 1)
                n = MOE_CHUNKS[p]

                def body(b):
                    k0 = b * n + MOE_BASE[p]
                    for c in range(n + 1):
                        if c < n:
                            act.wait_ge(ab_ready, k0 + c + 1)
                            if p == L1_MOE:
                                at_least(act, u_ready, k0 + c - 1)
                                a.activation(A1[c % 2], bank[c % 2][:, :], ACT.Identity, bias=cc("m_b1", c)).then_inc(a_evac, 1)
                            else:
                                at_least(act, u_ready, k0 + c - 1)
                                a.activation(A1[c % 2], bank[c % 2][:, :], ACT.Silu).then_inc(a_evac, 1)
                        if c and p == L1_MOE:
                            act.wait_ge(u_ready, k0 + c)
                            at_least(act, h_ready, k0 + c - 2)
                            a.activation(S1[(c - 1) % 2], U1[(c - 1) % 2], ACT.Silu).then_inc(s1_ready, 1)
                    xt_out(p, b)
                for_blocks(act, body)

            attention_act(0)
            moe_act(L1_MOE)
            attention_act(1)
            attention_act(2)
            moe_act(L2_MOE)
            attention_act(3)

            def ffn_act(b):
                for i in range(NT):
                    act.wait_ge(fb_ready, b * NT + i + 1)
                    a.activation(HG[:, i, :], HG[:, i, :], ACT.Gelu).then_inc(fg_ready, 1)
                for c in range(4):
                    act.wait_ge(ft_ready, b * 4 + c + 1)
                    if c == 0:
                        at_least(act, y_ready, b + NB * LAST)
                    a.activation(HT2[:, c, :], bank[2 + c % 2][:, :], ACT.Identity, scale=cc("f_ln2_g", c), bias=cc("f_ln2_b", c)).then_inc(ft_evac, 1)
            for_blocks(act, ffn_act)

        @block.vector
        def _(dve):
            v = nc.vector

            def stats(src):
                for i in range(NT):
                    v.bn_stats(ST[:, i, :], src[:, i, :])
                dve.drain()
                for i in range(NT):
                    v.bn_aggr(MV[:, i, :], ST[:, i, :])
                dve.drain()

            def norm(kind, src, dst, idx, first):
                stats(src)
                if kind == "ln":
                    v.tensor_copy(MS2[:, :], MV[:, :, 1]).then_inc(var_ready, 1)
                else:
                    v.tensor_tensor(MS2[:, :], MV[:, :, 0], MV[:, :, 0], ALU.mult)
                    dve.drain()
                    v.tensor_tensor(MS2[:, :], MS2[:, :], MV[:, :, 1], ALU.add).then_inc(var_ready, 1)

            def scale(kind, src, dst, idx):
                dve.wait_ge(rstd_ready, idx + 1)
                for i in range(NT):
                    if kind == "ln":
                        r = v.tensor_scalar(dst[:, i, :], src[:, i, :], MV[:, i, 0:1], RSTD[:, i:i + 1], ALU.subtract, ALU.mult)
                    else:
                        r = v.tensor_scalar(dst[:, i, :], src[:, i, :], RSTD[:, i:i + 1], None, ALU.mult)
                return r

            def post_sum(p, b):
                pi = post_index(p, b)
                dve.wait_ge(y_ready, pi + 1)
                before = NB * LAST if p == LAST else pi
                at_least(dve, x_saved, before)
                at_least(dve, xt_ready, before)
                if p == LAST:
                    at_least(dve, out_done, b * 16)
                if p == L2_MOE:
                    v.tensor_tensor(YB[:, :, :], tiles(Y[:, :]), tiles(blk(X1, b)), ALU.add).then_inc(y_added, 1)
                    dve.drain()
                    v.tensor_tensor(YB[:, :, :], YB[:, :, :], tiles(blk(X, b)), ALU.add)
                else:
                    v.tensor_tensor(YB[:, :, :], tiles(Y[:, :]), tiles(blk(X, b)), ALU.add).then_inc(y_added, 1)
                dve.drain()
                norm(NORMS[p][0], YB, N1, 0, True)

            def post_norm(p, b):
                n0 = norm_index(p, b)
                if len(NORMS[p]) == 1:
                    scale(NORMS[p][0], YB, N2 if p == L2_GQA else N1, n0).then_inc(normed, 1)
                    return
                scale(NORMS[p][0], YB, N1, n0)
                dve.drain()
                norm(NORMS[p][1], N1, N2, 1, False)
                scale(NORMS[p][1], N1, N2, n0 + 1).then_inc(normed, 1)

            dve.wait_ge(ld_0, 48)
            v.tensor_reduce(sel0[:, 4, 2:3], rc("logits"), AX_X, ALU.max)
            dve.drain()
            v.tensor_scalar(sel0[:, 2, :], rc("logits"), sel0[:, 4, 2:3], None, ALU.subtract).then_inc(z2_sem, 1)
            dve.wait_ge(z_sem, 2)
            v.tensor_scalar(sel0[:, 5, :], sel0[:, 2, :], sel0[:, 4, 1:2], None, ALU.subtract)
            dve.drain()
            v.tensor_tensor(sel0[:, 6, :], sel0[:, 5, :], sel0[:, 1, :], ALU.subtract)
            dve.drain()
            v.tensor_reduce(sel0[:, 4, 3:4], sel0[:, 6, :], AX_X, ALU.max)
            dve.drain()
            dve.wait_ge(pool_const, 2)
            v.scalar_tensor_tensor(sel0[:, 7, :], sel0[:, 6, :], sel0[:, 4, 3:4], rev[:, :], ALU.is_ge, ALU.mult)
            dve.drain()
            v.tensor_reduce(sel0[:, 4, 4:5], sel0[:, 7, :], AX_X, ALU.max)
            dve.drain()
            v.tensor_scalar(sel0[:, 8, :], sel0[:, 7, :], sel0[:, 4, 4:5], None, ALU.is_equal)
            dve.drain()
            for i in range(E):
                b0 = rc("l0_b")[:, i * P:(i + 1) * P]
                if i == 0:
                    v.tensor_scalar(WSEL[:, :], W0[:, 0, :], sel0[:, 8, 0:1], None, ALU.mult)
                    r = v.tensor_scalar(BSEL[:, :], b0, sel0[:, 8, 0:1], None, ALU.mult)
                else:
                    v.scalar_tensor_tensor(WSEL[:, :], W0[:, i, :], sel0[:, 8, i:i + 1], WSEL[:, :], ALU.mult, ALU.add)
                    r = v.scalar_tensor_tensor(BSEL[:, :], b0, sel0[:, 8, i:i + 1], BSEL[:, :], ALU.mult, ALU.add)
                dve.drain()
            v.tensor_scalar(cols0[:, 0:1], cc("mix"), -1.0, 1.0, ALU.mult, ALU.add).then_inc(c0b, 1)
            v.tensor_scalar(zcol[:, :], cc("mix"), 0.0, None, ALU.mult).then_inc(sel_ready, 1)
            dve.drain().then_inc(o_normed, 1)
            dve.wait_ge(c0a, 1)
            dve.wait_ge(ld_x, 48)

            def layer0_dve(b):
                xb = XTP[:, b, 1:T + 1] if isinstance(b, int) else XTP[:, bass.ds(b, 1), 1:T + 1].rearrange("p a b -> p (a b)")
                dve.wait_ge(xm0_ready, b + 1)
                v.scalar_tensor_tensor(XM, xb, cc("mix"), XM0, ALU.mult, ALU.add).then_inc(xm_ready, 1)
                dve.wait_ge(kvr_ready, b + 1)
                v.tensor_scalar(KM, bank[0][:, :], 60.0, None, ALU.min).then_inc(km_ready, 1)
                dve.wait_ge(ke_ready, b + 1)
                v.tensor_tensor(KV, KE, bank[1][:, :], ALU.mult)
                dve.drain()
                for i, src in enumerate((KV, KE)):
                    v.tensor_tensor_scan(SA[:, i, 1:T + 1], cols0[:, 2:3].to_broadcast([P, T]), src, 0.0, ALU.mult, ALU.add)
                dve.drain()
                v.scalar_tensor_tensor(KV, KV, cols0[:, 3:4], SA[:, 0, 0:T], ALU.mult, ALU.add)
                v.scalar_tensor_tensor(KE, KE, cols0[:, 3:4], SA[:, 1, 0:T], ALU.mult, ALU.add)
                dve.drain()
                v.tensor_scalar(KE, KE, 1e-9, None, ALU.add)
                dve.drain()
                v.reciprocal(KE, KE)
                dve.drain()
                v.tensor_tensor(KV, KV, KE, ALU.mult)
                dve.drain()
                dve.wait_ge(sg_ready, b + 1)
                v.tensor_tensor(RWKV, KV, SG, ALU.mult).then_inc(rwkv_ready, 1)
                post_sum(L0_MIX, b)
                post_norm(L0_MIX, b)
                post_sum(L0_LINEAR, b)
                post_norm(L0_LINEAR, b)
            for_blocks(dve, layer0_dve)

            def prep_dve(L, b, i):
                c = LAYERS[L]
                B = b + NB * L
                base = b * PREP_USES[L] + PREP_BASE[L]
                what = prep_uses(L)[i]
                nk = c["kv"] * HD
                if what == "v":
                    if c["alibi"]:
                        dve.wait_ge(proj_ready, base + i + 1)
                        at_least(dve, v_placed, B * NG)
                        v.tensor_tensor(VST[:, :, 0:nk], tiles(bank[6][:, :])[:, :, 0:nk],
                                        rc("bv").rearrange("p (a b) -> p a b", a=1).to_broadcast([P, NT, nk]), ALU.add).then_inc(prep_evac, 1)
                elif c["rope"] is not None:
                    n, k = (P, 0) if what[0] == "q" else (nk, 1)
                    sw = len(what) == 2
                    dve.wait_ge(proj_ready, base + i + 1)
                    at_least(dve, parts_ready, B * 2 - 1 + k)
                    v.tensor_tensor((RB if sw else RA)[0:n, k, :], bank[6][0:n, :], tables[0:n, c["rope"], int(sw), :],
                                    ALU.mult).then_inc(prep_evac, 1)

            def reduce(L, b, g, i):
                w = U(L, b, g)
                kl = k_to(L, i // GH)
                dve.wait_ge(s_ready, w * 16 + i + 1)
                v.tensor_reduce(M[g % 2][:, i:i + 1], bank[i % 2][:, 0:kl], AX_X, ALU.max, negate=True).then_inc(max_done, 1)

            def shift(L, b, g):
                w = U(L, b, g)
                m = M[g % 2][:, :].rearrange("p (t j) -> p t j", j=GH)
                r = MR[:, :].rearrange("p (t j) -> p t j", j=GH)
                s = MS[g % 2]
                dve.drain()
                at_least(dve, mt_ready, w - 1)
                v.tensor_copy(s[:, :, 0, :], m)
                dve.drain()
                v.tensor_tensor(r, m, s[:, :, 0, :], ALU.subtract)
                dve.drain()
                v.tensor_copy(s[:, :, 1, :], r)
                dve.drain()
                v.tensor_tensor(s[:, :, 2, :], r, s[:, :, 1, :], ALU.subtract).then_inc(m_split, 1)

            def o_norm(L, b, g, u):
                dve.wait_ge(ot_ready, u + 1)
                o = bank[7][:, :].rearrange("p (t j e) -> p t j e", t=NT, j=GH)
                r = OR[:, :].rearrange("p (t j e) -> p t j e", t=NT, j=GH)
                v.reciprocal(r, o[:, :, :, HD:HD + 1])
                dve.drain()
                v.tensor_tensor(AO[:, :, g * 32:(g + 1) * 32].rearrange("p t (j e) -> p t j e", j=GH), o[:, :, :, 0:HD],
                                r.to_broadcast([P, NT, GH, HD]), ALU.mult).then_inc(o_normed, 1)

            def attention_dve(L):
                p = LAYERS[L]["phase"]
                for i in range(PREP_USES[L]):
                    prep_dve(L, 0, i)
                for g in range(2):
                    for i in range(16):
                        reduce(L, 0, g, i)
                    shift(L, 0, g)
                places = prep_places(L)

                def unit(b, g, ahead=None, prep=None, end=None):
                    u = U(L, b, g)
                    for kt in range(NT):
                        for j in range(GH):
                            if ahead is not None:
                                reduce(L, *ahead, kt * GH + j)
                            if prep is not None and j % 2 and (kt, j - 1) in places:
                                prep_dve(L, prep, places[(kt, j - 1)])
                            if kt == 1 and j == 2 and not (isinstance(b, int) and b == 0 and g == 0):
                                if g:
                                    o_norm(L, b, g - 1, u - 1)
                                else:
                                    o_norm(L, b - 1, NG - 1, u - 1)
                            if end is not None and kt == 2 and j == 3:
                                post_sum(p, end)
                            if end is not None and kt == 3 and j == 1:
                                post_norm(p, end)
                    if ahead is not None:
                        shift(L, *ahead)
                sequence(L, unit, dve.Fori)
                o_norm(L, NB - 1, NG - 1, U(L, NB - 1, NG - 1))
                post_sum(p, NB - 1)
                post_norm(p, NB - 1)

            def top(src, onehot, tmp, keep):
                bc = lambda t: t.rearrange("p (a b) -> p a b", b=1).to_broadcast([P, NB * NT, E])
                v.tensor_reduce(GM[:, :], src, AX_X, ALU.max)
                dve.drain()
                v.tensor_tensor(tmp, src, bc(GM[:, :]), ALU.is_ge)
                dve.drain()
                v.tensor_tensor(tmp, tmp, rev[:, :].rearrange("p (a b) -> p a b", a=1).to_broadcast([P, NB * NT, E]), ALU.mult)
                dve.drain()
                v.tensor_reduce(GM[:, :], tmp, AX_X, ALU.max)
                dve.drain()
                v.tensor_tensor(onehot, tmp, bc(GM[:, :]), ALU.is_equal)
                dve.drain()

            def gates(p):
                gi = 0 if p == L1_MOE else 1
                bc = lambda t: t.rearrange("p (a b) -> p a b", b=1).to_broadcast([P, NB * NT, E])
                dve.wait_ge(lg_ready, gi + 1)
                lg = bank[5][:, 0:NB * NT * E].rearrange("p (a b) -> p a b", b=E)
                v.tensor_reduce(GM[:, :], lg, AX_X, ALU.max)
                dve.drain()
                v.tensor_tensor(GL[:, :, :], lg, bc(GM[:, :]), ALU.subtract).then_inc(gm_ready, 1)
                dve.wait_ge(ge_ready, gi + 1)
                v.tensor_reduce(GM[:, :], GE[:, :, :], AX_X, ALU.add)
                dve.drain()
                v.reciprocal(GM[:, :], GM[:, :])
                dve.drain()
                v.tensor_tensor(GE[:, :, :], GE[:, :, :], bc(GM[:, :]), ALU.mult)
                dve.drain()
                if p == L1_MOE:
                    v.tensor_tensor(GB[:, :, :], GE[:, :, :], rc("gate_b").rearrange("p (a b) -> p a b", a=1).to_broadcast([P, NB * NT, E]), ALU.add)
                else:
                    v.tensor_copy(GB[:, :, :], GE[:, :, :])
                dve.drain()
                top(GB[:, :, :], GO[:, :, :], GR[:, :, :], True)
                v.scalar_tensor_tensor(GB[:, :, :], GO[:, :, :], MASKED, GB[:, :, :], ALU.mult, ALU.add)
                dve.drain()
                top(GB[:, :, :], GL[:, :, :], GR[:, :, :], False)
                v.tensor_tensor(GO[:, :, :], GO[:, :, :], GL[:, :, :], ALU.add)
                dve.drain()
                w = GW[:, :, 0:E]
                v.memset(GW[:, :, E:NGATE], 1.0 if p == L1_MOE else 0.0)
                v.tensor_tensor(w, GE[:, :, :], GO[:, :, :], ALU.mult)
                dve.drain()
                if p == L2_MOE:
                    v.tensor_reduce(GM[:, :], w, AX_X, ALU.add)
                    dve.drain()
                    v.reciprocal(GM[:, :], GM[:, :])
                    dve.drain()
                    v.tensor_tensor(w, w, bc(GM[:, :]), ALU.mult)
                    dve.drain()
                v.tensor_copy(GWP[:, :, 0, :], GW[:, :, :])
                dve.drain()
                v.tensor_tensor(GWR[:, :, :], GW[:, :, :], GWP[:, :, 0, :], ALU.subtract)
                dve.drain()
                v.tensor_copy(GWP[:, :, 1, :], GWR[:, :, :])
                dve.drain()
                v.tensor_tensor(GWP[:, :, 2, :], GWR[:, :, :], GWP[:, :, 1, :], ALU.subtract).then_inc(gw_ready, 1)

            def moe_dve(p):
                gates(p)
                n = MOE_CHUNKS[p]

                def body(b):
                    k0 = b * n + MOE_BASE[p]
                    for c in range(n + 1):
                        if c < n:
                            dve.wait_ge(a_evac, k0 + c + 1)
                            if p == L1_MOE:
                                at_least(dve, s1_ready, b * n + c - 1)
                                v.scalar_tensor_tensor(U1[c % 2], bank[2 + c % 2][:, :], cc("m_b3", c), A1[c % 2], ALU.add, ALU.mult).then_inc(u_ready, 1)
                            else:
                                v.tensor_tensor(U1[c % 2], bank[2 + c % 2][:, :], A1[c % 2], ALU.mult).then_inc(u_ready, 1)
                        if c:
                            if p == L1_MOE:
                                dve.wait_ge(s1_ready, b * n + c)
                            else:
                                dve.drain()
                            at_least(dve, yc_done, k0 + c - 2)
                            v.tensor_tensor(H1[(c - 1) % 2], bank[4 + (c - 1) % 2][:, :], (S1 if p == L1_MOE else U1)[(c - 1) % 2],
                                            ALU.mult).then_inc(h_ready, 1)
                    post_sum(p, b)
                    post_norm(p, b)
                for_blocks(dve, body)

            def ternary():
                dve.wait_ge(ld_f, 48)
                w2 = FW2[:, :, :].rearrange("p a b -> p (a b)")
                v.tensor_reduce(qa[:, 0, 0:1], FW1[:, :], AX_X, ALU.add, apply_absolute_value=True)
                v.tensor_reduce(qa[:, 0, 1:2], w2, AX_X, ALU.add, apply_absolute_value=True).then_inc(qs_ready, 1)
                dve.wait_ge(qm_ready, 1)
                v.tensor_scalar(qa[:, 0, 2:4], bank[5][:, 0:2], 1.0 / (T * P), 1e-5, ALU.mult, ALU.max)
                dve.drain()
                v.reciprocal(qa[:, 0, 4:6], qa[:, 0, 2:4])
                dve.drain()
                v.reciprocal(qa[:, 0, 6:8], qa[:, 0, 4:6])
                dve.drain()
                for i, w in enumerate((FW1[:, :], w2)):
                    v.tensor_scalar(qt0[:, :], w, qa[:, 0, 4 + i:5 + i], 12582912.0, ALU.mult, ALU.add)
                    dve.drain()
                    v.tensor_scalar(qt0[:, :], qt0[:, :], 12582912.0, 1.0, ALU.subtract, ALU.min)
                    dve.drain()
                    v.tensor_scalar(qt0[:, :], qt0[:, :], -1.0, qa[:, 0, 6 + i:7 + i], ALU.max, ALU.mult)
                    dve.drain()
                    v.tensor_tensor(qt0[:, :], qt0[:, :], w, ALU.subtract)
                    dve.drain()
                    v.tensor_tensor(w, w, qt0[:, :], ALU.add)
                    dve.drain()
                v.tensor_scalar(bqs[:, :], cc("bq"), HD ** -0.5, None, ALU.mult)
                v.tensor_copy(slope_p[:, 0:1], slope[:, :])
                dve.drain()
                v.tensor_tensor(slope_r[:, :], slope[:, :], slope_p[:, 0:1], ALU.subtract)
                dve.drain()
                v.tensor_copy(slope_p[:, 1:2], slope_r[:, :])
                dve.drain()
                v.tensor_tensor(slope_p[:, 2:3], slope_r[:, :], slope_p[:, 1:2], ALU.subtract)
                dve.drain()
                v.tensor_copy(slope_w[:, :, :], slope_p[:, :].rearrange("p (a b) -> p a b", b=1).to_broadcast([H, PARTS, T])).then_inc(slope_ready, 1)

            attention_dve(0)
            moe_dve(L1_MOE)
            ternary()
            attention_dve(1)
            attention_dve(2)
            moe_dve(L2_MOE)
            attention_dve(3)

            def ffn_dve(b):
                for i in range(NT):
                    dve.wait_ge(fu_ready, b * NT + i + 1)
                    if i == 0:
                        at_least(dve, ft_ready, b * 4)
                    v.tensor_tensor(HG[:, i, :], bank[i % 2][:, :], rc("f_b1"), ALU.add).then_inc(fb_ready, 1)
                for i in range(NT):
                    dve.wait_ge(fg_ready, b * NT + i + 1)
                    v.bn_stats(FST[:, i, :], HG[:, i, :])
                dve.drain()
                for i in range(NT):
                    v.bn_aggr(MV[:, i, :], FST[:, i, :])
                dve.drain()
                v.tensor_copy(MS2[:, :], MV[:, :, 1]).then_inc(fv_ready, 1)
                dve.wait_ge(fr_ready, b + 1)
                for i in range(NT):
                    r = v.tensor_scalar(HG[:, i, :], HG[:, i, :], MV[:, i, 0:1], RSTD[:, i:i + 1], ALU.subtract, ALU.mult)
                r.then_inc(fn_ready, 1)
                post_sum(LAST, b)
                post_norm(LAST, b)
            for_blocks(dve, ffn_dve)

        @block.tensor
        def _(pe):
            mm = nc.tensor.matmul
            tr = nc.tensor.transpose

            def xt(p, b, to):
                src = N2 if p in (L2_ATTN, L2_GQA, L3_ATTN) else N1
                pe.wait_ge(normed, post_index(p, b) + 1)
                at_least(pe, xt_evac, post_index(p, b))
                for i in range(NT):
                    r = tr(to[:, i * P:(i + 1) * P], src[:, i, :], ident[:, :])
                r.then_inc(xt_ready, 1)

            def y_out(lhs, w, b, p):
                for i in range(NT):
                    r = mm(Y[:, i * P:(i + 1) * P], lhs[:, i * P:(i + 1) * P], w, start=True, stop=True)
                r.then_inc(y_ready, 1)

            pe.wait_ge(ld_w, 16)
            pe.wait_ge(ld_x, 48)

            def layer0_pe(b):
                pe.wait_ge(xm_ready, b + 1)
                at_least(pe, xt_evac, b * 2)
                for i, n in enumerate(("l0_k", "l0_v", "l0_r")):
                    r = mm(bank[i][:, :], wc(n), XM, start=True, stop=True)
                r.then_inc(kvr_ready, 1)
                pe.wait_ge(rwkv_ready, b + 1)
                y_out(RWKV, wc("l0_o"), b, L0_MIX)
                xt(L0_MIX, b, bank[7])
                pe.wait_ge(xt_evac, b * 2 + 1)
                pe.wait_ge(sel_ready, 1)
                y_out(XTS, WSEL[:, :], b, L0_LINEAR)
                xt(L0_LINEAR, b, bank[7])
            for_blocks(pe, layer0_pe)

            def prep_pe(L, b, i):
                c = LAYERS[L]
                B = b + NB * L
                base = b * PREP_USES[L] + PREP_BASE[L]
                what = prep_uses(L)[i]
                at_least(pe, prep_evac, base + i)
                if i == 0:
                    at_least(pe, xt_evac, post_index(c["phase"] - 1, b) + 1)
                    if not isinstance(b, int):
                        pe.wait_ge(xt_evac, b + NB * c["phase"] - 1)
                w = attn_weights(L)[("q", "qs", "k", "ks", "v").index(what)]
                n = w.shape[1]
                if what == "v":
                    pe.wait_ge(xts_ready, B + 1)
                    for t in range(NT):
                        r = mm(bank[6][:, t * P:t * P + n], XTS[:, t * P:(t + 1) * P], w, start=True, stop=True)
                else:
                    if not isinstance(b, int) and n < P:
                        pe.sem_inc(pe_passed, 1)
                    r = mm(bank[6][0:n, :], w, blk(XT, b), start=True, stop=True)
                r.then_inc(proj_ready, 1)

            def score(L, b, g, i):
                w = U(L, b, g)
                t, j = divmod(i, GH)
                kl = k_to(L, t)
                if i == 0:
                    pe.wait_ge(stack_landed[g], (b + NB * L + 1) * 32)
                    if LAYERS[L]["alibi"]:
                        pe.wait_ge(alibi_rows, 7 * 16)
                at_least(pe, max_done, w * 16 + i - 1)
                s = bank[i % 2]
                r = mm(s[:, 0:kl], QS[0:ROWS_SHIFT, g * GH + j, t * P:(t + 1) * P], KS[0:ROWS_SHIFT, kv_slot(L, g, j), 0:kl],
                       start=True, stop=not LAYERS[L]["causal"])
                if LAYERS[L]["causal"]:
                    r = mm(s[:, kl - P:kl], identb[:, :], maskb[:, :], start=False, stop=True)
                r.then_inc(s_ready, 1)

            def score_t(L, b, g, kt, j):
                u = U(L, b, g)
                n = u * 16 + kt * GH + j
                q0 = q_from(L, kt)
                if kt == 0 and j == 0:
                    pe.wait_ge(shift_landed[g % 2], (half(L, b, g) + 1) * 48)
                at_least(pe, exp_done, n - 1)
                s = bank[2 + j % 2]
                r = mm(s[:, 0:T - q0], KS[:, kv_slot(L, g, j), kt * P:(kt + 1) * P], QS[:, g * GH + j, q0:T],
                       start=True, stop=not LAYERS[L]["causal"])
                if LAYERS[L]["causal"]:
                    r = mm(s[:, 0:P], maskb[:, :], identb[:, :], start=False, stop=True)
                r.then_inc(st_ready, 1)

            def values(L, b, g, kt):
                u = U(L, b, g)
                q0 = q_from(L, kt)
                if kt == 0:
                    pe.wait_ge(v_placed, u + 1)
                pe.wait_ge(exp_done, u * 16 + kt * GH + GH)
                for j in range(GH):
                    r = mm(bank[4 + g % 2][32 * j:32 * (j + 1), q0:T], VA[:, kt, kv_slot(L, g, j), :], PT[kt % 2][:, j, q0:T],
                           start=(kt == 0), stop=(kt == NT - 1))
                r.then_inc(pv_done, 1)

            def shift_t(L, b, g):
                w = U(L, b, g)
                pe.wait_ge(m_split, w + 1)
                pe.wait_ge(o_normed, w - 1) if not isinstance(w, int) or w > 1 else None
                to = bank[7][0:PARTS * GH, 0:T // 2].bitcast(BF16)
                for t in range(NT):
                    r = tr(to[:, t * P:(t + 1) * P], MS[g % 2][:, t, :, :].rearrange("p a b -> p (a b)"), identb[:, :])
                r.then_inc(mt_ready, 1)

            def o_t(L, u, shifts, last=False):
                pe.wait_ge(o_evac, u + 1)
                pe.wait_ge(m_evac, shifts)
                if last:
                    pe.wait_ge(o_normed, u + 1)
                for t in range(NT):
                    r = tr(bank[7][:, t * P:(t + 1) * P], OT[:, t * P:(t + 1) * P], ident[:, :])
                r.then_inc(ot_ready, 1)

            def ao_t(L, b, preps):
                pe.wait_ge(o_normed, U(L, b, NG - 1) + 2)
                at_least(pe, prep_evac, preps)
                for t in range(NT):
                    r = tr(bank[6][:, t * P:(t + 1) * P], AO[:, t, :], ident[:, :])
                r.then_inc(ao_ready, 1)

            def attention_pe(L):
                c = LAYERS[L]
                p = c["phase"]
                wo = attn_weights(L)[5]
                at_least(pe, xt_evac, NB * p)
                if L == 0:
                    pe.wait_ge(ld_1, 16 * (2 + 3 * H + 4))
                    pe.wait_ge(pool_const, 4)
                for i in range(PREP_USES[L]):
                    prep_pe(L, 0, i)
                for g in range(2):
                    for i in range(16):
                        score(L, 0, g, i)
                shift_t(L, 0, 0)
                places = prep_places(L)

                def unit(b, g, ahead=None, prep=None, end=None):
                    u = U(L, b, g)
                    first = isinstance(b, int) and b == 0 and g == 0
                    last = g == 3 and ahead is None
                    for kt in range(NT):
                        for j in range(GH):
                            score_t(L, b, g, kt, j)
                            if ahead is not None:
                                score(L, *ahead, kt * GH + j)
                            if prep is not None and (kt, j) in places:
                                prep_pe(L, prep, places[(kt, j)])
                            if j == 1 and kt:
                                values(L, b, g, kt - 1)
                            if j == 1 and kt == 0 and not first:
                                values(L, b - 1 if g == 0 else b, (g - 1) % NG, NT - 1)
                            if kt == 0 and j == 3 and not last:
                                shift_t(L, b + (g + 1) // NG, (g + 1) % NG)
                            if kt == 1 and j == 1 and not first:
                                o_t(L, u - 1, u + 1 if last else u + 2, last)
                            if end is not None and (kt, j) == (2, 0):
                                ao_t(L, end, (end + 2) * PREP_USES[L] + PREP_BASE[L])
                            if end is not None and (kt, j) == (2, 3):
                                pe.wait_ge(ao_evac, end + NB * L + 1)
                                y_out(AOT, wo, end, p)
                            if end is not None and (kt, j) == (3, 3):
                                xt(p, end, bank[6])
                sequence(L, unit, pe.Fori)
                values(L, NB - 1, NG - 1, NT - 1)
                o_t(L, U(L, NB - 1, NG - 1), U(L, NB - 1, NG - 1) + 1, True)
                ao_t(L, NB - 1, NB * PREP_USES[L] + PREP_BASE[L])
                pe.wait_ge(ao_evac, NB * L + NB)
                y_out(AOT, wo, NB - 1, p)
                xt(p, NB - 1, bank[6])

            def moe_pe(p):
                gi = 0 if p == L1_MOE else 1
                n = MOE_CHUNKS[p]
                pe.wait_ge(xt_evac, NB * p)
                pe.wait_ge(ld_m1 if p == L1_MOE else ld_m2, 80 if p == L1_MOE else 64)
                pe.wait_ge(pool_const, 5)
                for i in range(NB * NT):
                    r = mm(bank[5][:, i * E:(i + 1) * E], XT[:, i * P:(i + 1) * P], wc("l1_gate" if p == L1_MOE else "l2_gate"),
                           start=True, stop=True)
                r.then_inc(lg_ready, 1)
                pe.wait_ge(gw_ready, gi + 1)
                for b in range(NB):
                    at_least(pe, gt_evac, (gi * NB + b) * 2)
                    for i in range(NT):
                        r = tr(bank[6][0:NGATE, i * P:(i + 1) * P], GW[:, b * NT + i, :], ident[:, :])
                    r.then_inc(gt_ready, 1)
                    to = bank[7][0:PARTS * NGATE, 0:T // 2].bitcast(BF16)
                    for i in range(NT):
                        r = tr(to[:, i * P:(i + 1) * P], GWP[:, b * NT + i, :, :].rearrange("p a b -> p (a b)"), identb[:, :])
                    r.then_inc(gt_ready, 1)
                pe.wait_ge(gt_evac, (gi * NB + NB) * 2)

                def up(b, c):
                    k0 = b * n + MOE_BASE[p]
                    at_least(pe, u_ready, k0 + c - 1)
                    at_least(pe, h_ready, k0 + c - 1)
                    mm(bank[c % 2][:, :], MW1[:, c * P:(c + 1) * P], blk(XT, b), start=True, stop=True)
                    mm(bank[2 + c % 2][:, :], MW3[:, c * P:(c + 1) * P], blk(XT, b), start=True, stop=True)
                    mm(bank[4 + c % 2][:, :], SEL[:, c, :], blk(RWT, b), start=True, stop=True).then_inc(ab_ready, 1)

                def down(b, c):
                    k0 = b * n + MOE_BASE[p]
                    if c == 0:
                        at_least(pe, y_added, b + NB * p)
                    pe.wait_ge(h_ready, k0 + c + 1)
                    for i in range(NT):
                        r = mm(Y[:, i * P:(i + 1) * P], H1[c % 2][:, i * P:(i + 1) * P], MW2[:, c, :], start=(c == 0 and i == 0),
                               stop=(p == L2_MOE and c == n - 1), skip_group_check=True)
                    r.then_inc(yc_done, 1)

                def body(b):
                    for c in range(n + 1):
                        if c < n:
                            up(b, c)
                        if c:
                            down(b, c - 1)
                    if p == L1_MOE:
                        pe.wait_ge(rwb_ready, b + 1)
                        for i in range(NT):
                            r = mm(Y[:, i * P:(i + 1) * P], RWB[:, i * P:(i + 1) * P], MB2[:, :], start=False, stop=True, skip_group_check=True)
                    else:
                        r = None
                    if r is not None:
                        r.then_inc(y_ready, 1)
                    else:
                        pe.drain().then_inc(y_ready, 1)
                    xt(p, b, bank[7])
                for_blocks(pe, body)
                if p == L1_MOE:
                    pe.wait_ge(qs_ready, 1)
                    mm(bank[5][:, 0:2], ones[:, :], qa[:, 0, 0:2], start=True, stop=True).then_inc(qm_ready, 1)

            attention_pe(0)
            moe_pe(L1_MOE)
            attention_pe(1)
            attention_pe(2)
            moe_pe(L2_MOE)
            attention_pe(3)

            def ffn_pe(b):
                pe.wait_ge(xts_ready, b + NB * 4 + 1)
                for i in range(NT):
                    at_least(pe, fb_ready, b * NT + i - 1)
                    if i == 0:
                        pe.wait_ge(xt_evac, NB * LAST)
                    mm(bank[i % 2][:, :], XTS[:, i * P:(i + 1) * P], FW1[:, :], start=True, stop=True).then_inc(fu_ready, 1)
                pe.wait_ge(fn_ready, b + 1)
                for c in range(4):
                    at_least(pe, ft_evac, b * 4 + c - 1)
                    for i in range(NT):
                        r = tr(bank[2 + c % 2][:, i * P:(i + 1) * P], HG[:, i, c * P:(c + 1) * P], ident[:, :])
                    r.then_inc(ft_ready, 1)
                at_least(pe, y_added, b + NB * LAST)
                for c in range(4):
                    pe.wait_ge(ft_evac, b * 4 + c + 1)
                    for i in range(NT):
                        r = mm(Y[:, i * P:(i + 1) * P], HT2[:, c, i * P:(i + 1) * P], FW2[:, c, :], start=(c == 0 and i == 0), stop=(c == 3),
                               skip_group_check=True)
                r.then_inc(y_ready, 1)
            for_blocks(pe, ffn_pe)


def _rotary(interleaved):
    freqs = np.float32(1.0) / np.float32(10000.0) ** (np.arange(0, HD, 2, dtype=np.float32) / np.float32(HD))
    angle = np.arange(T, dtype=np.float32)[None, :] * freqs[:, None].astype(np.float32)
    ch = np.arange(P) % HD
    f = ch // 2 if interleaved else ch % (HD // 2)
    sign = np.where((ch % 2 == 0) if interleaved else (ch < HD // 2), -1.0, 1.0).astype(np.float32)
    return np.stack([np.cos(angle)[f], np.sin(angle)[f] * sign[:, None]]).astype(np.float32)


def _swap(n, interleaved):
    ch = np.arange(n)
    return ch ^ 1 if interleaved else ch ^ (HD // 2)


def kernel(**inputs):
    import ml_dtypes
    import concourse.bacc as bacc
    from concourse.bass_utils import run_bass_kernel_spmd

    a = {k: np.asarray(x) for k, x in inputs.items()}
    c = np.ascontiguousarray
    bf = ml_dtypes.bfloat16
    arrays = {}
    x = a["L0_attn_x"]
    arrays["L0_attn_x"] = c(x)
    arrays["xT"] = c(x.reshape(NB * T, P).T)
    qkv = a["L2_ffn_wqkv"].T
    gq, gk, gv = qkv[:, :P], qkv[:, P:P + 32], qkv[:, P + 32:P + 64]
    l2q, l2k = a["L2_attn_wq"].T, a["L2_attn_wk"].T
    w = {"l0_k": a["L0_attn_Wk"].T, "l0_v": a["L0_attn_Wv"].T, "l0_r": a["L0_attn_Wr"].T, "l0_o": a["L0_attn_Wo"].T,
         "l1_out": a["L1_attn_W_out"].T, "l2_q": l2q, "l2_qs": l2q[:, _swap(P, True)], "l2_k": l2k,
         "l2_ks": l2k[:, _swap(P, True)], "l2_v": a["L2_attn_wv"].T, "l2_o": a["L2_attn_wo"].T,
         "g_q": gq, "g_qs": gq[:, _swap(P, False)], "g_k": gk, "g_ks": gk[:, _swap(32, False)], "g_v": gv,
         "g_o": a["L2_ffn_wo"].T, "l3_q": a["L3_attn_Wq"], "l3_k": a["L3_attn_Wk"], "l3_v": a["L3_attn_Wv"],
         "l3_o": a["L3_attn_Wo"], "l1_gate": a["L1_ffn_gate_w"].T, "l2_gate": a["L2_ffn_gate_w"].T}
    arrays["wpack"] = c(np.concatenate([w[n] for n in W_COLS], axis=1))

    def col(v):
        out = np.zeros((-(-v.size // P) * P,), np.float32)
        out[:v.size] = v.reshape(-1)
        return out.reshape(-1, P).T

    hidden = np.concatenate([a["L1_ffn_b1"].reshape(-1), a["L1_ffn_sb1"]])
    hidden3 = np.concatenate([a["L1_ffn_b3"].reshape(-1), a["L1_ffn_sb3"]])
    cols = {"decay": a["L0_attn_time_decay"], "first": a["L0_attn_time_first"], "mix": a["L0_attn_time_mix"],
            "ln1_w": a["L2_ffn_ln1_w"], "ln2_w": a["L2_ffn_ln2_w"], "bq": a["L3_attn_bq"], "bk": a["L3_attn_bk"],
            "f_ln1_g": a["L3_ffn_ln1_g"], "f_ln1_b": a["L3_ffn_ln1_b"], "f_ln2_g": a["L3_ffn_ln2_g"],
            "f_ln2_b": a["L3_ffn_ln2_b"], "m_b1": hidden, "m_b3": hidden3}
    arrays["cols"] = c(np.concatenate([col(cols[n]) for n in C_COLS], axis=1))
    rows = {"logits": a["L0_ffn_logits"], "u": a["L0_ffn_u"], "l0_b": a["L0_ffn_b"], "gate_b": a["L1_ffn_gate_b"],
            "b_out": a["L1_attn_b_out"], "bv": a["L3_attn_bv"], "bo": a["L3_attn_bo"], "f_b1": a["L3_ffn_b1"], "f_b2": a["L3_ffn_b2"]}
    arrays["rows"] = c(np.concatenate([rows[n].reshape(-1) for n in R_COLS]))
    arrays["L0_ffn_W"] = c(a["L0_ffn_W"])
    for n, k in (("l1_wq", "L1_attn_Wq"), ("l1_wk", "L1_attn_Wk"), ("l1_wv", "L1_attn_Wv")):
        arrays[n] = c(a[k].T)
    arrays["ident"] = np.eye(P, dtype=np.float32)
    arrays["identb"] = np.eye(P).astype(bf)
    arrays["maskb"] = np.where(np.arange(P)[None, :] > np.arange(P)[:, None], MASKED, 0.0).astype(bf)
    arrays["tables"] = c(np.stack([_rotary(True), _rotary(False)]))
    f1 = a["L1_ffn_w1"].shape[2]
    n1 = 13 * P

    def up(we, ws):
        out = np.zeros((P, n1), np.float32)
        out[:, :E * f1] = we.transpose(1, 0, 2).reshape(P, E * f1)
        out[:, E * f1:(E + 1) * f1] = ws
        return out

    arrays["m1_w1"], arrays["m1_w3"] = up(a["L1_ffn_w1"], a["L1_ffn_sw1"]), up(a["L1_ffn_w3"], a["L1_ffn_sw3"])
    w2 = np.zeros((n1, P), np.float32)
    w2[:E * f1] = a["L1_ffn_w2"].reshape(E * f1, P)
    w2[E * f1:(E + 1) * f1] = a["L1_ffn_sw2"]
    arrays["m1_w2"] = c(w2.reshape(13, P, P).transpose(1, 0, 2))
    arrays["m1_b2"] = c(np.concatenate([a["L1_ffn_b2"], a["L1_ffn_sb2"][None]]))
    w13 = a["L2_ffn_w13"]
    f2 = w13.shape[1] // 2
    arrays["m2_w1"] = c(w13[:, :f2].transpose(2, 0, 1).reshape(P, E * f2))
    arrays["m2_w3"] = c(w13[:, f2:].transpose(2, 0, 1).reshape(P, E * f2))
    arrays["m2_w2"] = c(a["L2_ffn_w2"].transpose(0, 2, 1).reshape(16, P, P).transpose(1, 0, 2))
    sel = np.zeros((2, P, 16, P), np.float32)
    for i, (f, n) in enumerate(((f1, 9 * f1), (f2, E * f2))):
        for r in range(n):
            for part in range(PARTS):
                sel[i, part * NGATE + r // f, r // P, r % P] = 1.0
    arrays["sel"] = sel.astype(bf)
    arrays["f_w1"] = c(a["L3_ffn_w1"].T)
    arrays["f_w2"] = c(a["L3_ffn_w2"].T.reshape(4, P, P).transpose(1, 0, 2))
    arrays["slopes"] = c(a["L3_attn_slopes"].reshape(H, 1))
    pos = np.arange(T)
    kp = np.stack([pos // 256 * 256, pos % 256]).astype(bf)
    arrays["kpos"] = c(np.broadcast_to(np.tile(kp, (PARTS, 1))[:, None, :], (ALIBI, NG, T)))

    nc = bacc.Bacc("TRN2", target_bir_lowering=False, num_devices=1)
    d = {n: nc.dram_tensor("in_" + n, v.shape, mybir.dt.from_np(v.dtype), kind="ExternalInput").ap() for n, v in arrays.items()}
    d["out"] = nc.dram_tensor("out_x", (NB, T, P), F32, kind="ExternalOutput").ap()
    build(nc, d)
    r = run_bass_kernel_spmd(nc, [{"in_" + n: v for n, v in arrays.items()}], core_ids=[0])
    return r.results[0]["out_x"]
```

```python
from contextlib import ExitStack

import numpy as np

import concourse.bass as bass
from concourse import mybir

F32 = mybir.dt.float32
BF16 = mybir.dt.bfloat16
ALU = mybir.AluOpType
ACT = mybir.ActivationFunctionType
AX_X = mybir.AxisListType.X
AX_XY = mybir.AxisListType.XY

P = 128
NB = 4
T = 512
NT = T // P
H = 16
HD = P // H
GH = 4
NG = H // GH
PARTS = 3
STACK = HD * PARTS * PARTS
ALIBI = 2 * PARTS
ROWS_SHIFT = P - PARTS
VW = 32
E = 8
NGATE = 9
MASKED = -1.0e30
LN_EPS = 1e-5

(L0_MIX, L0_LINEAR, L1_ATTN, L1_MOE, L2_ATTN, L2_GQA, L2_MOE, L3_ATTN, L3_FFN) = range(9)
LAST = L3_FFN
NORMS = {L0_MIX: ("ln",), L0_LINEAR: ("ln",), L1_ATTN: ("ln",), L1_MOE: ("ln",), L2_ATTN: ("ln", "rms"),
         L2_GQA: ("rms",), L2_MOE: ("ln",), L3_ATTN: ("ln", "ln"), L3_FFN: ("ln",)}
NH1 = {L1_MOE: 5, L2_MOE: 4}
SUM_AT, NORM_AT, XT_AT, XT_OUT_AT = 2, 4, 6, 6
NORM_BASE = [sum(NB * len(NORMS[q]) for q in range(p)) for p in range(9)]

LAYERS = [
    dict(phase=L1_ATTN, kv=H, scale=P ** -0.5, causal=False, rope=None, alibi=False),
    dict(phase=L2_ATTN, kv=H, scale=HD ** -0.5, causal=True, rope=0, alibi=False),
    dict(phase=L2_GQA, kv=NG, scale=HD ** -0.5, causal=True, rope=1, alibi=False),
    dict(phase=L3_ATTN, kv=NG, scale=1.0, causal=True, rope=None, alibi=True),
]
PREP_USES = [5 if c["rope"] is not None else 3 for c in LAYERS]
PREP_BASE = [sum(NB * n for n in PREP_USES[:i]) for i in range(4)]
CHAINS = [(0,), (1, 2), (3,)]

_WHOLE = [(t, [j]) for t in range(NT) for j in range(GH)]
_CAUSAL = [(t, [j]) for t in range(2) for j in range(GH)] + [(2, [0, 1]), (2, [2, 3]), (3, [0, 1, 2, 3])]
ST_ITEMS = [_CAUSAL if c["causal"] else _WHOLE for c in LAYERS]
S_ITEMS = [[(NT - 1 - t, js) for t, js in _CAUSAL] if c["causal"] else _WHOLE for c in LAYERS]
NI = [len(x) for x in S_ITEMS]
ITEM_BASE = [sum(NB * NG * n for n in NI[:i]) for i in range(4)]
S_ORDER = [[0, 1, 5] * 5 + [1] if n == 16 else ([0, 1, 5] * 4)[:n] for n in NI]


def s_back(L, i):
    order = S_ORDER[L] + S_ORDER[L][:i]
    return NI[L] + i - max(k for k in range(len(order)) if order[k] == S_ORDER[L][i])


def st_bank(L, g, i):
    return 2 + (g * NI[L] + i) % 2


def kt_end(L, kt):
    return max(i for i, (t, _) in enumerate(ST_ITEMS[L]) if t == kt) + 1


def neighbours(L, b, g):
    chain = next(c for c in CHAINS if L in c)
    at = chain.index(L)
    before = chain[at - 1] if at else None
    after = chain[at + 1] if at + 1 < len(chain) else None
    is_first, is_last = isinstance(b, int) and b == 0, isinstance(b, int) and b == NB - 1
    last_block = None if is_first and before is None else (before, NB - 1) if is_first else (L, b - 1)
    next_block = None if is_last and after is None else (after, 0) if is_last else (L, b + 1)
    prev = (L, b, g - 1) if g else last_block and (*last_block, NG - 1)
    follow = (L, b, g + 1) if g < NG - 1 else next_block and (*next_block, 0)
    ahead = (L, b, g + 2) if g < 2 else next_block and (*next_block, g - 2)
    return prev, follow, ahead, next_block if g == 0 else None, last_block if g < 2 else None


AFTER = {L1_MOE: 1, L2_MOE: 3}
PE_START = {L1_MOE: {7: 0, 8: 1, 9: 2, 10: 3, 11: 4}, L2_MOE: {7: 0, 8: 1, 9: 2}}
DVE_START = {L1_MOE: {7: 0, 8: 1, 9: 2, 10: 3}, L2_MOE: {10: 2}}
ACT_START = {L1_MOE: {10: ["q0"], 11: ["q1"], 12: ["v", "k0", "k1"]}, L2_MOE: {8: ["q"], 9: ["k"], 11: ["q1"], 12: ["k1"]}}
PE_PREP = {True: {0: 0, 1: 1, 3: 2, 4: 3, 6: 4}, False: {0: 0, 2: 1, 4: 2}}
DVE_PREP = {True: {1: 0, 2: 1, 4: 2, 5: 3}, False: {5: 2}}
ACT_PREP = {True: {0: ["xts"], 4: ["q0"], 6: ["q1"], 7: ["v", "k0"], 9: ["k1"]},
            False: {0: ["xts"], 1: ["q"], 3: ["k"], 4: ["q1"], 5: ["v"], 6: ["k1"]}}
CASTS = {True: ["q0", "q1", "k0", "k1"], False: ["q", "k", "q1", "k1"]}
SHIFT_T_AT, O_OUT_AT, O_T_AT, O_NORM_AT, AO_T_AT, AO_OUT_AT = 3, 2, 6, 7, 9, 10
Y_AT, Y_SUM_AT, Y_NORM_AT, Y_NORM2_AT, Y_XT_AT, Y_OUT_AT = 1, 2, 4, 7, 9, 10

MOE_CHUNKS = {L1_MOE: 13, L2_MOE: 16}
MOE_BASE = {L1_MOE: 0, L2_MOE: NB * 13}

W_COLS, _at = {}, 0
for _n, _w in [("l0_k", P), ("l0_v", P), ("l0_r", P), ("l0_o", P), ("l1_out", P),
               ("l2_q", P), ("l2_qs", P), ("l2_k", P), ("l2_ks", P), ("l2_v", P), ("l2_o", P),
               ("g_q", P), ("g_qs", P), ("g_k", 32), ("g_ks", 32), ("g_v", 32), ("g_o", P),
               ("l3_q", P), ("l3_k", 32), ("l3_v", 32), ("l3_o", P), ("l1_gate", E), ("l2_gate", E)]:
    W_COLS[_n] = (_at, _at + _w)
    _at += _w
W_TOTAL = _at
C_COLS, _at = {}, 0
for _n, _w in [("decay", 1), ("first", 1), ("mix", 1), ("ln1_w", 1), ("ln2_w", 1), ("bq", 1), ("bk", 1),
               ("f_ln1_g", 1), ("f_ln1_b", 1), ("f_ln2_g", 4), ("f_ln2_b", 4), ("m_b1", 13), ("m_b3", 13)]:
    C_COLS[_n] = (_at, _at + _w)
    _at += _w
C_TOTAL = _at
R_COLS, _at = {}, 0
for _n, _w in [("logits", E), ("u", E), ("l0_b", E * P), ("gate_b", E), ("b_out", P), ("bv", 32), ("bo", P),
               ("f_b1", T), ("f_b2", P)]:
    R_COLS[_n] = (_at, _at + _w)
    _at += _w
R_TOTAL = _at


def post_index(p, b):
    return b * 2 + p if p <= L0_LINEAR else b + NB * p


def norm_index(p, b):
    return b * 2 + p if p <= L0_LINEAR else b * len(NORMS[p]) + NORM_BASE[p]


def for_blocks(eng, body):
    body(0)
    with eng.Fori(1, NB) as b:
        body(b)


def for_inner_blocks(eng, body):
    body(0)
    with eng.Fori(1, NB - 1) as b:
        body(b)
    body(NB - 1)


def is_first(b):
    return isinstance(b, int) and b == 0


def is_last(b):
    return isinstance(b, int) and b == NB - 1


def back(p, c, m):
    n = MOE_CHUNKS[p]
    return m if c >= m else c + n - max(j for j in range(n) if j % m == c)


def at_least(eng, sem, count):
    if isinstance(count, int) and count <= 0:
        return
    eng.wait_ge(sem, count)


def build(nc, d):
    ctx = ExitStack()
    with ctx:
        def sb(name, shape, dt=F32):
            return ctx.enter_context(nc.sbuf_tensor(name, shape, dt))

        def sem(name):
            return ctx.enter_context(nc.semaphore(name))

        bank = [ctx.enter_context(nc.psum_tensor(f"bank{i}", [P, T], F32)) for i in range(8)]
        X = sb("X", [P, NB * T])
        X1buf = sb("X1", [P, NB * (T + 1)])
        X1 = X1buf[:, 0:NB * T]
        XTP = X1buf[:, :].rearrange("p (b t) -> p b t", b=NB)
        XT = sb("XT", [P, NB * T])
        XTS = sb("XTS", [P, T])
        WC = sb("WC", [P, W_TOTAL])
        CC = sb("CC", [P, C_TOTAL])
        RC = sb("RC", [P, R_TOTAL])
        ident = sb("ident", [P, P])
        identb = sb("identb", [P, P], BF16)
        maskb = sb("maskb", [P, P], BF16)
        WQKV1 = sb("WQKV1", [P, 3, P])
        WSEL = sb("WSEL", [P, P])
        BSEL = sb("BSEL", [P, P])
        tables = sb("tables", [P, 2, 2, T])
        MW1 = sb("MW1", [P, 16 * P])
        MW3 = sb("MW3", [P, 16 * P])
        MW2 = sb("MW2", [P, 16, P])
        MB2 = sb("MB2", [NGATE, P])
        SEL = sb("SEL", [P, 16, P], BF16)
        RWT = sb("RWT", [P, NB * T], BF16)
        RW9 = sb("RW9", [NGATE, NB * T])
        RWB = sb("RWB", [NGATE, T])
        FW1 = sb("FW1", [P, T])
        FW2 = sb("FW2", [P, 4, P])
        QS = sb("QS", [P, H, T], BF16)
        KS = sb("KS", [P, H, T], BF16)
        PQ = sb("PQ", [P, PARTS, T], BF16)
        PK = sb("PK", [P, PARTS, T], BF16)
        QF = sb("QF", [P, T])
        KF = sb("KF", [P, T])
        RA = sb("RA", [P, 2, T])
        SA = sb("RB", [P, 2, T + 1])
        RB = SA[:, :, 0:T]
        W0 = RA[:, :, :].rearrange("p a (n d) -> p (a n) d", d=P)
        VST = sb("VST", [P, NT, P])
        VA = sb("VA", [P, NT, H, VW])
        PT = [sb(f"PT{i}", [P, GH, T]) for i in range(2)]
        M = [sb(f"M{i}", [P, NT * GH]) for i in range(2)]
        MR = sb("MR", [P, NT * GH])
        MS = [sb(f"MS{i}", [P, NT, PARTS, GH], BF16) for i in range(2)]
        MSB = [sb(f"MSB{i}", [PARTS * GH, T], BF16) for i in range(2)]
        OT = sb("OT", [P, T])
        OR = sb("OR", [P, NT * GH])
        AO = sb("AO", [P, NT, P])
        AOT = sb("AOT", [P, T])
        slope = sb("slope", [H, 1])
        slope_r = sb("slope_r", [H, 1])
        slope_p = sb("slope_p", [H, PARTS], BF16)
        slope_w = sb("slope_w", [H, PARTS, T], BF16)
        YB = sb("YB", [P, NT, P])
        N1 = sb("N1", [P, NT, P])
        N2 = sb("N2", [P, NT, P])
        ST = sb("ST", [P, NT, 6])
        MV = sb("MV", [P, NT, 2])
        MS2 = sb("MS2", [P, NT])
        VE = sb("VE", [P, NT])
        RSTD = sb("RSTD", [P, NT])
        neg_half = sb("neg_half", [P, NT])
        bqs = sb("bqs", [P, 1])
        GL = sb("GL", [P, NB * NT, E])
        GE = sb("GE", [P, NB * NT, E])
        GB = sb("GB", [P, NB * NT, E])
        GR = sb("GR", [P, NB * NT, E])
        GO = sb("GO", [P, NB * NT, E])
        GM = sb("GM", [P, NB * NT])
        GW = sb("GW", [P, NB * NT, NGATE])
        GWR = sb("GWR", [P, NB * NT, NGATE])
        GWP = sb("GWP", [P, NB * NT, PARTS, NGATE], BF16)
        rev = sb("rev", [P, E])
        sel0 = sb("sel0", [P, 12, E])
        A1 = [PT[0][:, 0, :], PT[0][:, 1, :]]
        U1 = [PT[0][:, 2, :], PT[0][:, 3, :]]
        S1 = [OT[:, :], AOT[:, :]]
        H1 = [PT[1][:, i, :] for i in range(NT)] + [AO[:, :, :].rearrange("p a b -> p (a b)")]
        XM0, XM, KM, KE = (PT[0][:, i, :] for i in range(4))
        SG, KV, RWKV = (PT[1][:, i, :] for i in range(3))
        cols0 = sb("cols0", [P, 4])
        HG = PT[0]
        HT2 = PT[1]
        FST = sb("FST", [P, NT, 6])
        FMV = sb("FMV", [P, NT, 2])
        FMS, FVE, FRSTD = (sb(n, [P, NT]) for n in ("FMS", "FVE", "FRSTD"))
        qa = sb("qa", [P, 2, 8])
        ones = sb("ones", [P, P])
        qt0 = YB[:, :, :].rearrange("p a b -> p (a b)")

        LD_1 = 16 * (4 + 3 * H + 4)
        ld_c, ld_w0 = sem("load_first"), sem("load_l0_weights")
        ld_x, ld_0, ld_w, ld_1, ld_m1, ld_m2, ld_f = (sem("load_" + n) for n in
                                                      ("x", "l0", "weights", "l1", "moe1", "moe2", "ffn"))
        pool_const = sem("pool_const")
        pool_passed, pe_passed = sem("pool_passed"), sem("pe_passed")
        y_ready, y_added, var_ready, rstd_ready, normed, x_saved, xt_ready, xt_evac, out_done = (sem(n) for n in (
            "pe_y", "dve_y_added", "dve_var", "pool_rstd", "dve_normed", "pool_x_saved", "pe_xt", "act_xt", "dma_out"))
        z_sem, z2_sem, sel_ready, xm0_ready, xm_ready, kvr_ready, km_ready, ke_ready, rwkv_ready, y0_done = (sem(n) for n in (
            "act_z", "dve_z", "dve_sel", "pool_xm0", "dve_xm", "pe_kvr", "dve_km", "act_ke", "dve_rwkv", "pe_l0_done"))
        c0a, c0b, sg_ready = sem("act_cols0"), sem("dve_cols0"), sem("act_sigmoid")
        kv_ready = sem("dve_kv")
        (proj_ready, prep_evac, parts_ready, parts_stored, v_placed, s_ready, max_done, m_split, mt_ready, m_evac,
         st_ready, exp_done, pv_done, o_evac, ot_ready, o_normed, ao_ready, ao_evac, xts_ready, alibi_rows) = (sem(n) for n in (
             "pe_proj", "prep_evac", "pool_parts", "dma_parts", "pool_v", "pe_scores", "dve_max", "dve_shift",
             "pe_shift", "act_shift", "pe_scores_t", "act_exp", "pe_pv", "act_o", "pe_o_t", "dve_o", "pe_ao", "act_ao",
             "pool_xts", "dma_alibi"))
        qm_used = sem("dve_absum_used")
        slope_ready = sem("dve_slope")
        rotated, rest_ready, cast_done = sem("pool_rotated"), sem("pool_rest"), sem("act_cast")
        stack_landed = [sem(f"dma_stack{g}") for g in range(NG)]
        shift_landed = [sem(f"dma_shift{i}") for i in range(2)]
        (lg_ready, gm_ready, ge_ready, gw_ready, gt_ready, gt_evac, rwb_ready, ab_ready, a_evac, u_ready, s1_ready,
         h_ready, yc_done) = (sem(n) for n in (
             "pe_logits", "dve_gmax", "act_gexp", "dve_gates", "pe_gates_t", "act_gates_t", "pool_rwb", "pe_ab", "act_a", "dve_u",
             "act_silu", "dve_h", "pe_chunk"))
        (qs_ready, qm_ready, fu_ready, fb_ready, fg_ready, fv_ready, fr_ready, fn_ready, ft_ready, ft_evac) = (sem(n) for n in (
            "dve_absum", "pe_absum", "pe_up", "dve_up", "act_gelu", "dve_fvar", "pool_frstd", "dve_fnorm", "pe_ft", "act_ft"))

        scr_q = nc.dram_tensor("scr_q", [H * STACK * T], BF16, kind="Internal").ap().tensor
        scr_k = nc.dram_tensor("scr_k", [H * STACK * T], BF16, kind="Internal").ap().tensor

        def wc(name):
            return WC[:, W_COLS[name][0]:W_COLS[name][1]]

        def cc(name, i=0, rows=P):
            return CC[0:rows, C_COLS[name][0] + i:C_COLS[name][0] + i + 1]

        def rc(name):
            return RC[:, R_COLS[name][0]:R_COLS[name][1]]

        def blk(t, b):
            return t[:, b * T:(b + 1) * T] if isinstance(b, int) else t[:, bass.ds(b * T, T)]

        def tiles(ap, n=NT):
            return ap.rearrange("p (a b) -> p a b", a=n)

        Y = bank[6]
        block = ctx.enter_context(nc.Block())

        NEXT_BIAS = {L0_MIX: lambda: BSEL[:, :], L0_LINEAR: lambda: rc("b_out"), L2_MOE: lambda: rc("bo"),
                     L3_ATTN: lambda: rc("f_b2")}

        def attn_weights(L):
            return [(WQKV1[:, 0, :], None, WQKV1[:, 1, :], None, WQKV1[:, 2, :], wc("l1_out")),
                    (wc("l2_q"), wc("l2_qs"), wc("l2_k"), wc("l2_ks"), wc("l2_v"), wc("l2_o")),
                    (wc("g_q"), wc("g_qs"), wc("g_k"), wc("g_ks"), wc("g_v"), wc("g_o")),
                    (wc("l3_q"), None, wc("l3_k"), None, wc("l3_v"), wc("l3_o"))][L]

        def prep_uses(L):
            return ["q", "qs", "k", "ks", "v"] if LAYERS[L]["rope"] is not None else ["q", "k", "v"]

        def U(L, b, g):
            return (b + NB * L) * NG + g

        def half(L, b, g):
            return (b + NB * L) * 2 + g // 2

        def item(L, b, g, i=0):
            return (b * NG + g) * NI[L] + (ITEM_BASE[L] + i)

        def sequence(L, unit, Fori):
            for g in range(NG):
                unit(L, 0, g)
            with Fori(1, NB - 1) as b:
                for g in range(NG):
                    unit(L, b, g)
            for g in range(NG):
                unit(L, NB - 1, g)

        def prep_bank(L, b):
            if isinstance(b, int) and b == 0 and starts_chain(L):
                return bank[5] if L == 0 else bank[7]
            return bank[6]

        def starts_chain(L):
            return any(L == c[0] for c in CHAINS)

        def ends_chain(L):
            return any(L == c[-1] for c in CHAINS)

        def q_from(L, t):
            return t * P if LAYERS[L]["causal"] else 0

        def k_to(L, t):
            return (t + 1) * P if LAYERS[L]["causal"] else T

        def kv_slot(L, g, j):
            return g if LAYERS[L]["kv"] == NG else g * GH + j

        @block.sync
        def _(sp):
            xT = d["xT"].rearrange("c (b t) -> c b t", b=NB)
            sp.dma_start(CC[:, :], d["cols"]).then_inc(ld_c, 16)
            sp.dma_start(XTP[:, 0, 1:T + 1], xT[:, 0, :]).then_inc(ld_c, 16)
            sp.dma_start(WC[:, 0:4 * P], d["wpack"][:, 0:4 * P]).then_inc(ld_w0, 16)
            sp.dma_start(RC[:, :], d["rows"].partition_broadcast(P)).then_inc(ld_0, 16)
            sp.dma_start(XTP[:, 1:NB, 1:T + 1], xT[:, 1:NB, :]).then_inc(ld_x, 16)
            sp.dma_start(W0[:, :, :], d["L0_ffn_W"].rearrange("n d e -> d n e")).then_inc(ld_0, 16)
            sp.dma_start(ident[:, :], d["ident"]).then_inc(ld_x, 16)
            sp.dma_start(tiles(X[:, :], NB * NT), d["L0_attn_x"].rearrange("b (t p) c -> p (b t) c", p=P)).then_inc(ld_x, 16)
            sp.dma_start(WC[:, 4 * P:W_TOTAL], d["wpack"][:, 4 * P:W_TOTAL]).then_inc(ld_w, 16)
            sp.dma_start(QS[STACK:P, :, :], d["qpad"]).then_inc(ld_1, 16)
            sp.dma_start(KS[STACK:P, :, :], d["kpad"]).then_inc(ld_1, 16)
            sp.dma_start(identb[:, :], d["identb"]).then_inc(ld_1, 16)
            sp.dma_start(maskb[:, :], d["maskb"]).then_inc(ld_1, 16)
            sp.wait_ge(pool_const, 1)
            for i, n in enumerate(("l1_wq", "l1_wk", "l1_wv")):
                for h in range(H):
                    sp.dma_start(WQKV1[h * HD:(h + 1) * HD, i, h * HD:(h + 1) * HD], d[n]).then_inc(ld_1, 16)
            for i in range(2):
                for k in range(2):
                    sp.dma_start(tables[:, i, k, :], d["tables"][i, k]).then_inc(ld_1, 16)
            sp.dma_start(SEL[:, :, :], d["sel"][0]).then_inc(ld_m1, 16)
            sp.dma_start(MW1[:, 0:13 * P], d["m1_w1"]).then_inc(ld_m1, 16)
            sp.dma_start(MW3[:, 0:13 * P], d["m1_w3"]).then_inc(ld_m1, 16)
            sp.dma_start(MW2[:, 0:13, :], d["m1_w2"]).then_inc(ld_m1, 16)
            sp.dma_start(MB2[:, :], d["m1_b2"]).then_inc(ld_m1, 16)
            sp.dma_start(FW1[:, :], d["f_w1"]).then_inc(ld_f, 16)
            sp.dma_start(FW2[:, :, :], d["f_w2"]).then_inc(ld_f, 16)
            sp.dma_start(slope[:, :], d["slopes"]).then_inc(ld_f, 16)

            def store_parts(L, b):
                B = b + NB * L
                nk = LAYERS[L]["kv"] * HD
                for g in range(NG):
                    at_least(sp, stack_landed[g], B * 32)
                at_least(sp, parts_ready, B * 2 + 1)
                for j in range(PARTS):
                    sp.dma_start(bass.AP(tensor=scr_q, offset=j * T, ap=[[9 * T, P], [3 * T, 3], [1, T]]),
                                 PQ[:, :, :]).then_inc(parts_stored, 16)
                at_least(sp, parts_ready, B * 2 + 2)
                for i in range(PARTS):
                    sp.dma_start(bass.AP(tensor=scr_k, offset=3 * i * T, ap=[[9 * T, nk], [T, 3], [1, T]]),
                                 PK[0:nk, :, :]).then_inc(parts_stored, 16)
                at_least(sp, parts_stored, (B + 1) * 96)

            def load_stack(L, b, g):
                if not (L == 0 and isinstance(b, int) and b == 0):
                    if isinstance(b, int) and b == 0:
                        sp.wait_ge(st_ready, item(L - 1, NB - 1, g, NI[L - 1]))
                    else:
                        sp.wait_ge(st_ready, item(L, b - 1, g, NI[L]))
                sp.dma_start(QS[0:STACK, g * GH:(g + 1) * GH, :],
                             bass.AP(tensor=scr_q, offset=g * GH * STACK * T, ap=[[T, STACK], [STACK * T, GH], [1, T]])
                             ).then_inc(stack_landed[g], 16)
                n = GH if LAYERS[L]["kv"] == H else 1
                sp.dma_start(KS[0:STACK, g * n:(g + 1) * n, :],
                             bass.AP(tensor=scr_k, offset=g * n * STACK * T, ap=[[T, STACK], [STACK * T, n], [1, T]])
                             ).then_inc(stack_landed[g], 16)

            def load_shift(L, b, g):
                at_least(sp, m_evac, U(L, b, g) + 1)
                for i in range(PARTS):
                    sp.dma_start(QS[ROWS_SHIFT + i:ROWS_SHIFT + i + 1, g * GH:(g + 1) * GH, :],
                                 MSB[g % 2][i * GH:(i + 1) * GH, :]).then_inc(shift_landed[g % 2], 16)

            def attention_sp(L):
                if LAYERS[L]["alibi"]:
                    sp.wait_ge(slope_ready, 1)
                    sp.wait_ge(st_ready, ITEM_BASE[L])
                    for i in range(PARTS):
                        for k in range(2):
                            r = STACK + 2 * i + k
                            sp.dma_start(QS[r:r + 1, :, :], slope_w[:, i, :]).then_inc(alibi_rows, 16)
                    sp.dma_start(KS[STACK:STACK + ALIBI, 0:NG, :], d["kpos"]).then_inc(alibi_rows, 16)
                if starts_chain(L):
                    store_parts(L, 0)
                    for g in range(3):
                        load_stack(L, 0, g)
                    load_shift(L, 0, 0)

                def unit(L, b, g):
                    prev, follow, ahead, prep, end = neighbours(L, b, g)
                    if g == 0:
                        load_stack(L, b, 3)
                    if follow:
                        load_shift(*follow)
                    if prep:
                        store_parts(*prep)
                        load_stack(*prep, 0)
                    elif g >= 2 and ahead:
                        load_stack(ahead[0], ahead[1], g - 1)
                sequence(L, unit, sp.Fori)

            attention_sp(0)
            attention_sp(1)
            sp.wait_ge(xt_evac, 4 * (L1_MOE + 1))
            sp.dma_start(SEL[:, :, :], d["sel"][1]).then_inc(ld_m2, 16)
            sp.dma_start(MW1[:, :], d["m2_w1"]).then_inc(ld_m2, 16)
            sp.dma_start(MW3[:, :], d["m2_w3"]).then_inc(ld_m2, 16)
            sp.dma_start(MW2[:, :, :], d["m2_w2"]).then_inc(ld_m2, 16)
            attention_sp(2)
            attention_sp(3)
            with sp.Fori(0, NB) as b:
                sp.wait_ge(normed, b + 4 * LAST + 1)
                sp.dma_start(d["out"][bass.ds(b, 1)].rearrange("a (t p) c -> p (a t) c", p=P), N1[:, :, :]).then_inc(out_done, 16)
            sp.wait_ge(out_done, 16 * NB)

        @block.gpsimd
        def _(pool):
            g = nc.gpsimd

            def wait(sem, count):
                at_least(pool, sem, count)
                if not isinstance(count, int):
                    pool.sem_inc(pool_passed, 1)
            g.memset(WQKV1[:, :, :], 0.0).then_inc(pool_const, 1)
            g.memset(XTP[:, :, 0:1], 0.0)
            g.memset(SA[:, :, 0:1], 0.0)
            g.memset(neg_half[:, :], -0.5)
            g.iota(rev[:, :], pattern=[[-1, E]], base=E, channel_multiplier=0, allow_small_or_imprecise_dtypes=True)
            g.memset(ones[:, :], 1.0).then_inc(pool_const, 1)

            def shifted(b):
                at_least(pool, xm_ready, b)
                if not isinstance(b, int):
                    pool.sem_inc(pool_passed, 1)
                xs = XTP[:, b, 0:T] if isinstance(b, int) else XTP[:, bass.ds(b, 1), 0:T].rearrange("p a b -> p (a b)")
                g.tensor_tensor(XM0, xs, cols0[:, 0:1].to_broadcast([P, T]), ALU.mult).then_inc(xm0_ready, 1)
            pool.wait_ge(c0b, 1)
            pool.wait_ge(ld_c, 32)
            pool.drain()
            shifted(0)
            g.memset(VA[:, :, :, :], 0.0)
            pool.drain()
            g.memset(VA[:, :, :, HD:HD + 1], 1.0)
            g.memset(RWT[:, :], 0.0).then_inc(pool_const, 1)
            pool.drain()

            def rstd(idx, eps):
                wait(var_ready, idx + 1)
                g.tensor_scalar(VE[:, :], MS2[:, :], eps, 1.0, ALU.add, ALU.mult)
                pool.drain()
                g.tensor_tensor(RSTD[:, :], VE[:, :], neg_half[:, :], ALU.pow).then_inc(rstd_ready, 1)

            def post(p, b):
                pi = post_index(p, b)
                n0 = norm_index(p, b)
                if p == L2_GQA:
                    wait(var_ready, n0 + 1)
                    g.tensor_copy(blk(X1, b), YB[:, :, :].rearrange("p a b -> p (a b)")).then_inc(x_saved, 1)
                    rstd(n0, LN_EPS)
                    return
                rstd(n0, LN_EPS)
                if p == LAST:
                    return
                wait(normed, pi + 1) if len(NORMS[p]) == 1 else wait(var_ready, n0 + 2)
                if p in NEXT_BIAS:
                    if p == L0_MIX:
                        wait(sel_ready, 1)
                    bias = NEXT_BIAS[p]()
                    g.tensor_tensor(tiles(blk(X, b)), N1[:, :, :], bias.rearrange("p (a b) -> p a b", a=1).to_broadcast([P, NT, P]),
                                    ALU.add).then_inc(x_saved, 1)
                else:
                    g.tensor_copy(blk(X, b), N1[:, :, :].rearrange("p a b -> p (a b)")).then_inc(x_saved, 1)
                if len(NORMS[p]) == 2:
                    rstd(n0 + 1, LN_EPS)

            def layer0_pool(b):
                if not is_last(b):
                    if is_first(b):
                        pool.wait_ge(ld_x, 48)
                    shifted(b + 1)
                if not is_first(b):
                    post(L0_MIX, b - 1)
                    post(L0_LINEAR, b - 1)
            for_inner_blocks(pool, layer0_pool)

            def prep_pool(L, b):
                B = b + NB * L
                c = LAYERS[L]
                rope = c["rope"] is not None
                base = b * PREP_USES[L] + PREP_BASE[L]
                nk = c["kv"] * HD
                for i, (f, parts, n) in enumerate(((QF, PQ, P), (KF, PK, nk))):
                    x = "qk"[i]
                    if rope:
                        wait(prep_evac, base + 2 * i + 2)
                        g.tensor_tensor(f[0:n, :], RA[0:n, i, :], RB[0:n, i, :], ALU.add).then_inc(rotated, 1)
                        pool.drain()
                    else:
                        wait(prep_evac, base + i + 1)
                    wait(cast_done, B * 4 + 1 + CASTS[rope].index(x + "0" if rope else x))
                    g.tensor_tensor(RA[0:n, i, :], f[0:n, :], parts[0:n, 0, :], ALU.subtract).then_inc(rest_ready, 1)
                    wait(cast_done, B * 4 + 1 + CASTS[rope].index(x + "1"))
                    pool.drain()
                    g.tensor_tensor(parts[0:n, 2, :], RA[0:n, i, :], parts[0:n, 1, :], ALU.subtract).then_inc(parts_ready, 1)

            def place_v(L, b, gg):
                c = LAYERS[L]
                n = GH if c["kv"] == H else 1
                wait(prep_evac, (b + 1) * PREP_USES[L] + PREP_BASE[L])
                wait(pv_done, (U(L, b, gg) - 3) * NT)
                g.tensor_copy(VA[:, :, gg * n:(gg + 1) * n, 0:HD],
                              VST[:, :, gg * n * HD:(gg + 1) * n * HD].rearrange("p t (h e) -> p t h e", e=HD)
                              ).then_inc(v_placed, 1)

            def shift(L, b, gg):
                m = M[gg % 2][:, :].rearrange("p (t j) -> p t j", j=GH)
                r = MR[:, :].rearrange("p (t j) -> p t j", j=GH)
                to = MS[gg % 2]
                wait(max_done, item(L, b, gg, NI[L]))
                wait(mt_ready, U(L, b, gg) - 1)
                g.tensor_copy(to[:, :, 0, :], m)
                pool.drain()
                g.tensor_tensor(r, m, to[:, :, 0, :], ALU.subtract)
                pool.drain()
                g.tensor_copy(to[:, :, 1, :], r)
                pool.drain()
                g.tensor_tensor(to[:, :, 2, :], r, to[:, :, 1, :], ALU.subtract).then_inc(m_split, 1)

            def start_pool(L):
                prep_pool(L, 0)
                for gg in range(3):
                    place_v(L, 0, gg)

            def attention_pool(L):
                p = LAYERS[L]["phase"]
                if starts_chain(L):
                    shift(L, 0, 0)
                    shift(L, 0, 1)

                def unit(L, b, gg):
                    prev, follow, ahead, prep, end = neighbours(L, b, gg)
                    if gg == 0:
                        place_v(L, b, 3)
                    if prep:
                        prep_pool(*prep)
                    if gg == 1 and end:
                        post(LAYERS[end[0]]["phase"], end[1])
                    if gg == 2 and ahead:
                        place_v(ahead[0], ahead[1], 0)
                        place_v(ahead[0], ahead[1], 1)
                    if gg == 3 and ahead:
                        place_v(ahead[0], ahead[1], 2)
                    if ahead:
                        shift(*ahead)
                sequence(L, unit, pool.Fori)
                if ends_chain(L):
                    post(p, NB - 1)

            def moe_pool(p):
                def body(b):
                    if p == L1_MOE:
                        wait(gt_evac, b * 2 + 2)
                        wait(y_ready, b + NB * p)
                        g.tensor_copy(RWB[:, :], blk(RW9, b)).then_inc(rwb_ready, 1)
                    if not is_first(b):
                        post(p, b - 1)
                for_blocks(pool, body)
                start_pool(AFTER[p])
                post(p, NB - 1)

            start_pool(0)
            post(L0_MIX, NB - 1)
            post(L0_LINEAR, NB - 1)
            attention_pool(0)
            moe_pool(L1_MOE)
            attention_pool(1)
            attention_pool(2)
            moe_pool(L2_MOE)
            attention_pool(3)

            def ffn_pool(b):
                if not is_first(b):
                    post(LAST, b - 1)
                wait(fv_ready, b + 1)
                g.tensor_scalar(FVE[:, :], FMS[:, :], LN_EPS, 1.0, ALU.add, ALU.mult)
                pool.drain()
                g.tensor_tensor(FRSTD[:, :], FVE[:, :], neg_half[:, :], ALU.pow).then_inc(fr_ready, 1)
            for_blocks(pool, ffn_pool)
            post(LAST, NB - 1)

        @block.scalar
        def _(act):
            a = nc.scalar

            def xt_out(p, b):
                act.wait_ge(xt_ready, post_index(p, b) + 1)
                dst = XTS[:, :] if p == L0_MIX else blk(XT, b)
                src = (bank[6] if p in (L1_ATTN, L2_ATTN, L2_GQA, L3_ATTN) else bank[7])[:, :]
                if p == L2_ATTN:
                    i = a.activation(dst, src, ACT.Copy, scale=cc("ln1_w"))
                elif p == L2_GQA:
                    i = a.activation(dst, src, ACT.Copy, scale=cc("ln2_w"))
                elif p == L3_ATTN:
                    i = a.activation(dst, src, ACT.Identity, scale=cc("f_ln1_g"), bias=cc("f_ln1_b"))
                else:
                    i = a.activation(dst, src, ACT.Copy)
                i.then_inc(xt_evac, 1)

            act.wait_ge(ld_c, 32)
            a.activation(cols0[:, 1:2], cc("decay"), ACT.Exp)
            act.drain()
            a.activation(cols0[:, 2:3], cols0[:, 1:2], ACT.Exp, scale=-1.0)
            a.activation(cols0[:, 3:4], cc("first"), ACT.Exp).then_inc(c0a, 1)
            act.wait_ge(z2_sem, 1)
            a.activation(sel0[:, 3, :], sel0[:, 2, :], ACT.Exp, accum_out=sel0[:, 4, 0:1])
            act.drain()
            a.activation(sel0[:, 4, 1:2], sel0[:, 4, 0:1], ACT.Ln).then_inc(z_sem, 1)
            a.activation(sel0[:, 0, :], rc("u"), ACT.Ln)
            act.drain()
            a.activation(sel0[:, 1, :], sel0[:, 0, :], ACT.Ln, scale=-1.0).then_inc(z_sem, 1)

            def layer0_act(b):
                act.wait_ge(km_ready, b + 1)
                a.activation(KE, KM, ACT.Exp).then_inc(ke_ready, 1)
                at_least(act, rwkv_ready, b)
                a.activation(SG, bank[2][:, :], ACT.Sigmoid).then_inc(sg_ready, 1)
                if not is_first(b):
                    xt_out(L0_MIX, b - 1)
                    xt_out(L0_LINEAR, b - 1)
            for_blocks(act, layer0_act)

            def prep_act(L, b, what):
                c = LAYERS[L]
                B = b + NB * L
                base = b * PREP_USES[L] + PREP_BASE[L]
                nk = c["kv"] * HD
                rope = c["rope"] is not None
                i = 0 if what[0] == "q" else 1
                f, parts, n = ((QF, PQ, P), (KF, PK, nk))[i]
                if what == "xts" and isinstance(b, int):
                    return
                if what == "xts":
                    act.wait_ge(xt_evac, post_index(c["phase"] - 1, b) + 1)
                    at_least(act, proj_ready, base)
                    a.activation(XTS[:, :], blk(XT, b), ACT.Copy).then_inc(xts_ready, 1)
                elif what == "v":
                    if c["alibi"]:
                        return
                    act.wait_ge(proj_ready, base + PREP_USES[L])
                    at_least(act, v_placed, B * NG)
                    a.activation(VST[:, :, 0:nk], tiles(prep_bank(L, b)[:, :])[:, :, 0:nk], ACT.Copy).then_inc(prep_evac, 1)
                elif what in ("q", "k"):
                    act.wait_ge(proj_ready, base + i + 1)
                    at_least(act, parts_ready, B * 2 - 1 + i)
                    at_least(act, parts_stored, B * 96)
                    if c["alibi"]:
                        k = dict(func=ACT.Identity, scale=HD ** -0.5 if i == 0 else 1.0, bias=bqs[:, :] if i == 0 else cc("bk", rows=n))
                    else:
                        k = dict(func=ACT.Copy)
                    a.activation(parts[0:n, 0, :], prep_bank(L, b)[0:n, :], **k).then_inc(cast_done, 1)
                    a.activation(f[0:n, :], prep_bank(L, b)[0:n, :], **k).then_inc(prep_evac, 1)
                elif what[1] == "0":
                    act.wait_ge(rotated, b * 2 + (NB * 2 * (L - 1) + i + 1))
                    at_least(act, parts_stored, B * 96)
                    a.activation(parts[0:n, 0, :], f[0:n, :], ACT.Copy).then_inc(cast_done, 1)
                else:
                    act.wait_ge(rest_ready, B * 2 + i + 1)
                    a.activation(parts[0:n, 1, :], RA[0:n, i, :], ACT.Copy).then_inc(cast_done, 1)

            def m_out(L, b, g):
                w = U(L, b, g)
                act.wait_ge(mt_ready, w + 1)
                at_least(act, shift_landed[g % 2], half(L, b, g) * 48)
                a.activation(MSB[g % 2][:, :], bank[7][0:PARTS * GH, 0:T // 2].bitcast(BF16), ACT.Copy).then_inc(m_evac, 1)

            def o_out(L, u, g):
                act.wait_ge(pv_done, (u + 1) * NT)
                a.activation(OT[:, :], bank[4][:, :], ACT.Copy).then_inc(o_evac, 1)

            def ao_out(L, b):
                B = b + NB * L
                act.wait_ge(ao_ready, B + 1)
                at_least(act, y_ready, b + NB * LAYERS[L]["phase"])
                a.activation(AOT[:, :], bank[6][:, :], ACT.Copy).then_inc(ao_evac, 1)

            def attention_act(L):
                c = LAYERS[L]
                p = c["phase"]
                places = ACT_PREP
                if starts_chain(L):
                    m_out(L, 0, 0)

                def unit(L, b, g):
                    u = U(L, b, g)
                    prev, follow, ahead, prep, end = neighbours(L, b, g)
                    for i, (kt, js) in enumerate(ST_ITEMS[L]):
                        q0 = q_from(L, kt)
                        w = T - q0
                        act.wait_ge(st_ready, item(L, b, g, i) + 1)
                        at_least(act, pv_done, u * NT + kt - 1)
                        a.activation(PT[kt % 2][:, js[0]:js[-1] + 1, q0:T],
                                     tiles(bank[st_bank(L, g, i)][:, 0:w * len(js)], len(js)), ACT.Exp,
                                     scale=c["scale"]).then_inc(exp_done, 1)
                        if prep:
                            for what in places[LAYERS[prep[0]]["rope"] is not None].get(i, ()):
                                prep_act(*prep, what)
                        if prev and i == O_OUT_AT:
                            o_out(L, u - 1, g - 1)
                        if follow and i == SHIFT_T_AT + 1:
                            m_out(*follow)
                        if end and g == 0 and i == AO_OUT_AT:
                            ao_out(*end)
                        if end and g == 1 and i == Y_OUT_AT:
                            xt_out(LAYERS[end[0]]["phase"], end[1])
                sequence(L, unit, act.Fori)
                if ends_chain(L):
                    o_out(L, U(L, NB - 1, NG - 1), NG - 1)
                    ao_out(L, NB - 1)
                    xt_out(p, NB - 1)

            def moe_act(p):
                act.wait_ge(gm_ready, 1 if p == L1_MOE else 2)
                a.activation(GE[:, :, :], GL[:, :, :], ACT.Exp).then_inc(ge_ready, 1)
                gi = 0 if p == L1_MOE else 1
                for b in range(NB):
                    act.wait_ge(gt_ready, (gi * NB + b) * 2 + 1)
                    a.activation(blk(RW9, b), bank[6][0:NGATE, :], ACT.Copy).then_inc(gt_evac, 1)
                    act.wait_ge(gt_ready, (gi * NB + b) * 2 + 2)
                    a.activation(blk(RWT, b)[0:PARTS * NGATE, :], bank[7][0:PARTS * NGATE, 0:T // 2].bitcast(BF16), ACT.Copy).then_inc(gt_evac, 1)
                n = MOE_CHUNKS[p]

                def body(b):
                    k0 = b * n + MOE_BASE[p]
                    for c in range(n):
                        act.wait_ge(ab_ready, k0 + c + 1)
                        at_least(act, u_ready, k0 + c + 1 - back(p, c, 2))
                        if p == L1_MOE:
                            a.activation(A1[c % 2], bank[c % 2][:, :], ACT.Identity, bias=cc("m_b1", c)).then_inc(a_evac, 1)
                            act.wait_ge(u_ready, k0 + c + 1)
                            at_least(act, h_ready, k0 + c + 1 - back(p, c, 2))
                            a.activation(S1[c % 2], U1[c % 2], ACT.Silu).then_inc(s1_ready, 1)
                        else:
                            a.activation(A1[c % 2], bank[c % 2][:, :], ACT.Silu).then_inc(a_evac, 1)
                        if c == XT_OUT_AT and not is_first(b):
                            xt_out(p, b - 1)
                        if is_last(b):
                            for what in ACT_START[p].get(c, ()):
                                prep_act(AFTER[p], 0, what)
                for_inner_blocks(act, body)
                xt_out(p, NB - 1)

            for what in ("q", "k", "v", "q1", "k1"):
                prep_act(0, 0, what)
            xt_out(L0_MIX, NB - 1)
            xt_out(L0_LINEAR, NB - 1)
            attention_act(0)
            moe_act(L1_MOE)
            attention_act(1)
            attention_act(2)
            moe_act(L2_MOE)
            attention_act(3)

            def ffn_out(b):
                for c in range(4):
                    act.wait_ge(ft_ready, b * 4 + c + 1)
                    if c == 0:
                        at_least(act, y_ready, b + NB * LAST)
                    a.activation(HT2[:, c, :], bank[4 + c % 2][:, :], ACT.Identity, scale=cc("f_ln2_g", c), bias=cc("f_ln2_b", c)).then_inc(ft_evac, 1)

            def ffn_act(b):
                act.wait_ge(xt_evac, b + NB * LAST - NB + 1)
                at_least(act, fu_ready, b * NT)
                a.activation(XTS[:, :], blk(XT, b), ACT.Copy).then_inc(xts_ready, 1)
                if not is_first(b):
                    ffn_out(b - 1)
                for i in range(NT):
                    act.wait_ge(fb_ready, b * NT + i + 1)
                    a.activation(HG[:, i, :], HG[:, i, :], ACT.Gelu).then_inc(fg_ready, 1)
            for_blocks(act, ffn_act)
            ffn_out(NB - 1)

        @block.vector
        def _(dve):
            v = nc.vector

            def stats(src):
                for i in range(NT):
                    v.bn_stats(ST[:, i, :], src[:, i, :])
                dve.drain()
                for i in range(NT):
                    v.bn_aggr(MV[:, i, :], ST[:, i, :])
                dve.drain()

            def norm(kind, src, dst, idx, first):
                stats(src)
                if kind == "ln":
                    v.tensor_copy(MS2[:, :], MV[:, :, 1]).then_inc(var_ready, 1)
                else:
                    v.tensor_tensor(MS2[:, :], MV[:, :, 0], MV[:, :, 0], ALU.mult)
                    dve.drain()
                    v.tensor_tensor(MS2[:, :], MS2[:, :], MV[:, :, 1], ALU.add).then_inc(var_ready, 1)

            def scale(kind, src, dst, idx):
                dve.wait_ge(rstd_ready, idx + 1)
                for i in range(NT):
                    if kind == "ln":
                        r = v.tensor_scalar(dst[:, i, :], src[:, i, :], MV[:, i, 0:1], RSTD[:, i:i + 1], ALU.subtract, ALU.mult)
                    else:
                        r = v.tensor_scalar(dst[:, i, :], src[:, i, :], RSTD[:, i:i + 1], None, ALU.mult)
                return r

            def post_sum(p, b):
                pi = post_index(p, b)
                dve.wait_ge(y_ready, pi + 1)
                before = NB * LAST if p == LAST else pi
                if p != L0_MIX or isinstance(b, int):
                    at_least(dve, x_saved, before)
                    at_least(dve, xt_ready, before)
                if p == LAST:
                    at_least(dve, out_done, b * 16)
                if p == L2_MOE:
                    v.tensor_tensor(YB[:, :, :], tiles(Y[:, :]), tiles(blk(X1, b)), ALU.add).then_inc(y_added, 1)
                    dve.drain()
                    v.tensor_tensor(YB[:, :, :], YB[:, :, :], tiles(blk(X, b)), ALU.add)
                else:
                    v.tensor_tensor(YB[:, :, :], tiles(Y[:, :]), tiles(blk(X, b)), ALU.add).then_inc(y_added, 1)
                dve.drain()
                norm(NORMS[p][0], YB, N1, 0, True)

            def post_norm(p, b):
                n0 = norm_index(p, b)
                if len(NORMS[p]) == 1:
                    scale(NORMS[p][0], YB, N2 if p == L2_GQA else N1, n0).then_inc(normed, 1)
                    return
                scale(NORMS[p][0], YB, N1, n0)
                dve.drain()
                norm(NORMS[p][1], N1, N2, 1, False)

            def post_norm2(p, b):
                if len(NORMS[p]) == 2:
                    scale(NORMS[p][1], N1, N2, norm_index(p, b) + 1).then_inc(normed, 1)

            def mixed(b):
                xb = XTP[:, b, 1:T + 1] if isinstance(b, int) else XTP[:, bass.ds(b, 1), 1:T + 1].rearrange("p a b -> p (a b)")
                dve.wait_ge(xm0_ready, b + 1)
                v.scalar_tensor_tensor(XM, xb, cc("mix"), XM0, ALU.mult, ALU.add).then_inc(xm_ready, 1)

            dve.wait_ge(ld_c, 32)
            v.tensor_scalar(cols0[:, 0:1], cc("mix"), -1.0, 1.0, ALU.mult, ALU.add).then_inc(c0b, 1)
            dve.drain().then_inc(o_normed, 1)
            mixed(0)
            dve.wait_ge(ld_0, 32)
            v.tensor_reduce(sel0[:, 4, 2:3], rc("logits"), AX_X, ALU.max)
            dve.drain()
            v.tensor_scalar(sel0[:, 2, :], rc("logits"), sel0[:, 4, 2:3], None, ALU.subtract).then_inc(z2_sem, 1)

            def pick():
                dve.wait_ge(z_sem, 2)
                v.tensor_scalar(sel0[:, 5, :], sel0[:, 2, :], sel0[:, 4, 1:2], None, ALU.subtract)
                dve.drain()
                v.tensor_tensor(sel0[:, 6, :], sel0[:, 5, :], sel0[:, 1, :], ALU.subtract)
                dve.drain()
                v.tensor_reduce(sel0[:, 4, 3:4], sel0[:, 6, :], AX_X, ALU.max)
                dve.drain()
                dve.wait_ge(pool_const, 2)
                v.scalar_tensor_tensor(sel0[:, 7, :], sel0[:, 6, :], sel0[:, 4, 3:4], rev[:, :], ALU.is_ge, ALU.mult)
                dve.drain()
                v.tensor_reduce(sel0[:, 4, 4:5], sel0[:, 7, :], AX_X, ALU.max)
                dve.drain()
                v.tensor_scalar(sel0[:, 8, :], sel0[:, 7, :], sel0[:, 4, 4:5], None, ALU.is_equal)
                dve.drain()
                for i in range(E):
                    b0 = rc("l0_b")[:, i * P:(i + 1) * P]
                    if i == 0:
                        v.tensor_scalar(WSEL[:, :], W0[:, 0, :], sel0[:, 8, 0:1], None, ALU.mult)
                        r = v.tensor_scalar(BSEL[:, :], b0, sel0[:, 8, 0:1], None, ALU.mult)
                    else:
                        v.scalar_tensor_tensor(WSEL[:, :], W0[:, i, :], sel0[:, 8, i:i + 1], WSEL[:, :], ALU.mult, ALU.add)
                        r = v.scalar_tensor_tensor(BSEL[:, :], b0, sel0[:, 8, i:i + 1], BSEL[:, :], ALU.mult, ALU.add)
                    if i == E - 1:
                        r.then_inc(sel_ready, 1)
                    dve.drain()

            def layer0_dve(b):
                dve.wait_ge(kvr_ready, b + 1)
                v.tensor_scalar(KM, bank[0][:, :], 60.0, None, ALU.min).then_inc(km_ready, 1)
                if not is_last(b):
                    mixed(b + 1)
                if is_first(b):
                    dve.wait_ge(c0a, 1)
                    dve.wait_ge(ld_x, 48)
                else:
                    post_sum(L0_MIX, b - 1)
                dve.wait_ge(ke_ready, b + 1)
                v.tensor_tensor(KV, KE, bank[1][:, :], ALU.mult).then_inc(kv_ready, 1)
                dve.drain()
                for i, src in enumerate((KV, KE)):
                    v.tensor_tensor_scan(SA[:, i, 1:T + 1], cols0[:, 2:3].to_broadcast([P, T]), src, 0.0, ALU.mult, ALU.add)
                dve.drain()
                if not is_first(b):
                    post_norm(L0_MIX, b - 1)
                v.scalar_tensor_tensor(KV, KV, cols0[:, 3:4], SA[:, 0, 0:T], ALU.mult, ALU.add)
                v.scalar_tensor_tensor(KE, KE, cols0[:, 3:4], SA[:, 1, 0:T], ALU.mult, ALU.add)
                dve.drain()
                v.tensor_scalar(KE, KE, 1e-9, None, ALU.add)
                dve.drain()
                v.reciprocal(KE, KE)
                dve.wait_ge(sg_ready, b + 1)
                v.tensor_tensor(KV, KV, SG, ALU.mult)
                dve.drain()
                v.tensor_tensor(RWKV, KV, KE, ALU.mult).then_inc(rwkv_ready, 1)
                if is_first(b):
                    pick()
                else:
                    post_sum(L0_LINEAR, b - 1)
                    post_norm(L0_LINEAR, b - 1)
            for_inner_blocks(dve, layer0_dve)
            post_sum(L0_MIX, NB - 1)
            post_norm(L0_MIX, NB - 1)
            post_sum(L0_LINEAR, NB - 1)
            post_norm(L0_LINEAR, NB - 1)

            def prep_dve(L, b, i):
                c = LAYERS[L]
                B = b + NB * L
                base = b * PREP_USES[L] + PREP_BASE[L]
                what = prep_uses(L)[i]
                nk = c["kv"] * HD
                if what == "v":
                    if c["alibi"]:
                        dve.wait_ge(proj_ready, base + i + 1)
                        at_least(dve, v_placed, B * NG)
                        v.tensor_tensor(VST[:, :, 0:nk], tiles(prep_bank(L, b)[:, :])[:, :, 0:nk],
                                        rc("bv").rearrange("p (a b) -> p a b", a=1).to_broadcast([P, NT, nk]), ALU.add).then_inc(prep_evac, 1)
                elif c["rope"] is not None:
                    n, k = (P, 0) if what[0] == "q" else (nk, 1)
                    sw = len(what) == 2
                    dve.wait_ge(proj_ready, base + i + 1)
                    at_least(dve, parts_ready, B * 2 - 1 + k)
                    v.tensor_tensor((RB if sw else RA)[0:n, k, :], prep_bank(L, b)[0:n, :], tables[0:n, c["rope"], int(sw), :],
                                    ALU.mult).then_inc(prep_evac, 1)

            def reduce(L, b, g, i):
                t, js = S_ITEMS[L][i]
                kl = k_to(L, t)
                dve.wait_ge(s_ready, item(L, b, g, i) + 1)
                if i == 0:
                    at_least(dve, m_split, U(L, b, g) - 1)
                v.tensor_reduce(M[g % 2][:, t * GH + js[0]:t * GH + js[-1] + 1], tiles(bank[S_ORDER[L][i]][:, 0:kl * len(js)], len(js)),
                                AX_X, ALU.max, negate=True).then_inc(max_done, 1)

            def o_norm(L, b, g, u):
                dve.wait_ge(ot_ready, u + 1)
                o = bank[7][:, :].rearrange("p (t j e) -> p t j e", t=NT, j=GH)
                r = OR[:, :].rearrange("p (t j e) -> p t j e", t=NT, j=GH)
                v.reciprocal(r, o[:, :, :, HD:HD + 1])
                dve.drain()
                v.tensor_tensor(AO[:, :, g * 32:(g + 1) * 32].rearrange("p t (j e) -> p t j e", j=GH), o[:, :, :, 0:HD],
                                r.to_broadcast([P, NT, GH, HD]), ALU.mult).then_inc(o_normed, 1)

            def attention_dve(L):
                c = LAYERS[L]
                p = c["phase"]
                if starts_chain(L):
                    for g in range(2):
                        for i in range(NI[L]):
                            reduce(L, 0, g, i)

                def unit(L, b, g):
                    u = U(L, b, g)
                    prev, follow, ahead, prep, end = neighbours(L, b, g)
                    for i in range(NI[L]):
                        if ahead and i < NI[ahead[0]]:
                            reduce(*ahead, i)
                        if prep:
                            at = DVE_PREP[LAYERS[prep[0]]["rope"] is not None]
                            if i in at:
                                prep_dve(*prep, at[i])
                        if prev and i == O_NORM_AT:
                            o_norm(*prev, u - 1)
                        if end and g == 1 and i == Y_SUM_AT:
                            post_sum(LAYERS[end[0]]["phase"], end[1])
                        if end and g == 1 and i == Y_NORM_AT:
                            post_norm(LAYERS[end[0]]["phase"], end[1])
                        if end and g == 1 and i == Y_NORM2_AT:
                            post_norm2(LAYERS[end[0]]["phase"], end[1])
                sequence(L, unit, dve.Fori)
                if ends_chain(L):
                    o_norm(L, NB - 1, NG - 1, U(L, NB - 1, NG - 1))
                    post_sum(p, NB - 1)
                    post_norm(p, NB - 1)
                    post_norm2(p, NB - 1)

            def top(src, onehot, tmp, keep):
                bc = lambda t: t.rearrange("p (a b) -> p a b", b=1).to_broadcast([P, NB * NT, E])
                v.tensor_reduce(GM[:, :], src, AX_X, ALU.max)
                dve.drain()
                v.tensor_tensor(tmp, src, bc(GM[:, :]), ALU.is_ge)
                dve.drain()
                v.tensor_tensor(tmp, tmp, rev[:, :].rearrange("p (a b) -> p a b", a=1).to_broadcast([P, NB * NT, E]), ALU.mult)
                dve.drain()
                v.tensor_reduce(GM[:, :], tmp, AX_X, ALU.max)
                dve.drain()
                v.tensor_tensor(onehot, tmp, bc(GM[:, :]), ALU.is_equal)
                dve.drain()

            def gates(p):
                gi = 0 if p == L1_MOE else 1
                bc = lambda t: t.rearrange("p (a b) -> p a b", b=1).to_broadcast([P, NB * NT, E])
                dve.wait_ge(lg_ready, gi + 1)
                lg = bank[5][:, 0:NB * NT * E].rearrange("p (a b) -> p a b", b=E)
                v.tensor_reduce(GM[:, :], lg, AX_X, ALU.max)
                dve.drain()
                v.tensor_tensor(GL[:, :, :], lg, bc(GM[:, :]), ALU.subtract).then_inc(gm_ready, 1)
                dve.wait_ge(ge_ready, gi + 1)
                v.tensor_reduce(GM[:, :], GE[:, :, :], AX_X, ALU.add)
                dve.drain()
                v.reciprocal(GM[:, :], GM[:, :])
                dve.drain()
                v.tensor_tensor(GE[:, :, :], GE[:, :, :], bc(GM[:, :]), ALU.mult)
                dve.drain()
                if p == L1_MOE:
                    v.tensor_tensor(GB[:, :, :], GE[:, :, :], rc("gate_b").rearrange("p (a b) -> p a b", a=1).to_broadcast([P, NB * NT, E]), ALU.add)
                else:
                    v.tensor_copy(GB[:, :, :], GE[:, :, :])
                dve.drain()
                top(GB[:, :, :], GO[:, :, :], GR[:, :, :], True)
                v.scalar_tensor_tensor(GB[:, :, :], GO[:, :, :], MASKED, GB[:, :, :], ALU.mult, ALU.add)
                dve.drain()
                top(GB[:, :, :], GL[:, :, :], GR[:, :, :], False)
                v.tensor_tensor(GO[:, :, :], GO[:, :, :], GL[:, :, :], ALU.add)
                dve.drain()
                w = GW[:, :, 0:E]
                v.memset(GW[:, :, E:NGATE], 1.0 if p == L1_MOE else 0.0)
                v.tensor_tensor(w, GE[:, :, :], GO[:, :, :], ALU.mult)
                dve.drain()
                if p == L2_MOE:
                    v.tensor_reduce(GM[:, :], w, AX_X, ALU.add)
                    dve.drain()
                    v.reciprocal(GM[:, :], GM[:, :])
                    dve.drain()
                    v.tensor_tensor(w, w, bc(GM[:, :]), ALU.mult)
                    dve.drain()
                v.tensor_copy(GWP[:, :, 0, :], GW[:, :, :])
                dve.drain()
                v.tensor_tensor(GWR[:, :, :], GW[:, :, :], GWP[:, :, 0, :], ALU.subtract)
                dve.drain()
                v.tensor_copy(GWP[:, :, 1, :], GWR[:, :, :])
                dve.drain()
                v.tensor_tensor(GWP[:, :, 2, :], GWR[:, :, :], GWP[:, :, 1, :], ALU.subtract).then_inc(gw_ready, 1)

            def moe_dve(p):
                gates(p)
                n = MOE_CHUNKS[p]

                def body(b):
                    k0 = b * n + MOE_BASE[p]
                    first = isinstance(b, int) and b == 0
                    for c in range(n):
                        dve.wait_ge(a_evac, k0 + c + 1)
                        if p == L1_MOE:
                            at_least(dve, s1_ready, b * n + c + 1 - back(p, c, 2))
                            v.scalar_tensor_tensor(U1[c % 2], bank[2 + c % 2][:, :], cc("m_b3", c), A1[c % 2], ALU.add, ALU.mult).then_inc(u_ready, 1)
                            dve.wait_ge(s1_ready, b * n + c + 1)
                        else:
                            v.tensor_tensor(U1[c % 2], bank[2 + c % 2][:, :], A1[c % 2], ALU.mult).then_inc(u_ready, 1)
                            dve.drain()
                        at_least(dve, yc_done, k0 + c + 1 - back(p, c, NH1[p]))
                        v.tensor_tensor(H1[c % NH1[p]], bank[4 + c % 2][:, :], (S1 if p == L1_MOE else U1)[c % 2],
                                        ALU.mult).then_inc(h_ready, 1)
                        if c == SUM_AT and not first:
                            post_sum(p, b - 1)
                        if c == NORM_AT and not first:
                            post_norm(p, b - 1)
                        if is_last(b) and c in DVE_START[p]:
                            prep_dve(AFTER[p], 0, DVE_START[p][c])
                for_inner_blocks(dve, body)
                post_sum(p, NB - 1)
                post_norm(p, NB - 1)

            def ternary():
                dve.wait_ge(ld_f, 48)
                w2 = FW2[:, :, :].rearrange("p a b -> p (a b)")
                v.tensor_reduce(qa[:, 0, 0:1], FW1[:, :], AX_X, ALU.add, apply_absolute_value=True)
                v.tensor_reduce(qa[:, 0, 1:2], w2, AX_X, ALU.add, apply_absolute_value=True).then_inc(qs_ready, 1)
                dve.wait_ge(qm_ready, 1)
                v.tensor_scalar(qa[:, 0, 2:4], bank[5][:, 0:2], 1.0 / (T * P), 1e-5, ALU.mult, ALU.max).then_inc(qm_used, 1)
                dve.drain()
                v.reciprocal(qa[:, 0, 4:6], qa[:, 0, 2:4])
                dve.drain()
                v.reciprocal(qa[:, 0, 6:8], qa[:, 0, 4:6])
                dve.drain()
                for i, w in enumerate((FW1[:, :], w2)):
                    v.tensor_scalar(qt0[:, :], w, qa[:, 0, 4 + i:5 + i], 12582912.0, ALU.mult, ALU.add)
                    dve.drain()
                    v.tensor_scalar(qt0[:, :], qt0[:, :], 12582912.0, 1.0, ALU.subtract, ALU.min)
                    dve.drain()
                    v.tensor_scalar(qt0[:, :], qt0[:, :], -1.0, qa[:, 0, 6 + i:7 + i], ALU.max, ALU.mult)
                    dve.drain()
                    v.tensor_tensor(qt0[:, :], qt0[:, :], w, ALU.subtract)
                    dve.drain()
                    v.tensor_tensor(w, w, qt0[:, :], ALU.add)
                    dve.drain()
                v.tensor_scalar(bqs[:, :], cc("bq"), HD ** -0.5, None, ALU.mult)
                v.tensor_copy(slope_p[:, 0:1], slope[:, :])
                dve.drain()
                v.tensor_tensor(slope_r[:, :], slope[:, :], slope_p[:, 0:1], ALU.subtract)
                dve.drain()
                v.tensor_copy(slope_p[:, 1:2], slope_r[:, :])
                dve.drain()
                v.tensor_tensor(slope_p[:, 2:3], slope_r[:, :], slope_p[:, 1:2], ALU.subtract)
                dve.drain()
                v.tensor_copy(slope_w[:, :, :], slope_p[:, :].rearrange("p (a b) -> p a b", b=1).to_broadcast([H, PARTS, T])).then_inc(slope_ready, 1)

            attention_dve(0)
            moe_dve(L1_MOE)
            ternary()
            attention_dve(1)
            attention_dve(2)
            moe_dve(L2_MOE)
            attention_dve(3)

            def ffn_dve(b):
                for i in range(NT):
                    dve.wait_ge(fu_ready, b * NT + i + 1)
                    if i == 0:
                        at_least(dve, ft_ready, b * 4)
                    v.tensor_tensor(HG[:, i, :], bank[i][:, :], rc("f_b1"), ALU.add).then_inc(fb_ready, 1)
                if not is_first(b):
                    post_sum(LAST, b - 1)
                for i in range(NT):
                    dve.wait_ge(fg_ready, b * NT + i + 1)
                    v.bn_stats(FST[:, i, :], HG[:, i, :])
                dve.drain()
                for i in range(NT):
                    v.bn_aggr(FMV[:, i, :], FST[:, i, :])
                dve.drain()
                v.tensor_copy(FMS[:, :], FMV[:, :, 1]).then_inc(fv_ready, 1)
                if not is_first(b):
                    post_norm(LAST, b - 1)
                dve.wait_ge(fr_ready, b + 1)
                for i in range(NT):
                    r = v.tensor_scalar(HG[:, i, :], HG[:, i, :], FMV[:, i, 0:1], FRSTD[:, i:i + 1], ALU.subtract, ALU.mult)
                r.then_inc(fn_ready, 1)
            ffn_dve(0)
            ffn_dve(1)
            with dve.Fori(2, NB) as b:
                ffn_dve(b)
            post_sum(LAST, NB - 1)
            post_norm(LAST, NB - 1)

        @block.tensor
        def _(pe):
            mm = nc.tensor.matmul
            tr = nc.tensor.transpose

            def xt(p, b, to):
                src = N2 if p in (L2_ATTN, L2_GQA, L3_ATTN) else N1
                pe.wait_ge(normed, post_index(p, b) + 1)
                if p == L0_MIX and not isinstance(b, int):
                    pe.wait_ge(ke_ready, b + 2)
                else:
                    at_least(pe, xt_evac, post_index(p, b))
                for i in range(NT):
                    r = tr(to[:, i * P:(i + 1) * P], src[:, i, :], ident[:, :])
                r.then_inc(xt_ready, 1)

            def y_out(lhs, w, b, p):
                for i in range(NT):
                    r = mm(Y[:, i * P:(i + 1) * P], lhs[:, i * P:(i + 1) * P], w, start=True, stop=True)
                r.then_inc(y_ready, 1)

            pe.wait_ge(ld_w0, 16)
            pe.wait_ge(ld_c, 32)

            def kvr(b):
                pe.wait_ge(xm_ready, b + 1)
                at_least(pe, kv_ready, b)
                at_least(pe, sg_ready, b)
                for i, n in enumerate(("l0_k", "l0_v", "l0_r")):
                    r = mm(bank[i][:, :], wc(n), XM, start=True, stop=True)
                r.then_inc(kvr_ready, 1)

            def mix_end(b):
                pe.wait_ge(rwkv_ready, b + 1)
                y_out(RWKV, wc("l0_o"), b, L0_MIX)
                xt(L0_MIX, b, bank[7])

            def linear(b):
                pe.wait_ge(xt_evac, b * 2 + 1)
                pe.wait_ge(sel_ready, 1)
                y_out(XTS, WSEL[:, :], b, L0_LINEAR)
                xt(L0_LINEAR, b, bank[7])

            def layer0_pe(b):
                if not is_first(b):
                    mix_end(b - 1)
                if not is_last(b):
                    kvr(b + 1)
                if not is_first(b):
                    linear(b - 1)
            kvr(0)
            pe.wait_ge(ld_x, 48)
            for_inner_blocks(pe, layer0_pe)

            def prep_pe(L, b, i):
                c = LAYERS[L]
                B = b + NB * L
                base = b * PREP_USES[L] + PREP_BASE[L]
                what = prep_uses(L)[i]
                at_least(pe, prep_evac, base + i)
                if i == 0:
                    pe.wait_ge(xt_evac, b + NB * c["phase"] - (1 if prep_bank(L, b) is bank[7] else 2))
                w = attn_weights(L)[("q", "qs", "k", "ks", "v").index(what)]
                n = w.shape[1]
                if what == "v":
                    x = blk(XT, b) if isinstance(b, int) else XTS[:, :]
                    if not isinstance(b, int):
                        pe.wait_ge(xts_ready, b + (2 * L - 1))
                    for t in range(NT):
                        r = mm(prep_bank(L, b)[:, t * P:t * P + n], x[:, t * P:(t + 1) * P], w, start=True, stop=True)
                else:
                    if not isinstance(b, int) and n < P:
                        pe.sem_inc(pe_passed, 1)
                    r = mm(prep_bank(L, b)[0:n, :], w, blk(XT, b), start=True, stop=True)
                r.then_inc(proj_ready, 1)

            def score(L, b, g, i):
                t, js = S_ITEMS[L][i]
                causal = LAYERS[L]["causal"]
                kl = k_to(L, t)
                if i == 0:
                    pe.wait_ge(stack_landed[g], (b + NB * L + 1) * 32)
                    if LAYERS[L]["alibi"]:
                        pe.wait_ge(alibi_rows, 7 * 16)
                at_least(pe, max_done, item(L, b, g, i) + 1 - s_back(L, i))
                for n, j in enumerate(js):
                    s = bank[S_ORDER[L][i]][:, n * kl:(n + 1) * kl]
                    r = mm(s, QS[0:ROWS_SHIFT, g * GH + j, t * P:(t + 1) * P], KS[0:ROWS_SHIFT, kv_slot(L, g, j), 0:kl],
                           start=True, stop=not causal)
                    if causal:
                        r = mm(s[:, kl - P:kl], identb[:, :], maskb[:, :], start=False, stop=True)
                r.then_inc(s_ready, 1)

            def score_t(L, b, g, i):
                kt, js = ST_ITEMS[L][i]
                causal = LAYERS[L]["causal"]
                w = T - q_from(L, kt)
                if i == 0:
                    pe.wait_ge(shift_landed[g % 2], (half(L, b, g) + 1) * 48)
                at_least(pe, exp_done, item(L, b, g, i) - 1)
                for n, j in enumerate(js):
                    s = bank[st_bank(L, g, i)][:, n * w:(n + 1) * w]
                    r = mm(s, KS[:, kv_slot(L, g, j), kt * P:(kt + 1) * P], QS[:, g * GH + j, T - w:T], start=True, stop=not causal)
                    if causal:
                        r = mm(s[:, 0:P], maskb[:, :], identb[:, :], start=False, stop=True)
                r.then_inc(st_ready, 1)

            def values(L, b, g, kt):
                u = U(L, b, g)
                q0 = q_from(L, kt)
                if kt == 0:
                    at_least(pe, o_evac, u)
                    pe.wait_ge(v_placed, u + 1)
                pe.wait_ge(exp_done, item(L, b, g, kt_end(L, kt)))
                for j in range(GH):
                    r = mm(bank[4][32 * j:32 * (j + 1), q0:T], VA[:, kt, kv_slot(L, g, j), :], PT[kt % 2][:, j, q0:T],
                           start=(kt == 0), stop=(kt == NT - 1))
                r.then_inc(pv_done, 1)

            def shift_t(L, b, g):
                w = U(L, b, g)
                pe.wait_ge(m_split, w + 1)
                pe.wait_ge(o_normed, w - 1) if not isinstance(w, int) or w > 1 else None
                to = bank[7][0:PARTS * GH, 0:T // 2].bitcast(BF16)
                for t in range(NT):
                    r = tr(to[:, t * P:(t + 1) * P], MS[g % 2][:, t, :, :].rearrange("p a b -> p (a b)"), identb[:, :])
                r.then_inc(mt_ready, 1)

            def o_t(L, u, shifts, last=False):
                pe.wait_ge(o_evac, u + 1)
                pe.wait_ge(m_evac, shifts)
                if last:
                    pe.wait_ge(o_normed, u + 1)
                for t in range(NT):
                    r = tr(bank[7][:, t * P:(t + 1) * P], OT[:, t * P:(t + 1) * P], ident[:, :])
                r.then_inc(ot_ready, 1)

            def ao_t(L, b, preps):
                pe.wait_ge(o_normed, U(L, b, NG - 1) + 2)
                at_least(pe, prep_evac, preps)
                for t in range(NT):
                    r = tr(bank[6][:, t * P:(t + 1) * P], AO[:, t, :], ident[:, :])
                r.then_inc(ao_ready, 1)

            def attention_pe(L):
                c = LAYERS[L]
                p = c["phase"]
                if starts_chain(L):
                    if L == 0:
                        pe.wait_ge(pool_const, 3)
                    else:
                        pe.wait_ge(qm_used, 1)
                    pe.wait_ge(xt_evac, NB * p)
                    pe.wait_ge(prep_evac, PREP_BASE[L] + PREP_USES[L])
                    for g in range(2):
                        for i in range(NI[L]):
                            score(L, 0, g, i)
                    shift_t(L, 0, 0)

                def unit(L, b, g):
                    u = U(L, b, g)
                    prev, follow, ahead, prep, end = neighbours(L, b, g)
                    for i in range(NI[L]):
                        score_t(L, b, g, i)
                        if ahead:
                            score(*ahead, i)
                        if prep:
                            at = PE_PREP[LAYERS[prep[0]]["rope"] is not None]
                            if i in at:
                                prep_pe(*prep, at[i])
                        if prev and i == 1:
                            values(*prev, NT - 1)
                        for kt in range(NT - 1):
                            if i == min(kt_end(L, kt) + 1, NI[L] - 1):
                                values(L, b, g, kt)
                        if follow and i == SHIFT_T_AT:
                            shift_t(*follow)
                        if prev and i == O_T_AT:
                            o_t(L, u - 1, u + 2 if follow else u + 1, not follow)
                        if end and g == 0 and i == AO_T_AT:
                            ao_t(*end, PREP_BASE[prep[0]] + (prep[1] + 1) * PREP_USES[prep[0]] if prep else PREP_BASE[L] + NB * PREP_USES[L])
                        if end and g == 1 and i == Y_AT:
                            pe.wait_ge(ao_evac, end[1] + NB * end[0] + 1)
                            y_out(AOT, attn_weights(end[0])[5], end[1], LAYERS[end[0]]["phase"])
                        if end and g == 1 and i == Y_XT_AT:
                            xt(LAYERS[end[0]]["phase"], end[1], bank[6])
                sequence(L, unit, pe.Fori)
                if ends_chain(L):
                    values(L, NB - 1, NG - 1, NT - 1)
                    o_t(L, U(L, NB - 1, NG - 1), U(L, NB - 1, NG - 1) + 1, True)
                    ao_t(L, NB - 1, NB * PREP_USES[L] + PREP_BASE[L])
                    pe.wait_ge(ao_evac, NB * L + NB)
                    y_out(AOT, attn_weights(L)[5], NB - 1, p)
                    xt(p, NB - 1, bank[6])

            def moe_pe(p):
                gi = 0 if p == L1_MOE else 1
                n = MOE_CHUNKS[p]
                pe.wait_ge(xt_evac, NB * p)
                pe.wait_ge(ld_m1 if p == L1_MOE else ld_m2, 80 if p == L1_MOE else 64)
                pe.wait_ge(pool_const, 3)
                for i in range(NB * NT):
                    r = mm(bank[5][:, i * E:(i + 1) * E], XT[:, i * P:(i + 1) * P], wc("l1_gate" if p == L1_MOE else "l2_gate"),
                           start=True, stop=True)
                r.then_inc(lg_ready, 1)
                pe.wait_ge(gw_ready, gi + 1)
                for b in range(NB):
                    at_least(pe, gt_evac, (gi * NB + b) * 2)
                    for i in range(NT):
                        r = tr(bank[6][0:NGATE, i * P:(i + 1) * P], GW[:, b * NT + i, :], ident[:, :])
                    r.then_inc(gt_ready, 1)
                    to = bank[7][0:PARTS * NGATE, 0:T // 2].bitcast(BF16)
                    for i in range(NT):
                        r = tr(to[:, i * P:(i + 1) * P], GWP[:, b * NT + i, :, :].rearrange("p a b -> p (a b)"), identb[:, :])
                    r.then_inc(gt_ready, 1)
                pe.wait_ge(gt_evac, (gi * NB + NB) * 2)

                def up(b, c):
                    k0 = b * n + MOE_BASE[p]
                    at_least(pe, u_ready, k0 + c + 1 - back(p, c, 2))
                    at_least(pe, h_ready, k0 + c + 1 - back(p, c, 2))
                    mm(bank[c % 2][:, :], MW1[:, c * P:(c + 1) * P], blk(XT, b), start=True, stop=True)
                    mm(bank[2 + c % 2][:, :], MW3[:, c * P:(c + 1) * P], blk(XT, b), start=True, stop=True)
                    mm(bank[4 + c % 2][:, :], SEL[:, c, :], blk(RWT, b), start=True, stop=True).then_inc(ab_ready, 1)

                def down(b, c):
                    k = b * n + MOE_BASE[p] + c
                    if c == 0:
                        at_least(pe, y_added, b + NB * p)
                    pe.wait_ge(h_ready, k + 1)
                    for i in range(NT):
                        r = mm(Y[:, i * P:(i + 1) * P], H1[c % NH1[p]][:, i * P:(i + 1) * P], MW2[:, c, :], start=(c == 0 and i == 0),
                               stop=(p == L2_MOE and c == n - 1), skip_group_check=True)
                    r.then_inc(yc_done, 1)
                    if c == n - 1 and p == L1_MOE:
                        pe.wait_ge(rwb_ready, b + 1)
                        for i in range(NT):
                            r = mm(Y[:, i * P:(i + 1) * P], RWB[:, i * P:(i + 1) * P], MB2[:, :], start=False, stop=True, skip_group_check=True)
                        r.then_inc(y_ready, 1)
                    elif c == n - 1:
                        pe.drain().then_inc(y_ready, 1)

                def body(b):
                    first = isinstance(b, int) and b == 0
                    for c in range(n):
                        if c == 0 and not first:
                            down(b - 1, n - 2)
                        up(b, c)
                        if c == 1 and not first:
                            down(b - 1, n - 1)
                        elif c < SUM_AT:
                            pass
                        elif c == SUM_AT + 1:
                            down(b, 0)
                            down(b, 1)
                        elif c > SUM_AT + 1:
                            down(b, c - 2)
                        if c == XT_AT and not first:
                            xt(p, b - 1, bank[7])
                        if is_last(b) and c in PE_START[p]:
                            prep_pe(AFTER[p], 0, PE_START[p][c])
                for_inner_blocks(pe, body)
                down(NB - 1, n - 2)
                down(NB - 1, n - 1)
                pe.wait_ge(prep_evac, PREP_BASE[AFTER[p]] + PREP_USES[AFTER[p]])
                xt(p, NB - 1, bank[7])
                if p == L1_MOE:
                    pe.wait_ge(qs_ready, 1)
                    mm(bank[5][:, 0:2], ones[:, :], qa[:, 0, 0:2], start=True, stop=True).then_inc(qm_ready, 1)

            pe.wait_ge(ld_w, 16)
            pe.wait_ge(ld_1, LD_1)
            for i in range(PREP_USES[0]):
                prep_pe(0, 0, i)
            mix_end(NB - 1)
            linear(NB - 1)
            attention_pe(0)
            moe_pe(L1_MOE)
            attention_pe(1)
            attention_pe(2)
            moe_pe(L2_MOE)
            attention_pe(3)

            def ffn_turn(b):
                pe.wait_ge(fn_ready, b + 1)
                for c in range(4):
                    if c > 1:
                        pe.wait_ge(ft_evac, b * 4 + c - 1)
                    for i in range(NT):
                        r = tr(bank[4 + c % 2][:, i * P:(i + 1) * P], HG[:, i, c * P:(c + 1) * P], ident[:, :])
                    r.then_inc(ft_ready, 1)

            def ffn_down(b):
                at_least(pe, y_added, b + NB * LAST)
                for c in range(4):
                    pe.wait_ge(ft_evac, b * 4 + c + 1)
                    for i in range(NT):
                        r = mm(Y[:, i * P:(i + 1) * P], HT2[:, c, i * P:(i + 1) * P], FW2[:, c, :], start=(c == 0 and i == 0), stop=(c == 3),
                               skip_group_check=True)
                r.then_inc(y_ready, 1)

            def ffn_pe(b):
                if not is_first(b):
                    ffn_turn(b - 1)
                pe.wait_ge(xts_ready, b + (2 * 4 + 1))
                if is_first(b):
                    pe.wait_ge(xt_evac, NB * LAST)
                for i in range(NT):
                    at_least(pe, fb_ready, b * NT + i + 1 - NT)
                    mm(bank[i][:, :], XTS[:, i * P:(i + 1) * P], FW1[:, :], start=True, stop=True).then_inc(fu_ready, 1)
                if not is_first(b):
                    ffn_down(b - 1)
            for_blocks(pe, ffn_pe)
            ffn_turn(NB - 1)
            ffn_down(NB - 1)


def _rotary(interleaved):
    freqs = np.float32(1.0) / np.float32(10000.0) ** (np.arange(0, HD, 2, dtype=np.float32) / np.float32(HD))
    angle = np.arange(T, dtype=np.float32)[None, :] * freqs[:, None].astype(np.float32)
    ch = np.arange(P) % HD
    f = ch // 2 if interleaved else ch % (HD // 2)
    sign = np.where((ch % 2 == 0) if interleaved else (ch < HD // 2), -1.0, 1.0).astype(np.float32)
    return np.stack([np.cos(angle)[f], np.sin(angle)[f] * sign[:, None]]).astype(np.float32)


def _swap(n, interleaved):
    ch = np.arange(n)
    return ch ^ 1 if interleaved else ch ^ (HD // 2)


def kernel(**inputs):
    import ml_dtypes
    import concourse.bacc as bacc
    from concourse.bass_utils import run_bass_kernel_spmd

    a = {k: np.asarray(x) for k, x in inputs.items()}
    c = np.ascontiguousarray
    bf = ml_dtypes.bfloat16
    arrays = {}
    x = a["L0_attn_x"]
    arrays["L0_attn_x"] = c(x)
    arrays["xT"] = c(x.reshape(NB * T, P).T)
    qkv = a["L2_ffn_wqkv"].T
    gq, gk, gv = qkv[:, :P], qkv[:, P:P + 32], qkv[:, P + 32:P + 64]
    l2q, l2k = a["L2_attn_wq"].T, a["L2_attn_wk"].T
    w = {"l0_k": a["L0_attn_Wk"].T, "l0_v": a["L0_attn_Wv"].T, "l0_r": a["L0_attn_Wr"].T, "l0_o": a["L0_attn_Wo"].T,
         "l1_out": a["L1_attn_W_out"].T, "l2_q": l2q, "l2_qs": l2q[:, _swap(P, True)], "l2_k": l2k,
         "l2_ks": l2k[:, _swap(P, True)], "l2_v": a["L2_attn_wv"].T, "l2_o": a["L2_attn_wo"].T,
         "g_q": gq, "g_qs": gq[:, _swap(P, False)], "g_k": gk, "g_ks": gk[:, _swap(32, False)], "g_v": gv,
         "g_o": a["L2_ffn_wo"].T, "l3_q": a["L3_attn_Wq"], "l3_k": a["L3_attn_Wk"], "l3_v": a["L3_attn_Wv"],
         "l3_o": a["L3_attn_Wo"], "l1_gate": a["L1_ffn_gate_w"].T, "l2_gate": a["L2_ffn_gate_w"].T}
    arrays["wpack"] = c(np.concatenate([w[n] for n in W_COLS], axis=1))

    def col(v):
        out = np.zeros((-(-v.size // P) * P,), np.float32)
        out[:v.size] = v.reshape(-1)
        return out.reshape(-1, P).T

    hidden = np.concatenate([a["L1_ffn_b1"].reshape(-1), a["L1_ffn_sb1"]])
    hidden3 = np.concatenate([a["L1_ffn_b3"].reshape(-1), a["L1_ffn_sb3"]])
    cols = {"decay": a["L0_attn_time_decay"], "first": a["L0_attn_time_first"], "mix": a["L0_attn_time_mix"],
            "ln1_w": a["L2_ffn_ln1_w"], "ln2_w": a["L2_ffn_ln2_w"], "bq": a["L3_attn_bq"], "bk": a["L3_attn_bk"],
            "f_ln1_g": a["L3_ffn_ln1_g"], "f_ln1_b": a["L3_ffn_ln1_b"], "f_ln2_g": a["L3_ffn_ln2_g"],
            "f_ln2_b": a["L3_ffn_ln2_b"], "m_b1": hidden, "m_b3": hidden3}
    arrays["cols"] = c(np.concatenate([col(cols[n]) for n in C_COLS], axis=1))
    rows = {"logits": a["L0_ffn_logits"], "u": a["L0_ffn_u"], "l0_b": a["L0_ffn_b"], "gate_b": a["L1_ffn_gate_b"],
            "b_out": a["L1_attn_b_out"], "bv": a["L3_attn_bv"], "bo": a["L3_attn_bo"], "f_b1": a["L3_ffn_b1"], "f_b2": a["L3_ffn_b2"]}
    arrays["rows"] = c(np.concatenate([rows[n].reshape(-1) for n in R_COLS]))
    arrays["L0_ffn_W"] = c(a["L0_ffn_W"])
    for n, k in (("l1_wq", "L1_attn_Wq"), ("l1_wk", "L1_attn_Wk"), ("l1_wv", "L1_attn_Wv")):
        arrays[n] = c(a[k].T)
    arrays["ident"] = np.eye(P, dtype=np.float32)
    arrays["identb"] = np.eye(P).astype(bf)
    arrays["maskb"] = np.where(np.arange(P)[None, :] > np.arange(P)[:, None], MASKED, 0.0).astype(bf)
    arrays["tables"] = c(np.stack([_rotary(True), _rotary(False)]))
    f1 = a["L1_ffn_w1"].shape[2]
    n1 = 13 * P

    def up(we, ws):
        out = np.zeros((P, n1), np.float32)
        out[:, :E * f1] = we.transpose(1, 0, 2).reshape(P, E * f1)
        out[:, E * f1:(E + 1) * f1] = ws
        return out

    arrays["m1_w1"], arrays["m1_w3"] = up(a["L1_ffn_w1"], a["L1_ffn_sw1"]), up(a["L1_ffn_w3"], a["L1_ffn_sw3"])
    w2 = np.zeros((n1, P), np.float32)
    w2[:E * f1] = a["L1_ffn_w2"].reshape(E * f1, P)
    w2[E * f1:(E + 1) * f1] = a["L1_ffn_sw2"]
    arrays["m1_w2"] = c(w2.reshape(13, P, P).transpose(1, 0, 2))
    arrays["m1_b2"] = c(np.concatenate([a["L1_ffn_b2"], a["L1_ffn_sb2"][None]]))
    w13 = a["L2_ffn_w13"]
    f2 = w13.shape[1] // 2
    arrays["m2_w1"] = c(w13[:, :f2].transpose(2, 0, 1).reshape(P, E * f2))
    arrays["m2_w3"] = c(w13[:, f2:].transpose(2, 0, 1).reshape(P, E * f2))
    arrays["m2_w2"] = c(a["L2_ffn_w2"].transpose(0, 2, 1).reshape(16, P, P).transpose(1, 0, 2))
    sel = np.zeros((2, P, 16, P), np.float32)
    for i, (f, n) in enumerate(((f1, 9 * f1), (f2, E * f2))):
        for r in range(n):
            for part in range(PARTS):
                sel[i, part * NGATE + r // f, r // P, r % P] = 1.0
    arrays["sel"] = sel.astype(bf)
    arrays["f_w1"] = c(a["L3_ffn_w1"].T)
    arrays["f_w2"] = c(a["L3_ffn_w2"].T.reshape(4, P, P).transpose(1, 0, 2))
    arrays["slopes"] = c(a["L3_attn_slopes"].reshape(H, 1))
    pad = np.zeros((P - STACK, H, T))
    arrays["qpad"] = pad.astype(bf)
    pad[ROWS_SHIFT - STACK:] = 1.0
    arrays["kpad"] = pad.astype(bf)
    pos = np.arange(T)
    kp = np.stack([pos // 256 * 256, pos % 256]).astype(bf)
    arrays["kpos"] = c(np.broadcast_to(np.tile(kp, (PARTS, 1))[:, None, :], (ALIBI, NG, T)))

    nc = bacc.Bacc("TRN2", target_bir_lowering=False, num_devices=1)
    d = {n: nc.dram_tensor("in_" + n, v.shape, mybir.dt.from_np(v.dtype), kind="ExternalInput").ap() for n, v in arrays.items()}
    d["out"] = nc.dram_tensor("out_x", (NB, T, P), F32, kind="ExternalOutput").ap()
    build(nc, d)
    r = run_bass_kernel_spmd(nc, [{"in_" + n: v for n, v in arrays.items()}], core_ids=[0])
    return r.results[0]["out_x"]
```

```python
from contextlib import ExitStack

import numpy as np

import concourse.bass as bass
from concourse import mybir

F32 = mybir.dt.float32
BF16 = mybir.dt.bfloat16
ALU = mybir.AluOpType
ACT = mybir.ActivationFunctionType
AX_X = mybir.AxisListType.X
AX_XY = mybir.AxisListType.XY

P = 128
NB = 4
T = 512
NT = T // P
H = 16
HD = P // H
GH = 4
NG = H // GH
PARTS = 3
STACK = HD * PARTS * PARTS
ALIBI = 2 * PARTS
ROWS_SHIFT = P - PARTS
VW = 32
E = 8
NGATE = 9
MASKED = -1.0e30
LN_EPS = 1e-5

(L0_MIX, L0_LINEAR, L1_ATTN, L1_MOE, L2_ATTN, L2_GQA, L2_MOE, L3_ATTN, L3_FFN) = range(9)
LAST = L3_FFN
NORMS = {L0_MIX: ("ln",), L0_LINEAR: ("ln",), L1_ATTN: ("ln",), L1_MOE: ("ln",), L2_ATTN: ("ln", "rms"),
         L2_GQA: ("rms",), L2_MOE: ("ln",), L3_ATTN: ("ln", "ln"), L3_FFN: ("ln",)}
NH1 = {L1_MOE: 5, L2_MOE: 4}
SUM_AT, NORM_AT, XT_AT, XT_OUT_AT = {L1_MOE: 1, L2_MOE: 2}, 3, 5, 5
DOWN_AT = 3
NORM_BASE = [sum(NB * len(NORMS[q]) for q in range(p)) for p in range(9)]

LAYERS = [
    dict(phase=L1_ATTN, kv=H, scale=P ** -0.5, causal=False, rope=None, alibi=False),
    dict(phase=L2_ATTN, kv=H, scale=HD ** -0.5, causal=True, rope=0, alibi=False),
    dict(phase=L2_GQA, kv=NG, scale=HD ** -0.5, causal=True, rope=1, alibi=False),
    dict(phase=L3_ATTN, kv=NG, scale=1.0, causal=True, rope=None, alibi=True),
]
PREP_USES = [5 if c["rope"] is not None else 3 for c in LAYERS]
PREP_BASE = [sum(NB * n for n in PREP_USES[:i]) for i in range(4)]
CHAINS = [(0,), (1, 2), (3,)]

_WHOLE = [(t, [j]) for t in range(NT) for j in range(GH)]
_CAUSAL = [(t, [j]) for t in range(2) for j in range(GH)] + [(2, [0, 1]), (2, [2, 3]), (3, [0, 1, 2, 3])]
ST_ITEMS = [_CAUSAL if c["causal"] else _WHOLE for c in LAYERS]
S_ITEMS = [[(NT - 1 - t, js) for t, js in _CAUSAL] if c["causal"] else _WHOLE for c in LAYERS]
NI = [len(x) for x in S_ITEMS]
ITEM_BASE = [sum(NB * NG * n for n in NI[:i]) for i in range(4)]
S_ORDER = [[0, 1, 5] * 5 + [1] if n == 16 else ([0, 1, 5] * 4)[:n] for n in NI]


def s_back(L, i):
    order = S_ORDER[L] + S_ORDER[L][:i]
    return NI[L] + i - max(k for k in range(len(order)) if order[k] == S_ORDER[L][i])


def st_bank(L, g, i):
    return 2 + (g * NI[L] + i) % 2


def kt_end(L, kt):
    return max(i for i, (t, _) in enumerate(ST_ITEMS[L]) if t == kt) + 1


def neighbours(L, b, g):
    chain = next(c for c in CHAINS if L in c)
    at = chain.index(L)
    before = chain[at - 1] if at else None
    after = chain[at + 1] if at + 1 < len(chain) else None
    is_first, is_last = isinstance(b, int) and b == 0, isinstance(b, int) and b == NB - 1
    last_block = None if is_first and before is None else (before, NB - 1) if is_first else (L, b - 1)
    next_block = None if is_last and after is None else (after, 0) if is_last else (L, b + 1)
    prev = (L, b, g - 1) if g else last_block and (*last_block, NG - 1)
    follow = (L, b, g + 1) if g < NG - 1 else next_block and (*next_block, 0)
    ahead = (L, b, g + 2) if g < 2 else next_block and (*next_block, g - 2)
    return prev, follow, ahead, next_block if g == 0 else None, last_block


NORM_BESIDE, LINEAR_SUM_BESIDE, LINEAR_NORM_BESIDE = 0, 5, 7
XT_BESIDE, LINEAR_BESIDE, LINEAR_XT_BESIDE = 3, 4, 11
SHIFT_BESIDE = {0: 7, 1: 4, 3: 4}
AFTER = {L1_MOE: 1, L2_MOE: 3}
PE_START = {L1_MOE: {0: 0, 1: 1, 2: 2, 3: 3, 4: 4}, L2_MOE: {0: 0, 1: 1, 2: 2}}
DVE_START = {L1_MOE: {0: 0, 1: 1, 2: 2, 3: 3}, L2_MOE: {3: 2}}
ACT_START = {L1_MOE: {4: ["v"], 6: ["q0"], 7: ["q1"], 8: ["k0"], 9: ["k1"]}, L2_MOE: {1: ["q"], 2: ["k"], 6: ["q1"], 8: ["k1"]}}
PE_PREP = {True: {0: 0, 2: 1, 4: 2, 6: 3, 8: 4}, False: {0: 0, 2: 1, 4: 2}}
DVE_PREP = {True: {0: 0, 2: 1, 4: 2, 6: 3}, False: {5: 2}}
ACT_PREP = {True: {0: ["xts"], 4: ["q0"], 6: ["q1"], 8: ["v", "k0"], 9: ["k1"]},
            False: {0: ["xts"], 1: ["q"], 3: ["k"], 4: ["q1"], 5: ["v"], 6: ["k1"]}}
CASTS = {True: ["q0", "q1", "k0", "k1"], False: ["q", "k", "q1", "k1"]}
SHIFT_T_AT, O_OUT_AT, O_T_AT, O_NORM_AT, AO_T_AT, AO_OUT_AT = 3, 3, 6, 7, 9, 10
Y_AT, Y_SUM_AT, Y_STATS_AT = (1, 1), (1, 4), (1, 6)
LATER = dict(norm=(2, 2), stats2=(2, 5), norm2=(3, 3), xt=(3, 6), out=(3, 7))
EARLIER = dict(norm=(2, 1), stats2=(2, 1), norm2=(2, 3), xt=(2, 6), out=(2, 7))
GATED_FIRST = NB - 1
LOGITS_AT, GATES_AT = {2: 0, 4: 1, 9: 2}, 9
GATES_T_AT = {5: 0, 7: 1, 9: 2}
TERNARY_ABS_AT, TERNARY_SUM_AT, TERNARY_AT, SLOPES_AT = (2, 0), (2, 1), (2, 8), (3, 12)
LATE_LOGITS_AT, LATE_GATES_AT, LATE_T_AT = 6, 7, 11
GATED_BY = {0: L1_MOE, 2: L2_MOE}
BEFORE = {L1_MOE: 0, L2_MOE: 2}

MOE_CHUNKS = {L1_MOE: 13, L2_MOE: 16}
MOE_BASE = {L1_MOE: 0, L2_MOE: NB * 13}

W_COLS, _at = {}, 0
for _n, _w in [("l0_k", P), ("l0_v", P), ("l0_r", P), ("l0_o", P), ("l1_out", P),
               ("l2_q", P), ("l2_qs", P), ("l2_k", P), ("l2_ks", P), ("l2_v", P), ("l2_o", P),
               ("g_q", P), ("g_qs", P), ("g_k", 32), ("g_ks", 32), ("g_v", 32), ("g_o", P),
               ("l3_q", P), ("l3_k", 32), ("l3_v", 32), ("l3_o", P), ("l1_gate", E), ("l2_gate", E)]:
    W_COLS[_n] = (_at, _at + _w)
    _at += _w
W_TOTAL = _at
C_COLS, _at = {}, 0
for _n, _w in [("decay", 1), ("first", 1), ("mix", 1), ("ln1_w", 1), ("ln2_w", 1), ("bq", 1), ("bk", 1),
               ("f_ln1_g", 1), ("f_ln1_b", 1), ("f_ln2_g", 4), ("f_ln2_b", 4), ("m_b1", 13), ("m_b3", 13)]:
    C_COLS[_n] = (_at, _at + _w)
    _at += _w
C_TOTAL = _at
R_COLS, _at = {}, 0
for _n, _w in [("logits", E), ("u", E), ("l0_b", E * P), ("gate_b", E), ("b_out", P), ("bv", 32), ("bo", P),
               ("f_b1", T), ("f_b2", P)]:
    R_COLS[_n] = (_at, _at + _w)
    _at += _w
R_TOTAL = _at


def post_index(p, b):
    return b * 2 + p if p <= L0_LINEAR else b + NB * p


def norm_index(p, b):
    return b * 2 + p if p <= L0_LINEAR else b * len(NORMS[p]) + NORM_BASE[p]


def for_blocks(eng, body):
    body(0)
    with eng.Fori(1, NB) as b:
        body(b)


def for_inner_blocks(eng, body):
    body(0)
    with eng.Fori(1, NB - 1) as b:
        body(b)
    body(NB - 1)


def is_first(b):
    return isinstance(b, int) and b == 0


def is_last(b):
    return isinstance(b, int) and b == NB - 1


def back(p, c, m):
    n = MOE_CHUNKS[p]
    return m if c >= m else c + n - max(j for j in range(n) if j % m == c)


def end_at(L, b):
    return EARLIER if is_last(b) and any(L == c[-1] for c in CHAINS) else LATER


def at_least(eng, sem, count):
    if isinstance(count, int) and count <= 0:
        return
    eng.wait_ge(sem, count)


def build(nc, d):
    ctx = ExitStack()
    with ctx:
        def sb(name, shape, dt=F32):
            return ctx.enter_context(nc.sbuf_tensor(name, shape, dt))

        def sem(name):
            return ctx.enter_context(nc.semaphore(name))

        bank = [ctx.enter_context(nc.psum_tensor(f"bank{i}", [P, T], F32)) for i in range(8)]
        X = sb("X", [P, NB * T])
        X1buf = sb("X1", [P, NB * (T + 1)])
        X1 = X1buf[:, 0:NB * T]
        XTP = X1buf[:, :].rearrange("p (b t) -> p b t", b=NB)
        XT = sb("XT", [P, NB * T])
        XTS = sb("XTS", [P, T])
        WC = sb("WC", [P, W_TOTAL])
        CC = sb("CC", [P, C_TOTAL])
        RC = sb("RC", [P, R_TOTAL])
        ident = sb("ident", [P, P])
        identb = sb("identb", [P, P], BF16)
        maskb = sb("maskb", [P, P], BF16)
        WQKV1 = sb("WQKV1", [P, 3, P])
        WSEL = sb("WSEL", [P, P])
        BSEL = sb("BSEL", [P, P])
        tables = sb("tables", [P, 2, 2, T])
        MW1 = sb("MW1", [P, 16 * P])
        MW3 = sb("MW3", [P, 16 * P])
        MW2 = sb("MW2", [P, 16, P])
        MB2 = sb("MB2", [NGATE, P])
        SEL = sb("SEL", [P, 13, P], BF16)
        RWT = sb("RWT", [P, NB * T], BF16)
        RW9 = sb("RW9", [NGATE, NB * T])
        RWB = sb("RWB", [NGATE, T])
        FW1 = sb("FW1", [P, T])
        FW2 = sb("FW2", [P, 4, P])
        QS = sb("QS", [P, H, T], BF16)
        KS = sb("KS", [P, H, T], BF16)
        PQ = sb("PQ", [P, PARTS, T], BF16)
        PK = sb("PK", [P, PARTS, T], BF16)
        QF = sb("QF", [P, T])
        KF = sb("KF", [P, T])
        RA = sb("RA", [P, 2, T])
        SA = sb("RB", [P, 2, T + 1])
        RB = SA[:, :, 0:T]
        W0 = RA[:, :, :].rearrange("p a (n d) -> p (a n) d", d=P)
        VST = sb("VST", [P, NT, P])
        VA = sb("VA", [P, NT, H, VW])
        PT = [sb(f"PT{i}", [P, GH, T]) for i in range(2)]
        M = [sb(f"M{i}", [P, NT * GH]) for i in range(2)]
        MR = sb("MR", [P, NT * GH])
        MS = [sb(f"MS{i}", [P, NT, PARTS, GH], BF16) for i in range(2)]
        MSB = [sb(f"MSB{i}", [PARTS * GH, T], BF16) for i in range(2)]
        OT = sb("OT", [P, T])
        OR = sb("OR", [P, NT * GH])
        AO = sb("AO", [P, NT, P])
        AOT = sb("AOT", [P, T])
        slope = sb("slope", [H, 1])
        slope_r = sb("slope_r", [H, 1])
        slope_p = sb("slope_p", [H, PARTS], BF16)
        slope_w = sb("slope_w", [H, PARTS, T], BF16)
        YB = sb("YB", [P, NT, P])
        N1 = sb("N1", [P, NT, P])
        N2 = sb("N2", [P, NT, P])
        ST = sb("ST", [P, NT, 6])
        MV = sb("MV", [P, NT, 2])
        MS2 = sb("MS2", [P, NT])
        VE = sb("VE", [P, NT])
        RSTD = sb("RSTD", [P, NT])
        neg_half = sb("neg_half", [P, NT])
        bqs = sb("bqs", [P, 1])
        GL = sb("GL", [P, NB * NT, E])
        GE = sb("GE", [P, NB * NT, E])
        GB = sb("GB", [P, NB * NT, E])
        GR = sb("GR", [P, NB * NT, E])
        GO = sb("GO", [P, NB * NT, E])
        GM = sb("GM", [P, NB * NT])
        GW = sb("GW", [P, NB * NT, NGATE])
        GWR = sb("GWR", [P, NB * NT, NGATE])
        GWP = sb("GWP", [P, NB * NT, PARTS, NGATE], BF16)
        rev = sb("rev", [P, E])
        sel0 = sb("sel0", [P, 12, E])
        A1 = [PT[0][:, 0, :], PT[0][:, 1, :]]
        U1 = [PT[0][:, 2, :], PT[0][:, 3, :]]
        S1 = [sb(f"S1{i}", [P, T])[:, :] for i in range(2)]
        H1 = [PT[1][:, i, :] for i in range(NT)] + [sb("H4", [P, T])[:, :]]
        gates_here = sb("gates_here", [P, NT, E])
        routed = S1[0].rearrange("p (a b) -> p a b", a=NT)
        XM0, XM, KM, KE = (PT[0][:, i, :] for i in range(4))
        SG, KV, RWKV = (PT[1][:, i, :] for i in range(3))
        cols0 = sb("cols0", [P, 4])
        HG = [PT[0][:, :, :], MW1[:, :].rearrange("p (a b) -> p a b", a=NT)]
        HT2 = PT[1]
        FST = sb("FST", [P, NT, 6])
        FMV = sb("FMV", [P, NT, 2])
        FMS, FVE, FRSTD = (sb(n, [P, NT]) for n in ("FMS", "FVE", "FRSTD"))
        qa = sb("qa", [P, 2, 8])
        ones = sb("ones", [P, P])
        qt0 = S1[0]

        LD_1 = 16 * (4 + 3 * H + 4)
        ld_c, ld_w0 = sem("load_first"), sem("load_l0_weights")
        ld_x, ld_0, ld_w, ld_1, ld_m1, ld_m2, ld_f = (sem("load_" + n) for n in
                                                      ("x", "l0", "weights", "l1", "moe1", "moe2", "ffn"))
        pool_const = sem("pool_const")
        pool_passed, pe_passed = sem("pool_passed"), sem("pe_passed")
        y_ready, y_added, var_ready, rstd_ready, normed, x_saved, xt_ready, xt_evac, out_done = (sem(n) for n in (
            "pe_y", "dve_y_added", "dve_var", "pool_rstd", "dve_normed", "pool_x_saved", "pe_xt", "act_xt", "dma_out"))
        z_sem, z2_sem, sel_ready, xm0_ready, xm_ready, kvr_ready, km_ready, ke_ready, rwkv_ready = (sem(n) for n in (
            "act_z", "dve_z", "dve_sel", "pool_xm0", "dve_xm", "pe_kvr", "dve_km", "act_ke", "dve_rwkv"))
        c0a, c0b, sg_ready = sem("act_cols0"), sem("dve_cols0"), sem("act_sigmoid")
        kv_ready, wkv_ready, gated = sem("dve_kv"), sem("dve_wkv"), sem("pool_gated")
        (proj_ready, prep_evac, parts_ready, parts_stored, v_placed, s_ready, max_done, m_split, mt_ready, m_evac,
         st_ready, exp_done, pv_done, o_evac, ot_ready, o_normed, ao_ready, ao_evac, xts_ready, alibi_rows) = (sem(n) for n in (
             "pe_proj", "prep_evac", "pool_parts", "dma_parts", "pool_v", "pe_scores", "dve_max", "dve_shift",
             "pe_shift", "act_shift", "pe_scores_t", "act_exp", "pe_pv", "act_o", "pe_o_t", "dve_o", "pe_ao", "act_ao",
             "pool_xts", "dma_alibi"))
        qm_used, tern_ready = sem("dve_absum_used"), sem("dve_ternary")
        slope_ready = sem("dve_slope")
        rotated, rest_ready, cast_done = sem("pool_rotated"), sem("pool_rest"), sem("act_cast")
        stack_landed = [sem(f"dma_stack{g}") for g in range(NG)]
        shift_landed = [sem(f"dma_shift{i}") for i in range(2)]
        (lg_ready, gm_ready, ge_ready, gw_ready, gt_ready, gt_evac, rwb_ready, ab_ready, a_evac, u_ready, s1_ready,
         h_ready, yc_done) = (sem(n) for n in (
             "pe_logits", "dve_gmax", "act_gexp", "dve_gates", "pe_gates_t", "act_gates_t", "pool_rwb", "pe_ab", "act_a", "dve_u",
             "act_silu", "dve_h", "pe_chunk"))
        gates_placed, summed = sem("pool_gates"), sem("dve_summed")
        (qs_ready, qm_ready, fu_ready, fb_ready, fg_ready, fv_ready, fr_ready, fn_ready, ft_ready, ft_evac) = (sem(n) for n in (
            "dve_absum", "pe_absum", "pe_up", "dve_up", "act_gelu", "dve_fvar", "pool_frstd", "dve_fnorm", "pe_ft", "act_ft"))

        scr_q = nc.dram_tensor("scr_q", [H * STACK * T], BF16, kind="Internal").ap().tensor
        scr_k = nc.dram_tensor("scr_k", [H * STACK * T], BF16, kind="Internal").ap().tensor

        def wc(name):
            return WC[:, W_COLS[name][0]:W_COLS[name][1]]

        def cc(name, i=0, rows=P):
            return CC[0:rows, C_COLS[name][0] + i:C_COLS[name][0] + i + 1]

        def rc(name):
            return RC[:, R_COLS[name][0]:R_COLS[name][1]]

        def blk(t, b):
            return t[:, b * T:(b + 1) * T] if isinstance(b, int) else t[:, bass.ds(b * T, T)]

        def tiles(ap, n=NT):
            return ap.rearrange("p (a b) -> p a b", a=n)

        Y = bank[6]
        block = ctx.enter_context(nc.Block())

        NEXT_BIAS = {L0_MIX: lambda: BSEL[:, :], L0_LINEAR: lambda: rc("b_out"), L2_MOE: lambda: rc("bo"),
                     L3_ATTN: lambda: rc("f_b2")}

        def attn_weights(L):
            return [(WQKV1[:, 0, :], None, WQKV1[:, 1, :], None, WQKV1[:, 2, :], wc("l1_out")),
                    (wc("l2_q"), wc("l2_qs"), wc("l2_k"), wc("l2_ks"), wc("l2_v"), wc("l2_o")),
                    (wc("g_q"), wc("g_qs"), wc("g_k"), wc("g_ks"), wc("g_v"), wc("g_o")),
                    (wc("l3_q"), None, wc("l3_k"), None, wc("l3_v"), wc("l3_o"))][L]

        def prep_uses(L):
            return ["q", "qs", "k", "ks", "v"] if LAYERS[L]["rope"] is not None else ["q", "k", "v"]

        def U(L, b, g):
            return (b + NB * L) * NG + g

        def half(L, b, g):
            return (b + NB * L) * 2 + g // 2

        def item(L, b, g, i=0):
            return (b * NG + g) * NI[L] + (ITEM_BASE[L] + i)

        def sequence(L, unit, Fori):
            for g in range(NG):
                unit(L, 0, g)
            with Fori(1, NB - 1) as b:
                for g in range(NG):
                    unit(L, b, g)
            for g in range(NG):
                unit(L, NB - 1, g)

        def xt_bank(p, b):
            here = p in (L1_ATTN, L2_ATTN, L2_GQA, L3_ATTN) and not (is_last(b) and p != L2_ATTN)
            return bank[6] if here else bank[7]

        def prep_bank(L, b, what):
            if isinstance(b, int) and b == 0 and starts_chain(L):
                return bank[3 + "qkv".index(what)] if L == 0 else bank[7]
            return bank[6]

        def gate_part(p, part):
            return (0 if p == L1_MOE else 2) + part

        def gate_tiles(part):
            return slice(GATED_FIRST * NT, NB * NT) if part else slice(0, GATED_FIRST * NT)

        def starts_chain(L):
            return any(L == c[0] for c in CHAINS)

        def ends_chain(L):
            return any(L == c[-1] for c in CHAINS)

        def q_from(L, t):
            return t * P if LAYERS[L]["causal"] else 0

        def k_to(L, t):
            return (t + 1) * P if LAYERS[L]["causal"] else T

        def kv_slot(L, g, j):
            return g if LAYERS[L]["kv"] == NG else g * GH + j

        @block.sync
        def _(sp):
            xT = d["xT"].rearrange("c (b t) -> c b t", b=NB)
            sp.dma_start(CC[:, :], d["cols"]).then_inc(ld_c, 16)
            sp.dma_start(XTP[:, 0, 1:T + 1], xT[:, 0, :]).then_inc(ld_c, 16)
            sp.dma_start(WC[:, 0:4 * P], d["wpack"][:, 0:4 * P]).then_inc(ld_w0, 16)
            sp.dma_start(RC[:, :], d["rows"].partition_broadcast(P)).then_inc(ld_0, 16)
            sp.dma_start(XTP[:, 1:NB, 1:T + 1], xT[:, 1:NB, :]).then_inc(ld_x, 16)
            sp.dma_start(W0[:, :, :], d["L0_ffn_W"].rearrange("n d e -> d n e")).then_inc(ld_0, 16)
            sp.dma_start(ident[:, :], d["ident"]).then_inc(ld_x, 16)
            sp.dma_start(tiles(X[:, :], NB * NT), d["L0_attn_x"].rearrange("b (t p) c -> p (b t) c", p=P)).then_inc(ld_x, 16)
            sp.dma_start(WC[:, 4 * P:W_TOTAL], d["wpack"][:, 4 * P:W_TOTAL]).then_inc(ld_w, 16)
            sp.dma_start(QS[STACK:P, :, :], d["qpad"]).then_inc(ld_1, 16)
            sp.dma_start(KS[STACK:P, :, :], d["kpad"]).then_inc(ld_1, 16)
            sp.dma_start(identb[:, :], d["identb"]).then_inc(ld_1, 16)
            sp.dma_start(maskb[:, :], d["maskb"]).then_inc(ld_1, 16)
            sp.wait_ge(pool_const, 1)
            for i, n in enumerate(("l1_wq", "l1_wk", "l1_wv")):
                for h in range(H):
                    sp.dma_start(WQKV1[h * HD:(h + 1) * HD, i, h * HD:(h + 1) * HD], d[n]).then_inc(ld_1, 16)
            for i in range(2):
                for k in range(2):
                    sp.dma_start(tables[:, i, k, :], d["tables"][i, k]).then_inc(ld_1, 16)
            sp.dma_start(SEL[:, :, :], d["sel"]).then_inc(ld_m1, 16)
            sp.dma_start(MW1[:, 0:13 * P], d["m1_w1"]).then_inc(ld_m1, 16)
            sp.dma_start(MW3[:, 0:13 * P], d["m1_w3"]).then_inc(ld_m1, 16)
            sp.dma_start(MW2[:, 0:13, :], d["m1_w2"]).then_inc(ld_m1, 16)
            sp.dma_start(MB2[:, :], d["m1_b2"]).then_inc(ld_m1, 16)
            sp.dma_start(FW1[:, :], d["f_w1"]).then_inc(ld_f, 16)
            sp.dma_start(FW2[:, :, :], d["f_w2"]).then_inc(ld_f, 16)
            sp.dma_start(slope[:, :], d["slopes"]).then_inc(ld_f, 16)

            def store_parts(L, b):
                B = b + NB * L
                nk = LAYERS[L]["kv"] * HD
                for g in range(NG):
                    at_least(sp, stack_landed[g], B * 32)
                at_least(sp, parts_ready, B * 2 + 1)
                for j in range(PARTS):
                    sp.dma_start(bass.AP(tensor=scr_q, offset=j * T, ap=[[9 * T, P], [3 * T, 3], [1, T]]),
                                 PQ[:, :, :]).then_inc(parts_stored, 16)
                at_least(sp, parts_ready, B * 2 + 2)
                for i in range(PARTS):
                    sp.dma_start(bass.AP(tensor=scr_k, offset=3 * i * T, ap=[[9 * T, nk], [T, 3], [1, T]]),
                                 PK[0:nk, :, :]).then_inc(parts_stored, 16)
                at_least(sp, parts_stored, (B + 1) * 96)

            def load_stack(L, b, g):
                if not (L == 0 and isinstance(b, int) and b == 0):
                    if isinstance(b, int) and b == 0:
                        sp.wait_ge(st_ready, item(L - 1, NB - 1, g, NI[L - 1]))
                    else:
                        sp.wait_ge(st_ready, item(L, b - 1, g, NI[L]))
                sp.dma_start(QS[0:STACK, g * GH:(g + 1) * GH, :],
                             bass.AP(tensor=scr_q, offset=g * GH * STACK * T, ap=[[T, STACK], [STACK * T, GH], [1, T]])
                             ).then_inc(stack_landed[g], 16)
                n = GH if LAYERS[L]["kv"] == H else 1
                sp.dma_start(KS[0:STACK, g * n:(g + 1) * n, :],
                             bass.AP(tensor=scr_k, offset=g * n * STACK * T, ap=[[T, STACK], [STACK * T, n], [1, T]])
                             ).then_inc(stack_landed[g], 16)

            def load_shift(L, b, g):
                at_least(sp, m_evac, U(L, b, g) + 1)
                for i in range(PARTS):
                    sp.dma_start(QS[ROWS_SHIFT + i:ROWS_SHIFT + i + 1, g * GH:(g + 1) * GH, :],
                                 MSB[g % 2][i * GH:(i + 1) * GH, :]).then_inc(shift_landed[g % 2], 16)

            def attention_sp(L):
                if LAYERS[L]["alibi"]:
                    sp.wait_ge(slope_ready, 1)
                    sp.wait_ge(st_ready, ITEM_BASE[L])
                    for i in range(PARTS):
                        for k in range(2):
                            r = STACK + 2 * i + k
                            sp.dma_start(QS[r:r + 1, :, :], slope_w[:, i, :]).then_inc(alibi_rows, 16)
                    sp.dma_start(KS[STACK:STACK + ALIBI, 0:NG, :], d["kpos"]).then_inc(alibi_rows, 16)
                if starts_chain(L):
                    store_parts(L, 0)
                    for g in range(3):
                        load_stack(L, 0, g)
                    load_shift(L, 0, 0)

                def unit(L, b, g):
                    prev, follow, ahead, prep, end = neighbours(L, b, g)
                    if g == 0:
                        load_stack(L, b, 3)
                    if follow:
                        load_shift(*follow)
                    if prep:
                        store_parts(*prep)
                        load_stack(*prep, 0)
                    elif g >= 2 and ahead:
                        load_stack(ahead[0], ahead[1], g - 1)
                sequence(L, unit, sp.Fori)

            attention_sp(0)
            attention_sp(1)
            sp.wait_ge(xt_evac, 4 * (L1_MOE + 1))
            sp.dma_start(MW1[:, :], d["m2_w1"]).then_inc(ld_m2, 16)
            sp.dma_start(MW3[:, :], d["m2_w3"]).then_inc(ld_m2, 16)
            sp.dma_start(MW2[:, :, :], d["m2_w2"]).then_inc(ld_m2, 16)
            attention_sp(2)
            attention_sp(3)
            with sp.Fori(0, NB) as b:
                sp.wait_ge(normed, b + 4 * LAST + 1)
                sp.dma_start(d["out"][bass.ds(b, 1)].rearrange("a (t p) c -> p (a t) c", p=P), N1[:, :, :]).then_inc(out_done, 16)
            sp.wait_ge(out_done, 16 * NB)

        @block.gpsimd
        def _(pool):
            g = nc.gpsimd

            def wait(sem, count):
                at_least(pool, sem, count)
                if not isinstance(count, int):
                    pool.sem_inc(pool_passed, 1)
            g.memset(WQKV1[:, :, :], 0.0).then_inc(pool_const, 1)
            g.memset(XTP[:, :, 0:1], 0.0)
            g.memset(SA[:, :, 0:1], 0.0)
            g.memset(neg_half[:, :], -0.5)
            g.iota(rev[:, :], pattern=[[-1, E]], base=E, channel_multiplier=0, allow_small_or_imprecise_dtypes=True)
            g.memset(ones[:, :], 1.0).then_inc(pool_const, 1)

            def shifted(b):
                at_least(pool, xm_ready, b)
                if not isinstance(b, int):
                    pool.sem_inc(pool_passed, 1)
                xs = XTP[:, b, 0:T] if isinstance(b, int) else XTP[:, bass.ds(b, 1), 0:T].rearrange("p a b -> p (a b)")
                g.tensor_tensor(XM0, xs, cols0[:, 0:1].to_broadcast([P, T]), ALU.mult).then_inc(xm0_ready, 1)
            pool.wait_ge(c0b, 1)
            pool.wait_ge(ld_c, 32)
            pool.drain()
            shifted(0)
            g.memset(VA[:, :, :, :], 0.0)
            pool.drain()
            g.memset(VA[:, :, :, HD:HD + 1], 1.0)
            g.memset(RWT[:, :], 0.0).then_inc(pool_const, 1)
            pool.drain()

            def rstd(idx, eps):
                wait(var_ready, idx + 1)
                g.tensor_scalar(VE[:, :], MS2[:, :], eps, 1.0, ALU.add, ALU.mult)
                pool.drain()
                g.tensor_tensor(RSTD[:, :], VE[:, :], neg_half[:, :], ALU.pow).then_inc(rstd_ready, 1)

            def post_root(p, b):
                n0 = norm_index(p, b)
                if p == L2_GQA:
                    wait(var_ready, n0 + 1)
                    g.tensor_copy(blk(X1, b), YB[:, :, :].rearrange("p a b -> p (a b)")).then_inc(x_saved, 1)
                rstd(n0, LN_EPS)

            def post_save(p, b):
                pi = post_index(p, b)
                n0 = norm_index(p, b)
                if p in (L2_GQA, LAST):
                    return
                wait(normed, pi + 1) if len(NORMS[p]) == 1 else wait(var_ready, n0 + 2)
                if p in NEXT_BIAS:
                    if p == L0_MIX:
                        wait(sel_ready, 1)
                    bias = NEXT_BIAS[p]()
                    g.tensor_tensor(tiles(blk(X, b)), N1[:, :, :], bias.rearrange("p (a b) -> p a b", a=1).to_broadcast([P, NT, P]),
                                    ALU.add).then_inc(x_saved, 1)
                else:
                    g.tensor_copy(blk(X, b), N1[:, :, :].rearrange("p a b -> p (a b)")).then_inc(x_saved, 1)
                if len(NORMS[p]) == 2:
                    rstd(n0 + 1, LN_EPS)

            def post(p, b):
                post_root(p, b)
                post_save(p, b)

            def layer0_pool(b):
                if not is_last(b):
                    if is_first(b):
                        pool.wait_ge(ld_x, 48)
                    shifted(b + 1)
                if not is_first(b):
                    post(L0_MIX, b - 1)
                wait(wkv_ready, b + 1)
                wait(sg_ready, b + 1)
                g.tensor_tensor(KV, KV, SG, ALU.mult).then_inc(gated, 1)
                if not is_first(b):
                    if is_last(b):
                        prep_pool(0, 0)
                    post(L0_LINEAR, b - 1)

            def prep_pool(L, b):
                B = b + NB * L
                c = LAYERS[L]
                rope = c["rope"] is not None
                base = b * PREP_USES[L] + PREP_BASE[L]
                nk = c["kv"] * HD
                for i, (f, parts, n) in enumerate(((QF, PQ, P), (KF, PK, nk))):
                    x = "qk"[i]
                    if rope:
                        wait(prep_evac, base + 2 * i + 2)
                        g.tensor_tensor(f[0:n, :], RA[0:n, i, :], RB[0:n, i, :], ALU.add).then_inc(rotated, 1)
                        pool.drain()
                    else:
                        wait(prep_evac, base + i + 1)
                    wait(cast_done, B * 4 + 1 + CASTS[rope].index(x + "0" if rope else x))
                    g.tensor_tensor(RA[0:n, i, :], f[0:n, :], parts[0:n, 0, :], ALU.subtract).then_inc(rest_ready, 1)
                    wait(cast_done, B * 4 + 1 + CASTS[rope].index(x + "1"))
                    pool.drain()
                    g.tensor_tensor(parts[0:n, 2, :], RA[0:n, i, :], parts[0:n, 1, :], ALU.subtract).then_inc(parts_ready, 1)

            def place_v(L, b, gg):
                c = LAYERS[L]
                n = GH if c["kv"] == H else 1
                wait(prep_evac, (b + 1) * PREP_USES[L] + PREP_BASE[L])
                wait(pv_done, (U(L, b, gg) - 3) * NT)
                g.tensor_copy(VA[:, :, gg * n:(gg + 1) * n, 0:HD],
                              VST[:, :, gg * n * HD:(gg + 1) * n * HD].rearrange("p t (h e) -> p t h e", e=HD)
                              ).then_inc(v_placed, 1)

            def shift(L, b, gg):
                m = M[gg % 2][:, :].rearrange("p (t j) -> p t j", j=GH)
                r = MR[:, :].rearrange("p (t j) -> p t j", j=GH)
                to = MS[gg % 2]
                wait(max_done, item(L, b, gg, NI[L]))
                wait(mt_ready, U(L, b, gg) - 1)
                g.tensor_copy(to[:, :, 0, :], m)
                pool.drain()
                g.tensor_tensor(r, m, to[:, :, 0, :], ALU.subtract)
                pool.drain()
                g.tensor_copy(to[:, :, 1, :], r)
                pool.drain()
                g.tensor_tensor(to[:, :, 2, :], r, to[:, :, 1, :], ALU.subtract).then_inc(m_split, 1)

            def start_pool(L):
                if L:
                    prep_pool(L, 0)
                for gg in range(3):
                    place_v(L, 0, gg)

            def attention_pool(L):
                p = LAYERS[L]["phase"]
                if starts_chain(L):
                    shift(L, 0, 0)
                    shift(L, 0, 1)

                def unit(L, b, gg):
                    prev, follow, ahead, prep, end = neighbours(L, b, gg)
                    if gg == 0:
                        place_v(L, b, 3)
                    if prep:
                        prep_pool(*prep)
                    if gg == 1 and end:
                        post_root(LAYERS[end[0]]["phase"], end[1])
                    if gg == 2 and end:
                        post_save(LAYERS[end[0]]["phase"], end[1])
                    if gg == 2 and ahead:
                        place_v(ahead[0], ahead[1], 0)
                        place_v(ahead[0], ahead[1], 1)
                    if gg == 3 and ahead:
                        place_v(ahead[0], ahead[1], 2)
                    if ahead:
                        shift(*ahead)
                sequence(L, unit, pool.Fori)

            def moe_pool(p):
                def body(b):
                    if p == L1_MOE:
                        wait(gt_evac, b * 2 + 2)
                        wait(y_ready, b + NB * p)
                        g.tensor_copy(RWB[:, :], blk(RW9, b)).then_inc(rwb_ready, 1)
                    else:
                        pool.wait_ge(gw_ready, gate_part(p, int(is_last(b))) + 1)
                        if not is_first(b):
                            wait(summed, b * E)
                        here = GW[:, b * NT:(b + 1) * NT, 0:E] if isinstance(b, int) else GW[:, bass.ds(b * NT, NT), 0:E]
                        g.tensor_copy(gates_here[:, :, :], here).then_inc(gates_placed, 1)
                    if is_first(b):
                        post(LAYERS[BEFORE[p]]["phase"], NB - 1)
                    else:
                        post(p, b - 1)
                for_inner_blocks(pool, body)
                start_pool(AFTER[p])
                post(p, NB - 1)

            for_inner_blocks(pool, layer0_pool)
            post(L0_MIX, NB - 1)
            post(L0_LINEAR, NB - 1)
            start_pool(0)
            attention_pool(0)
            moe_pool(L1_MOE)
            attention_pool(1)
            attention_pool(2)
            moe_pool(L2_MOE)
            attention_pool(3)

            def ffn_root(b):
                wait(fv_ready, b + 1)
                g.tensor_scalar(FVE[:, :], FMS[:, :], LN_EPS, 1.0, ALU.add, ALU.mult)
                pool.drain()
                g.tensor_tensor(FRSTD[:, :], FVE[:, :], neg_half[:, :], ALU.pow).then_inc(fr_ready, 1)

            post_root(L3_ATTN, NB - 1)
            ffn_root(0)
            post_save(L3_ATTN, NB - 1)
            ffn_root(1)
            for b in range(2, NB):
                post_root(LAST, b - 2)
                ffn_root(b)
            post_root(LAST, NB - 2)
            post_root(LAST, NB - 1)

        @block.scalar
        def _(act):
            a = nc.scalar

            def xt_out(p, b):
                act.wait_ge(xt_ready, post_index(p, b) + 1)
                dst = XTS[:, :] if p == L0_MIX else blk(XT, b)
                src = xt_bank(p, b)[:, :]
                if p == L2_ATTN:
                    i = a.activation(dst, src, ACT.Copy, scale=cc("ln1_w"))
                elif p == L2_GQA:
                    i = a.activation(dst, src, ACT.Copy, scale=cc("ln2_w"))
                elif p == L3_ATTN:
                    i = a.activation(dst, src, ACT.Identity, scale=cc("f_ln1_g"), bias=cc("f_ln1_b"))
                else:
                    i = a.activation(dst, src, ACT.Copy)
                i.then_inc(xt_evac, 1)

            act.wait_ge(ld_c, 32)
            a.activation(cols0[:, 1:2], cc("decay"), ACT.Exp)
            act.drain()
            a.activation(cols0[:, 2:3], cols0[:, 1:2], ACT.Exp, scale=-1.0)
            a.activation(cols0[:, 3:4], cc("first"), ACT.Exp).then_inc(c0a, 1)

            def layer0_act(b):
                act.wait_ge(km_ready, b + 1)
                a.activation(KE, KM, ACT.Exp).then_inc(ke_ready, 1)
                at_least(act, rwkv_ready, b)
                a.activation(SG, bank[2][:, :], ACT.Sigmoid).then_inc(sg_ready, 1)
                if is_first(b):
                    act.wait_ge(z2_sem, 1)
                    a.activation(sel0[:, 3, :], sel0[:, 2, :], ACT.Exp, accum_out=sel0[:, 4, 0:1])
                    act.drain()
                    a.activation(sel0[:, 4, 1:2], sel0[:, 4, 0:1], ACT.Ln).then_inc(z_sem, 1)
                    a.activation(sel0[:, 0, :], rc("u"), ACT.Ln)
                    act.drain()
                    a.activation(sel0[:, 1, :], sel0[:, 0, :], ACT.Ln, scale=-1.0).then_inc(z_sem, 1)
                else:
                    xt_out(L0_MIX, b - 1)
                    if is_last(b):
                        for what in ("q", "k", "v", "q1", "k1"):
                            prep_act(0, 0, what)
                    xt_out(L0_LINEAR, b - 1)

            def prep_act(L, b, what):
                c = LAYERS[L]
                B = b + NB * L
                base = b * PREP_USES[L] + PREP_BASE[L]
                nk = c["kv"] * HD
                rope = c["rope"] is not None
                i = 0 if what[0] == "q" else 1
                f, parts, n = ((QF, PQ, P), (KF, PK, nk))[i]
                if what == "xts" and isinstance(b, int):
                    return
                if what == "xts":
                    act.wait_ge(xt_evac, post_index(c["phase"] - 1, b) + 1)
                    at_least(act, proj_ready, base)
                    a.activation(XTS[:, :], blk(XT, b), ACT.Copy).then_inc(xts_ready, 1)
                elif what == "v":
                    if c["alibi"]:
                        return
                    act.wait_ge(proj_ready, base + PREP_USES[L])
                    at_least(act, v_placed, B * NG)
                    a.activation(VST[:, :, 0:nk], tiles(prep_bank(L, b, "v")[:, :])[:, :, 0:nk], ACT.Copy).then_inc(prep_evac, 1)
                elif what in ("q", "k"):
                    act.wait_ge(proj_ready, base + i + 1)
                    at_least(act, parts_ready, B * 2 - 1 + i)
                    at_least(act, parts_stored, B * 96)
                    if c["alibi"]:
                        k = dict(func=ACT.Identity, scale=HD ** -0.5 if i == 0 else 1.0, bias=bqs[:, :] if i == 0 else cc("bk", rows=n))
                    else:
                        k = dict(func=ACT.Copy)
                    a.activation(parts[0:n, 0, :], prep_bank(L, b, what)[0:n, :], **k).then_inc(cast_done, 1)
                    a.activation(f[0:n, :], prep_bank(L, b, what)[0:n, :], **k).then_inc(prep_evac, 1)
                elif what[1] == "0":
                    act.wait_ge(rotated, b * 2 + (NB * 2 * (L - 1) + i + 1))
                    at_least(act, parts_stored, B * 96)
                    a.activation(parts[0:n, 0, :], f[0:n, :], ACT.Copy).then_inc(cast_done, 1)
                else:
                    act.wait_ge(rest_ready, B * 2 + i + 1)
                    a.activation(parts[0:n, 1, :], RA[0:n, i, :], ACT.Copy).then_inc(cast_done, 1)

            def m_out(L, b, g):
                w = U(L, b, g)
                act.wait_ge(mt_ready, w + 1)
                at_least(act, shift_landed[g % 2], half(L, b, g) * 48)
                a.activation(MSB[g % 2][:, :], bank[7][0:PARTS * GH, 0:T // 2].bitcast(BF16), ACT.Copy).then_inc(m_evac, 1)

            def o_out(L, u, g):
                act.wait_ge(pv_done, (u + 1) * NT)
                a.activation(OT[:, :], bank[4][:, :], ACT.Copy).then_inc(o_evac, 1)

            def ao_out(L, b):
                B = b + NB * L
                act.wait_ge(ao_ready, B + 1)
                at_least(act, y_ready, b + NB * LAYERS[L]["phase"])
                a.activation(AOT[:, :], bank[6][:, :], ACT.Copy).then_inc(ao_evac, 1)

            def attention_act(L):
                c = LAYERS[L]
                p = c["phase"]
                places = ACT_PREP
                if starts_chain(L):
                    m_out(L, 0, 0)

                def unit(L, b, g):
                    u = U(L, b, g)
                    prev, follow, ahead, prep, end = neighbours(L, b, g)
                    for i, (kt, js) in enumerate(ST_ITEMS[L]):
                        q0 = q_from(L, kt)
                        w = T - q0
                        act.wait_ge(st_ready, item(L, b, g, i) + 1)
                        at_least(act, pv_done, u * NT + kt - 1)
                        a.activation(PT[kt % 2][:, js[0]:js[-1] + 1, q0:T],
                                     tiles(bank[st_bank(L, g, i)][:, 0:w * len(js)], len(js)), ACT.Exp,
                                     scale=c["scale"]).then_inc(exp_done, 1)
                        if prep:
                            for what in places[LAYERS[prep[0]]["rope"] is not None].get(i, ()):
                                prep_act(*prep, what)
                        if prev and i == O_OUT_AT:
                            o_out(L, u - 1, g - 1)
                        if follow and i == SHIFT_T_AT + 1:
                            m_out(*follow)
                        if end and g == 0 and i == AO_OUT_AT:
                            ao_out(*end)
                        if end and (g, i) == end_at(L, b)["out"]:
                            xt_out(LAYERS[end[0]]["phase"], end[1])
                        if L in GATED_BY and is_last(b) and (g, i) == (2, GATES_AT):
                            gate_exp(GATED_BY[L], 0)
                sequence(L, unit, act.Fori)
                if ends_chain(L):
                    o_out(L, U(L, NB - 1, NG - 1), NG - 1)

            def gate_exp(p, part):
                act.wait_ge(gm_ready, gate_part(p, part) + 1)
                t = gate_tiles(part)
                a.activation(GE[:, t, :], GL[:, t, :], ACT.Exp).then_inc(ge_ready, 1)

            def moe_act(p):
                L = BEFORE[p]
                n = MOE_CHUNKS[p]

                def body(b):
                    k0 = b * n + MOE_BASE[p]
                    for c in range(n):
                        act.wait_ge(ab_ready, k0 + c + 1)
                        at_least(act, u_ready if p == L1_MOE else h_ready, k0 + c + 1 - back(p, c, 2))
                        if p == L1_MOE:
                            a.activation(A1[c % 2], bank[c % 2][:, :], ACT.Identity, bias=cc("m_b1", c)).then_inc(a_evac, 1)
                            act.wait_ge(u_ready, k0 + c + 1)
                            at_least(act, h_ready, k0 + c + 1 - back(p, c, 2))
                            a.activation(S1[c % 2], U1[c % 2], ACT.Silu).then_inc(s1_ready, 1)
                        else:
                            a.activation(A1[c % 2], bank[c % 2][:, :], ACT.Silu).then_inc(a_evac, 1)
                        if is_first(b):
                            if c == 0:
                                ao_out(L, NB - 1)
                            if c == XT_OUT_AT:
                                xt_out(LAYERS[L]["phase"], NB - 1)
                            if c == LATE_GATES_AT:
                                gate_exp(p, 1)
                        elif c == XT_OUT_AT:
                            xt_out(p, b - 1)
                        if is_last(b):
                            for what in ACT_START[p].get(c, ()):
                                prep_act(AFTER[p], 0, what)
                for_inner_blocks(act, body)
                xt_out(p, NB - 1)

            for_inner_blocks(act, layer0_act)
            xt_out(L0_MIX, NB - 1)
            xt_out(L0_LINEAR, NB - 1)
            attention_act(0)
            moe_act(L1_MOE)
            attention_act(1)
            attention_act(2)
            moe_act(L2_MOE)
            attention_act(3)

            def ffn_out(b):
                for c in range(4):
                    act.wait_ge(ft_ready, b * 4 + c + 1)
                    if c == 0:
                        at_least(act, y_ready, b + NB * LAST)
                    a.activation(HT2[:, c, :], bank[4 + c % 2][:, :], ACT.Identity, scale=cc("f_ln2_g", c), bias=cc("f_ln2_b", c)).then_inc(ft_evac, 1)

            for b in range(NB + 1):
                if b == 0:
                    ao_out(3, NB - 1)
                if b < NB:
                    for i in range(NT):
                        act.wait_ge(fb_ready, b * NT + i + 1)
                        a.activation(HG[b % 2][:, i, :], HG[b % 2][:, i, :], ACT.Gelu).then_inc(fg_ready, 1)
                if b == 2:
                    xt_out(L3_ATTN, NB - 1)
                if b > 0:
                    ffn_out(b - 1)

        @block.vector
        def _(dve):
            v = nc.vector

            def stats(src):
                for i in range(NT):
                    v.bn_stats(ST[:, i, :], src[:, i, :])
                dve.drain()
                for i in range(NT):
                    v.bn_aggr(MV[:, i, :], ST[:, i, :])
                dve.drain()

            def norm(kind, src, dst, idx, first):
                stats(src)
                if kind == "ln":
                    v.tensor_copy(MS2[:, :], MV[:, :, 1]).then_inc(var_ready, 1)
                else:
                    v.tensor_tensor(MS2[:, :], MV[:, :, 0], MV[:, :, 0], ALU.mult)
                    dve.drain()
                    v.tensor_tensor(MS2[:, :], MS2[:, :], MV[:, :, 1], ALU.add).then_inc(var_ready, 1)

            def scale(kind, src, dst, idx):
                dve.wait_ge(rstd_ready, idx + 1)
                for i in range(NT):
                    if kind == "ln":
                        r = v.tensor_scalar(dst[:, i, :], src[:, i, :], MV[:, i, 0:1], RSTD[:, i:i + 1], ALU.subtract, ALU.mult)
                    else:
                        r = v.tensor_scalar(dst[:, i, :], src[:, i, :], RSTD[:, i:i + 1], None, ALU.mult)
                return r

            def post_sum(p, b):
                pi = post_index(p, b)
                dve.wait_ge(y_ready, pi + 1)
                before = NB * LAST if p == LAST else pi
                if p != L0_MIX or isinstance(b, int):
                    at_least(dve, x_saved, before)
                    at_least(dve, xt_ready, before)
                if p == LAST:
                    at_least(dve, out_done, b * 16)
                if p == L2_MOE:
                    v.tensor_tensor(YB[:, :, :], routed, tiles(blk(X1, b)), ALU.add).then_inc(y_added, 1)
                    dve.drain()
                    v.tensor_tensor(YB[:, :, :], YB[:, :, :], tiles(blk(X, b)), ALU.add)
                else:
                    v.tensor_tensor(YB[:, :, :], tiles(Y[:, :]), tiles(blk(X, b)), ALU.add).then_inc(y_added, 1)
                dve.drain()

            def post_stats(p, b):
                norm(NORMS[p][0], YB, N1, 0, True)

            def post_norm(p, b):
                n0 = norm_index(p, b)
                if len(NORMS[p]) == 1:
                    scale(NORMS[p][0], YB, N2 if p == L2_GQA else N1, n0).then_inc(normed, 1)
                    return
                scale(NORMS[p][0], YB, N1, n0)
                dve.drain()

            def post_stats2(p, b):
                if len(NORMS[p]) == 2:
                    norm(NORMS[p][1], N1, N2, 1, False)

            def post_norm2(p, b):
                if len(NORMS[p]) == 2:
                    scale(NORMS[p][1], N1, N2, norm_index(p, b) + 1).then_inc(normed, 1)

            def mixed(b):
                xb = XTP[:, b, 1:T + 1] if isinstance(b, int) else XTP[:, bass.ds(b, 1), 1:T + 1].rearrange("p a b -> p (a b)")
                dve.wait_ge(xm0_ready, b + 1)
                v.scalar_tensor_tensor(XM, xb, cc("mix"), XM0, ALU.mult, ALU.add).then_inc(xm_ready, 1)

            dve.wait_ge(ld_c, 32)
            v.tensor_scalar(cols0[:, 0:1], cc("mix"), -1.0, 1.0, ALU.mult, ALU.add).then_inc(c0b, 1)
            dve.drain().then_inc(o_normed, 1)
            mixed(0)
            dve.wait_ge(ld_0, 32)
            v.tensor_reduce(sel0[:, 4, 2:3], rc("logits"), AX_X, ALU.max)
            dve.drain()
            v.tensor_scalar(sel0[:, 2, :], rc("logits"), sel0[:, 4, 2:3], None, ALU.subtract).then_inc(z2_sem, 1)

            def pick():
                dve.wait_ge(z_sem, 2)
                v.tensor_scalar(sel0[:, 5, :], sel0[:, 2, :], sel0[:, 4, 1:2], None, ALU.subtract)
                dve.drain()
                v.tensor_tensor(sel0[:, 6, :], sel0[:, 5, :], sel0[:, 1, :], ALU.subtract)
                dve.drain()
                v.tensor_reduce(sel0[:, 4, 3:4], sel0[:, 6, :], AX_X, ALU.max)
                dve.drain()
                dve.wait_ge(pool_const, 2)
                v.scalar_tensor_tensor(sel0[:, 7, :], sel0[:, 6, :], sel0[:, 4, 3:4], rev[:, :], ALU.is_ge, ALU.mult)
                dve.drain()
                v.tensor_reduce(sel0[:, 4, 4:5], sel0[:, 7, :], AX_X, ALU.max)
                dve.drain()
                v.tensor_scalar(sel0[:, 8, :], sel0[:, 7, :], sel0[:, 4, 4:5], None, ALU.is_equal)
                dve.drain()
                for i in range(E):
                    b0 = rc("l0_b")[:, i * P:(i + 1) * P]
                    if i == 0:
                        v.tensor_scalar(WSEL[:, :], W0[:, 0, :], sel0[:, 8, 0:1], None, ALU.mult)
                        r = v.tensor_scalar(BSEL[:, :], b0, sel0[:, 8, 0:1], None, ALU.mult)
                    else:
                        v.scalar_tensor_tensor(WSEL[:, :], W0[:, i, :], sel0[:, 8, i:i + 1], WSEL[:, :], ALU.mult, ALU.add)
                        r = v.scalar_tensor_tensor(BSEL[:, :], b0, sel0[:, 8, i:i + 1], BSEL[:, :], ALU.mult, ALU.add)
                    if i == E - 1:
                        r.then_inc(sel_ready, 1)
                    dve.drain()

            def layer0_dve(b):
                dve.wait_ge(kvr_ready, b + 1)
                v.tensor_scalar(KM, bank[0][:, :], 60.0, None, ALU.min).then_inc(km_ready, 1)
                if is_first(b):
                    dve.wait_ge(c0a, 1)
                else:
                    post_sum(L0_MIX, b - 1)
                    post_stats(L0_MIX, b - 1)
                dve.wait_ge(ke_ready, b + 1)
                v.tensor_tensor(KV, KE, bank[1][:, :], ALU.mult).then_inc(kv_ready, 1)
                dve.drain()
                for i, src in enumerate((KV, KE)):
                    v.tensor_tensor_scan(SA[:, i, 1:T + 1], cols0[:, 2:3].to_broadcast([P, T]), src, 0.0, ALU.mult, ALU.add)
                if is_first(b):
                    dve.wait_ge(ld_x, 48)
                if not is_last(b):
                    mixed(b + 1)
                if not is_first(b):
                    post_norm(L0_MIX, b - 1)
                    post_stats2(L0_MIX, b - 1)
                dve.drain()
                v.scalar_tensor_tensor(KV, KV, cols0[:, 3:4], SA[:, 0, 0:T], ALU.mult, ALU.add).then_inc(wkv_ready, 1)
                v.scalar_tensor_tensor(KE, KE, cols0[:, 3:4], SA[:, 1, 0:T], ALU.mult, ALU.add)
                dve.drain()
                v.tensor_scalar(KE, KE, 1e-9, None, ALU.add)
                dve.drain()
                v.reciprocal(KE, KE)
                if not is_first(b):
                    post_sum(L0_LINEAR, b - 1)
                    post_stats(L0_LINEAR, b - 1)
                dve.drain()
                dve.wait_ge(gated, b + 1)
                v.tensor_tensor(RWKV, KV, KE, ALU.mult).then_inc(rwkv_ready, 1)
                if is_first(b):
                    pick()
                else:
                    post_norm(L0_LINEAR, b - 1)
                    post_stats2(L0_LINEAR, b - 1)
            for_inner_blocks(dve, layer0_dve)
            post_sum(L0_MIX, NB - 1)
            post_stats(L0_MIX, NB - 1)

            def prep_dve(L, b, i):
                c = LAYERS[L]
                B = b + NB * L
                base = b * PREP_USES[L] + PREP_BASE[L]
                what = prep_uses(L)[i]
                nk = c["kv"] * HD
                if what == "v":
                    if c["alibi"]:
                        dve.wait_ge(proj_ready, base + i + 1)
                        at_least(dve, v_placed, B * NG)
                        v.tensor_tensor(VST[:, :, 0:nk], tiles(prep_bank(L, b, "v")[:, :])[:, :, 0:nk],
                                        rc("bv").rearrange("p (a b) -> p a b", a=1).to_broadcast([P, NT, nk]), ALU.add).then_inc(prep_evac, 1)
                elif c["rope"] is not None:
                    n, k = (P, 0) if what[0] == "q" else (nk, 1)
                    sw = len(what) == 2
                    dve.wait_ge(proj_ready, base + i + 1)
                    at_least(dve, parts_ready, B * 2 - 1 + k)
                    v.tensor_tensor((RB if sw else RA)[0:n, k, :], prep_bank(L, b, what)[0:n, :], tables[0:n, c["rope"], int(sw), :],
                                    ALU.mult).then_inc(prep_evac, 1)

            def reduce(L, b, g, i):
                t, js = S_ITEMS[L][i]
                kl = k_to(L, t)
                dve.wait_ge(s_ready, item(L, b, g, i) + 1)
                if i == 0:
                    at_least(dve, m_split, U(L, b, g) - 1)
                v.tensor_reduce(M[g % 2][:, t * GH + js[0]:t * GH + js[-1] + 1], tiles(bank[S_ORDER[L][i]][:, 0:kl * len(js)], len(js)),
                                AX_X, ALU.max, negate=True).then_inc(max_done, 1)

            def o_norm(L, b, g, u):
                dve.wait_ge(ot_ready, u + 1)
                o = bank[7][:, :].rearrange("p (t j e) -> p t j e", t=NT, j=GH)
                r = OR[:, :].rearrange("p (t j e) -> p t j e", t=NT, j=GH)
                v.reciprocal(r, o[:, :, :, HD:HD + 1])
                dve.drain()
                v.tensor_tensor(AO[:, :, g * 32:(g + 1) * 32].rearrange("p t (j e) -> p t j e", j=GH), o[:, :, :, 0:HD],
                                r.to_broadcast([P, NT, GH, HD]), ALU.mult).then_inc(o_normed, 1)

            def attention_dve(L):
                c = LAYERS[L]
                p = c["phase"]
                if starts_chain(L):
                    for g in range(2):
                        for i in range(NI[L]):
                            reduce(L, 0, g, i)
                            if g == 0 and i == NORM_BESIDE:
                                post_norm(L0_MIX if L == 0 else p - 1, NB - 1)
                                post_stats2(L0_MIX if L == 0 else p - 1, NB - 1)
                            if g == 0 and L == 0 and i == LINEAR_SUM_BESIDE:
                                post_sum(L0_LINEAR, NB - 1)
                                post_stats(L0_LINEAR, NB - 1)
                            if g == 0 and L == 0 and i == LINEAR_NORM_BESIDE:
                                post_norm(L0_LINEAR, NB - 1)
                                post_stats2(L0_LINEAR, NB - 1)

                def unit(L, b, g):
                    u = U(L, b, g)
                    prev, follow, ahead, prep, end = neighbours(L, b, g)
                    for i in range(NI[L]):
                        if ahead and i < NI[ahead[0]]:
                            reduce(*ahead, i)
                        if prep:
                            at = DVE_PREP[LAYERS[prep[0]]["rope"] is not None]
                            if i in at:
                                prep_dve(*prep, at[i])
                        if prev and i == O_NORM_AT:
                            o_norm(*prev, u - 1)
                        if end and (g, i) == Y_SUM_AT:
                            post_sum(LAYERS[end[0]]["phase"], end[1])
                        if end and (g, i) == Y_STATS_AT:
                            post_stats(LAYERS[end[0]]["phase"], end[1])
                        if end and (g, i) == end_at(L, b)["norm"]:
                            post_norm(LAYERS[end[0]]["phase"], end[1])
                        if end and (g, i) == end_at(L, b)["stats2"]:
                            post_stats2(LAYERS[end[0]]["phase"], end[1])
                        if end and (g, i) == end_at(L, b)["norm2"]:
                            post_norm2(LAYERS[end[0]]["phase"], end[1])
                        if L == 3 and is_last(b) and (g, i) == TERNARY_ABS_AT:
                            ternary_sums()
                        if L == 3 and is_last(b) and (g, i) == TERNARY_AT:
                            ternary()
                        if L == 0 and is_last(b) and (g, i) == SLOPES_AT:
                            slopes()
                        if L in GATED_BY and is_last(b):
                            if (g, i) == (2, GATES_AT):
                                gates(GATED_BY[L], 0)
                            if GATED_BY[L] == L1_MOE and g == 3 and i in GATES_T_AT:
                                gates_out(GATED_BY[L], GATES_T_AT[i], bank[0])
                                gates_out(GATED_BY[L], GATES_T_AT[i], bank[1], True)
                sequence(L, unit, dve.Fori)
                if ends_chain(L):
                    o_norm(L, NB - 1, NG - 1, U(L, NB - 1, NG - 1))

            def top(src, onehot, tmp, mx):
                n = src.shape[1]
                bc = lambda t: t.rearrange("p (a b) -> p a b", b=1).to_broadcast([P, n, E])
                v.tensor_reduce(mx, src, AX_X, ALU.max)
                dve.drain()
                v.tensor_tensor(tmp, src, bc(mx), ALU.is_ge)
                dve.drain()
                v.tensor_tensor(tmp, tmp, rev[:, :].rearrange("p (a b) -> p a b", a=1).to_broadcast([P, n, E]), ALU.mult)
                dve.drain()
                v.tensor_reduce(mx, tmp, AX_X, ALU.max)
                dve.drain()
                v.tensor_tensor(onehot, tmp, bc(mx), ALU.is_equal)
                dve.drain()

            def gates(p, part, steps=range(3)):
                t = gate_tiles(part)
                n = t.stop - t.start
                bc = lambda x: x.rearrange("p (a b) -> p a b", b=1).to_broadcast([P, n, E])
                mx, ge, gb, go, gl, gr, gw, gwr = GM[:, t], GE[:, t, :], GB[:, t, :], GO[:, t, :], GL[:, t, :], GR[:, t, :], GW[:, t, :], GWR[:, t, :]
                parts = GWP[:, t, :, :]
                if 0 in steps:
                    dve.wait_ge(lg_ready, gate_part(p, part) + 1)
                    lg = bank[7 if part else 5][:, 0:n * E].rearrange("p (a b) -> p a b", b=E)
                    v.tensor_reduce(mx, lg, AX_X, ALU.max)
                    dve.drain()
                    v.tensor_tensor(gl, lg, bc(mx), ALU.subtract).then_inc(gm_ready, 1)
                if 1 in steps:
                    dve.wait_ge(ge_ready, gate_part(p, part) + 1)
                    v.tensor_reduce(mx, ge, AX_X, ALU.add)
                    dve.drain()
                    v.reciprocal(mx, mx)
                    dve.drain()
                    v.tensor_tensor(ge, ge, bc(mx), ALU.mult)
                    dve.drain()
                    if p == L1_MOE:
                        v.tensor_tensor(gb, ge, rc("gate_b").rearrange("p (a b) -> p a b", a=1).to_broadcast([P, n, E]), ALU.add)
                    else:
                        v.tensor_copy(gb, ge)
                    dve.drain()
                    top(gb, go, gr, mx)
                if 2 in steps:
                    v.scalar_tensor_tensor(gb, go, MASKED, gb, ALU.mult, ALU.add)
                    dve.drain()
                    top(gb, gl, gr, mx)
                    v.tensor_tensor(go, go, gl, ALU.add)
                    dve.drain()
                    w = GW[:, t, 0:E]
                    if p == L1_MOE:
                        v.memset(GW[:, t, E:NGATE], 1.0)
                    v.tensor_tensor(w, ge, go, ALU.mult)
                    dve.drain()
                    if p == L2_MOE:
                        v.tensor_reduce(mx, w, AX_X, ALU.add)
                        dve.drain()
                        v.reciprocal(mx, mx)
                        dve.drain()
                        v.tensor_tensor(w, w, bc(mx), ALU.mult).then_inc(gw_ready, 1)
                        return
                    v.tensor_copy(parts[:, :, 0, :], gw)
                    dve.drain()
                    v.tensor_tensor(gwr, gw, parts[:, :, 0, :], ALU.subtract)
                    dve.drain()
                    v.tensor_copy(parts[:, :, 1, :], gwr)
                    dve.drain()
                    v.tensor_tensor(parts[:, :, 2, :], gwr, parts[:, :, 1, :], ALU.subtract).then_inc(gw_ready, 1)

            def gates_out(p, b, src, parts=False):
                gi = 0 if p == L1_MOE else 1
                dve.wait_ge(gt_ready, (gi * NB + b) * 2 + (2 if parts else 1))
                if parts:
                    v.tensor_copy(blk(RWT, b)[0:PARTS * NGATE, :], src[0:PARTS * NGATE, 0:T // 2].bitcast(BF16)).then_inc(gt_evac, 1)
                else:
                    v.tensor_copy(blk(RW9, b), src[0:NGATE, :]).then_inc(gt_evac, 1)

            def add_expert(b, e):
                if e == 0:
                    dve.wait_ge(gates_placed, b + 1)
                dve.wait_ge(yc_done, b * MOE_CHUNKS[L2_MOE] + (MOE_BASE[L2_MOE] + 2 * e + 2))
                for i in range(NT):
                    y, gate = bank[4 + e % 2][:, i * P:(i + 1) * P], gates_here[:, i, e:e + 1]
                    if e == 0:
                        k = v.tensor_scalar(routed[:, i, :], y, gate, None, ALU.mult)
                    else:
                        k = v.scalar_tensor_tensor(routed[:, i, :], y, gate, routed[:, i, :], ALU.mult, ALU.add)
                k.then_inc(summed, 1)
                dve.drain()

            def moe_dve(p):
                n = MOE_CHUNKS[p]
                before = LAYERS[BEFORE[p]]["phase"]

                def body(b):
                    k0 = b * n + MOE_BASE[p]
                    first = isinstance(b, int) and b == 0
                    for c in range(n):
                        dve.wait_ge(a_evac, k0 + c + 1)
                        if p == L1_MOE:
                            at_least(dve, s1_ready, b * n + c + 1 - back(p, c, 2))
                            v.scalar_tensor_tensor(U1[c % 2], bank[2 + c % 2][:, :], cc("m_b3", c), A1[c % 2], ALU.add, ALU.mult).then_inc(u_ready, 1)
                            dve.wait_ge(s1_ready, b * n + c + 1)
                        at_least(dve, yc_done, k0 + c + 1 - back(p, c, NH1[p]))
                        if p == L1_MOE:
                            v.tensor_tensor(H1[c % NH1[p]], bank[4 + c % 2][:, :], S1[c % 2], ALU.mult).then_inc(h_ready, 1)
                        else:
                            v.tensor_tensor(H1[c % NH1[p]], bank[2 + c % 2][:, :], A1[c % 2], ALU.mult).then_inc(h_ready, 1)
                            if c >= 4 and c % 2 == 0:
                                add_expert(b, c // 2 - 2)
                            elif c in (0, 2) and not first:
                                add_expert(b - 1, E - 2 + c // 2)
                        end = (before, NB - 1) if first else (p, b - 1)
                        if c == SUM_AT[p]:
                            post_sum(*end)
                            post_stats(*end)
                        if c == NORM_AT:
                            post_norm(*end)
                            post_stats2(*end)
                        if c == NORM_AT + 1:
                            post_norm2(*end)
                        if first and LATE_GATES_AT <= c < LATE_GATES_AT + 3:
                            gates(p, 1, [c - LATE_GATES_AT])
                        if p == L1_MOE and first and c in (LATE_T_AT, LATE_T_AT + 1):
                            gates_out(p, NB - 1, bank[7], c > LATE_T_AT)
                        if is_last(b) and c in DVE_START[p]:
                            prep_dve(AFTER[p], 0, DVE_START[p][c])
                for_inner_blocks(dve, body)
                if p == L2_MOE:
                    add_expert(NB - 1, E - 2)
                    add_expert(NB - 1, E - 1)
                post_sum(p, NB - 1)
                post_stats(p, NB - 1)

            def ternary_sums():
                dve.wait_ge(ld_f, 48)
                w2 = FW2[:, :, :].rearrange("p a b -> p (a b)")
                v.tensor_reduce(qa[:, 0, 0:1], FW1[:, :], AX_X, ALU.add, apply_absolute_value=True)
                v.tensor_reduce(qa[:, 0, 1:2], w2, AX_X, ALU.add, apply_absolute_value=True).then_inc(qs_ready, 1)

            def ternary():
                w2 = FW2[:, :, :].rearrange("p a b -> p (a b)")
                dve.wait_ge(qm_ready, 1)
                v.tensor_scalar(qa[:, 0, 2:4], bank[5][:, 0:2], 1.0 / (T * P), 1e-5, ALU.mult, ALU.max).then_inc(qm_used, 1)
                dve.drain()
                v.reciprocal(qa[:, 0, 4:6], qa[:, 0, 2:4])
                dve.drain()
                v.reciprocal(qa[:, 0, 6:8], qa[:, 0, 4:6])
                dve.drain()
                for i, w in enumerate((FW1[:, :], w2)):
                    v.tensor_scalar(qt0[:, :], w, qa[:, 0, 4 + i:5 + i], 12582912.0, ALU.mult, ALU.add)
                    dve.drain()
                    v.tensor_scalar(qt0[:, :], qt0[:, :], 12582912.0, 1.0, ALU.subtract, ALU.min)
                    dve.drain()
                    v.tensor_scalar(qt0[:, :], qt0[:, :], -1.0, qa[:, 0, 6 + i:7 + i], ALU.max, ALU.mult)
                    dve.drain()
                    v.tensor_tensor(qt0[:, :], qt0[:, :], w, ALU.subtract)
                    dve.drain()
                    r = v.tensor_tensor(w, w, qt0[:, :], ALU.add)
                    if i:
                        r.then_inc(tern_ready, 1)
                    dve.drain()
            def slopes():
                dve.wait_ge(ld_f, 48)
                v.tensor_scalar(bqs[:, :], cc("bq"), HD ** -0.5, None, ALU.mult)
                v.tensor_copy(slope_p[:, 0:1], slope[:, :])
                dve.drain()
                v.tensor_tensor(slope_r[:, :], slope[:, :], slope_p[:, 0:1], ALU.subtract)
                dve.drain()
                v.tensor_copy(slope_p[:, 1:2], slope_r[:, :])
                dve.drain()
                v.tensor_tensor(slope_p[:, 2:3], slope_r[:, :], slope_p[:, 1:2], ALU.subtract)
                dve.drain()
                v.tensor_copy(slope_w[:, :, :], slope_p[:, :].rearrange("p (a b) -> p a b", b=1).to_broadcast([H, PARTS, T])).then_inc(slope_ready, 1)

            attention_dve(0)
            moe_dve(L1_MOE)
            attention_dve(1)
            attention_dve(2)
            moe_dve(L2_MOE)
            attention_dve(3)

            def ffn_bias(b):
                at_least(dve, ft_ready, (b - 1) * 4)
                for i in range(NT):
                    dve.wait_ge(fu_ready, b * NT + i + 1)
                    v.tensor_tensor(HG[b % 2][:, i, :], bank[i][:, :], rc("f_b1"), ALU.add).then_inc(fb_ready, 1)

            def ffn_stats(b):
                for i in range(NT):
                    dve.wait_ge(fg_ready, b * NT + i + 1)
                    v.bn_stats(FST[:, i, :], HG[b % 2][:, i, :])
                dve.drain()
                for i in range(NT):
                    v.bn_aggr(FMV[:, i, :], FST[:, i, :])
                dve.drain()
                v.tensor_copy(FMS[:, :], FMV[:, :, 1]).then_inc(fv_ready, 1)

            def ffn_norm(b):
                dve.wait_ge(fr_ready, b + 1)
                for i in range(NT):
                    r = v.tensor_scalar(HG[b % 2][:, i, :], HG[b % 2][:, i, :], FMV[:, i, 0:1], FRSTD[:, i:i + 1], ALU.subtract, ALU.mult)
                r.then_inc(fn_ready, 1)

            for b in range(NB + 1):
                if b > 0:
                    ffn_norm(b - 1)
                if b < NB:
                    ffn_bias(b)
                if b == 0:
                    post_sum(L3_ATTN, NB - 1)
                    post_stats(L3_ATTN, NB - 1)
                elif b == 1:
                    post_norm(L3_ATTN, NB - 1)
                    post_stats2(L3_ATTN, NB - 1)
                else:
                    post_sum(LAST, b - 2)
                    post_stats(LAST, b - 2)
                if b < NB:
                    ffn_stats(b)
                if b == 1:
                    post_norm2(L3_ATTN, NB - 1)
                elif b > 1:
                    post_norm(LAST, b - 2)
            post_sum(LAST, NB - 1)
            post_stats(LAST, NB - 1)
            post_norm(LAST, NB - 1)

        @block.tensor
        def _(pe):
            mm = nc.tensor.matmul
            tr = nc.tensor.transpose

            def xt(p, b, to):
                src = N2 if p in (L2_ATTN, L2_GQA, L3_ATTN) else N1
                pe.wait_ge(normed, post_index(p, b) + 1)
                if p == L0_MIX and not isinstance(b, int):
                    pe.wait_ge(ke_ready, b + 2)
                else:
                    at_least(pe, xt_evac, post_index(p, b))
                for i in range(NT):
                    r = tr(to[:, i * P:(i + 1) * P], src[:, i, :], ident[:, :])
                r.then_inc(xt_ready, 1)

            def y_out(lhs, w, b, p):
                for i in range(NT):
                    r = mm(Y[:, i * P:(i + 1) * P], lhs[:, i * P:(i + 1) * P], w, start=True, stop=True)
                r.then_inc(y_ready, 1)

            pe.wait_ge(ld_w0, 16)
            pe.wait_ge(ld_c, 32)

            def kvr(b):
                pe.wait_ge(xm_ready, b + 1)
                at_least(pe, kv_ready, b)
                at_least(pe, sg_ready, b)
                for i, n in enumerate(("l0_k", "l0_v", "l0_r")):
                    r = mm(bank[i][:, :], wc(n), XM, start=True, stop=True)
                r.then_inc(kvr_ready, 1)

            def mix_y(b):
                pe.wait_ge(rwkv_ready, b + 1)
                y_out(RWKV, wc("l0_o"), b, L0_MIX)

            def linear_y(b):
                pe.wait_ge(xt_evac, b * 2 + 1)
                pe.wait_ge(sel_ready, 1)
                y_out(XTS, WSEL[:, :], b, L0_LINEAR)

            def layer0_pe(b):
                if not is_first(b):
                    mix_y(b - 1)
                    xt(L0_MIX, b - 1, bank[7])
                    linear_y(b - 1)
                if not is_last(b):
                    kvr(b + 1)
                else:
                    pe.wait_ge(ld_w, 16)
                    pe.wait_ge(ld_1, LD_1)
                    for i in range(PREP_USES[0]):
                        prep_pe(0, 0, i)
                if not is_first(b):
                    xt(L0_LINEAR, b - 1, bank[7])
            def prep_pe(L, b, i):
                c = LAYERS[L]
                B = b + NB * L
                base = b * PREP_USES[L] + PREP_BASE[L]
                what = prep_uses(L)[i]
                if prep_bank(L, b, what) in bank[6:]:
                    at_least(pe, prep_evac, base + i)
                if i == 0:
                    if prep_bank(L, b, what) is bank[7]:
                        pe.wait_ge(xt_evac, NB * c["phase"] - 2)
                    elif prep_bank(L, b, what) is bank[6]:
                        pe.wait_ge(xt_evac, b + NB * c["phase"] - 2)
                    else:
                        pe.wait_ge(xt_evac, post_index(L0_LINEAR, 0) + 1)
                w = attn_weights(L)[("q", "qs", "k", "ks", "v").index(what)]
                n = w.shape[1]
                if what == "v":
                    x = blk(XT, b) if isinstance(b, int) else XTS[:, :]
                    if not isinstance(b, int):
                        pe.wait_ge(xts_ready, b + (2 * L - 1))
                    for t in range(NT):
                        r = mm(prep_bank(L, b, what)[:, t * P:t * P + n], x[:, t * P:(t + 1) * P], w, start=True, stop=True)
                else:
                    if not isinstance(b, int) and n < P:
                        pe.sem_inc(pe_passed, 1)
                    r = mm(prep_bank(L, b, what)[0:n, :], w, blk(XT, b), start=True, stop=True)
                r.then_inc(proj_ready, 1)

            def score(L, b, g, i):
                t, js = S_ITEMS[L][i]
                causal = LAYERS[L]["causal"]
                kl = k_to(L, t)
                if i == 0:
                    pe.wait_ge(stack_landed[g], (b + NB * L + 1) * 32)
                    if LAYERS[L]["alibi"]:
                        pe.wait_ge(alibi_rows, 7 * 16)
                at_least(pe, max_done, item(L, b, g, i) + 1 - s_back(L, i))
                for n, j in enumerate(js):
                    s = bank[S_ORDER[L][i]][:, n * kl:(n + 1) * kl]
                    r = mm(s, QS[0:ROWS_SHIFT, g * GH + j, t * P:(t + 1) * P], KS[0:ROWS_SHIFT, kv_slot(L, g, j), 0:kl],
                           start=True, stop=not causal)
                    if causal:
                        r = mm(s[:, kl - P:kl], identb[:, :], maskb[:, :], start=False, stop=True)
                r.then_inc(s_ready, 1)

            def score_t(L, b, g, i):
                kt, js = ST_ITEMS[L][i]
                causal = LAYERS[L]["causal"]
                w = T - q_from(L, kt)
                if i == 0:
                    pe.wait_ge(shift_landed[g % 2], (half(L, b, g) + 1) * 48)
                at_least(pe, exp_done, item(L, b, g, i) - 1)
                for n, j in enumerate(js):
                    s = bank[st_bank(L, g, i)][:, n * w:(n + 1) * w]
                    r = mm(s, KS[:, kv_slot(L, g, j), kt * P:(kt + 1) * P], QS[:, g * GH + j, T - w:T], start=True, stop=not causal)
                    if causal:
                        r = mm(s[:, 0:P], maskb[:, :], identb[:, :], start=False, stop=True)
                r.then_inc(st_ready, 1)

            def values(L, b, g, kt):
                u = U(L, b, g)
                q0 = q_from(L, kt)
                if kt == 0:
                    at_least(pe, o_evac, u)
                    pe.wait_ge(v_placed, u + 1)
                pe.wait_ge(exp_done, item(L, b, g, kt_end(L, kt)))
                for j in range(GH):
                    r = mm(bank[4][32 * j:32 * (j + 1), q0:T], VA[:, kt, kv_slot(L, g, j), :], PT[kt % 2][:, j, q0:T],
                           start=(kt == 0), stop=(kt == NT - 1))
                r.then_inc(pv_done, 1)

            def shift_t(L, b, g):
                w = U(L, b, g)
                pe.wait_ge(m_split, w + 1)
                pe.wait_ge(o_normed, w - 1) if not isinstance(w, int) or w > 1 else None
                to = bank[7][0:PARTS * GH, 0:T // 2].bitcast(BF16)
                for t in range(NT):
                    r = tr(to[:, t * P:(t + 1) * P], MS[g % 2][:, t, :, :].rearrange("p a b -> p (a b)"), identb[:, :])
                r.then_inc(mt_ready, 1)

            def o_t(L, u, shifts, last=False):
                pe.wait_ge(o_evac, u + 1)
                pe.wait_ge(m_evac, shifts)
                if last:
                    pe.wait_ge(o_normed, u + 1)
                for t in range(NT):
                    r = tr(bank[7][:, t * P:(t + 1) * P], OT[:, t * P:(t + 1) * P], ident[:, :])
                r.then_inc(ot_ready, 1)

            def ao_t(L, b, preps):
                pe.wait_ge(o_normed, U(L, b, NG - 1) + 2)
                at_least(pe, prep_evac, preps)
                for t in range(NT):
                    r = tr(bank[6][:, t * P:(t + 1) * P], AO[:, t, :], ident[:, :])
                r.then_inc(ao_ready, 1)

            def attention_pe(L):
                c = LAYERS[L]
                p = c["phase"]
                if starts_chain(L):
                    if L == 0:
                        pe.wait_ge(pool_const, 3)
                        pe.wait_ge(kv_ready, NB)
                        pe.wait_ge(sg_ready, NB)
                    pe.wait_ge(prep_evac, PREP_BASE[L] + PREP_USES[L])
                    for g in range(2):
                        for i in range(NI[L]):
                            if L == 3 and (g, S_ORDER[L][i]) == (0, 5):
                                pe.wait_ge(summed, NB * E)
                            score(L, 0, g, i)
                            if g == 1 and i == SHIFT_BESIDE[L]:
                                pe.wait_ge(xt_evac, NB * p)
                                shift_t(L, 0, 0)
                            if g == 0 and i == XT_BESIDE:
                                xt(L0_MIX if L == 0 else p - 1, NB - 1, bank[7])
                            if g == 0 and L == 0 and i == LINEAR_BESIDE:
                                linear_y(NB - 1)
                            if g == 0 and L == 0 and i == LINEAR_XT_BESIDE:
                                xt(L0_LINEAR, NB - 1, bank[7])

                def unit(L, b, g):
                    u = U(L, b, g)
                    prev, follow, ahead, prep, end = neighbours(L, b, g)
                    for i in range(NI[L]):
                        score_t(L, b, g, i)
                        if ahead:
                            score(*ahead, i)
                        if prep:
                            at = PE_PREP[LAYERS[prep[0]]["rope"] is not None]
                            if i in at:
                                prep_pe(*prep, at[i])
                        if prev and i == 1:
                            values(*prev, NT - 1)
                        for kt in range(NT - 1):
                            if i == min(kt_end(L, kt) + 1, NI[L] - 1):
                                values(L, b, g, kt)
                        if follow and i == SHIFT_T_AT:
                            shift_t(*follow)
                        if prev and i == O_T_AT:
                            o_t(L, u - 1, u + 2 if follow else u + 1, not follow)
                        if end and g == 0 and i == AO_T_AT:
                            ao_t(*end, PREP_BASE[prep[0]] + (prep[1] + 1) * PREP_USES[prep[0]] if prep else PREP_BASE[L] + NB * PREP_USES[L])
                        if end and (g, i) == Y_AT:
                            pe.wait_ge(ao_evac, end[1] + NB * end[0] + 1)
                            y_out(AOT, attn_weights(end[0])[5], end[1], LAYERS[end[0]]["phase"])
                        if end and (g, i) == end_at(L, b)["xt"]:
                            xt(LAYERS[end[0]]["phase"], end[1], bank[6])
                        if L == 3 and is_last(b) and (g, i) == TERNARY_SUM_AT:
                            pe.wait_ge(qs_ready, 1)
                            pe.wait_ge(max_done, ITEM_BASE[L] + NB * NG * NI[L])
                            mm(bank[5][:, 0:2], ones[:, :], qa[:, 0, 0:2], start=True, stop=True).then_inc(qm_ready, 1)
                        if L in GATED_BY and is_last(b):
                            if g == 2 and i in LOGITS_AT:
                                logits(GATED_BY[L], LOGITS_AT[i], bank[5])
                            if GATED_BY[L] == L1_MOE and g == 3 and i in GATES_T_AT:
                                gates_t(GATED_BY[L], GATES_T_AT[i], bank[0])
                                gates_t(GATED_BY[L], GATES_T_AT[i], bank[1], True)
                sequence(L, unit, pe.Fori)
                if ends_chain(L):
                    values(L, NB - 1, NG - 1, NT - 1)
                    o_t(L, U(L, NB - 1, NG - 1), U(L, NB - 1, NG - 1) + 1, True)

            def last_ao(L):
                ao_t(L, NB - 1, NB * PREP_USES[L] + PREP_BASE[L])

            def last_y(L):
                pe.wait_ge(ao_evac, NB * L + NB)
                y_out(AOT, attn_weights(L)[5], NB - 1, LAYERS[L]["phase"])

            def scored(L):
                pe.wait_ge(exp_done, ITEM_BASE[L] + NB * NG * NI[L])
                pe.wait_ge(max_done, ITEM_BASE[L] + NB * NG * NI[L])

            def logits(p, b, to):
                pe.wait_ge(xt_evac, NB * (p - 1) + b + 1)
                first = 0 if b < GATED_FIRST else b
                if b == 0:
                    pe.wait_ge(max_done, ITEM_BASE[BEFORE[p]] + NB * NG * NI[BEFORE[p]])
                for i in range(b * NT, (b + 1) * NT):
                    at = (i - first * NT) * E
                    r = mm(to[:, at:at + E], XT[:, i * P:(i + 1) * P], wc("l1_gate" if p == L1_MOE else "l2_gate"), start=True, stop=True)
                if b >= GATED_FIRST - 1:
                    r.then_inc(lg_ready, 1)

            def gates_t(p, b, to, parts=False):
                pe.wait_ge(gw_ready, gate_part(p, b // GATED_FIRST) + 1)
                if b < GATED_FIRST:
                    at_least(pe, gt_evac, b * 2 - (0 if parts else 1))
                elif parts:
                    pe.wait_ge(gt_evac, b * 2 + 1)
                for i in range(NT):
                    if parts:
                        r = tr(to[0:PARTS * NGATE, 0:T // 2].bitcast(BF16)[:, i * P:(i + 1) * P],
                               GWP[:, b * NT + i, :, :].rearrange("p a b -> p (a b)"), identb[:, :])
                    else:
                        r = tr(to[0:NGATE, i * P:(i + 1) * P], GW[:, b * NT + i, :], ident[:, :])
                r.then_inc(gt_ready, 1)

            def moe_pe(p):
                L = BEFORE[p]
                n = MOE_CHUNKS[p]
                scored(L)
                pe.wait_ge(ld_m1 if p == L1_MOE else ld_m2, 80 if p == L1_MOE else 48)
                pe.wait_ge(pool_const, 3)
                if p == L1_MOE:
                    pe.wait_ge(gt_evac, GATED_FIRST * 2)
                else:
                    pe.wait_ge(gw_ready, gate_part(p, 0) + 1)

                def up(b, c):
                    k0 = b * n + MOE_BASE[p]
                    if p == L1_MOE:
                        at_least(pe, u_ready, k0 + c + 1 - back(p, c, 2))
                    at_least(pe, h_ready, k0 + c + 1 - back(p, c, 2))
                    mm(bank[c % 2][:, :], MW1[:, c * P:(c + 1) * P], blk(XT, b), start=True, stop=True)
                    r = mm(bank[2 + c % 2][:, :], MW3[:, c * P:(c + 1) * P], blk(XT, b), start=True, stop=True)
                    if p == L1_MOE:
                        if c == 0 and is_last(b):
                            pe.wait_ge(gt_evac, NB * 2)
                        r = mm(bank[4 + c % 2][:, :], SEL[:, c, :], blk(RWT, b), start=True, stop=True)
                    r.then_inc(ab_ready, 1)

                def down(b, c):
                    k = b * n + MOE_BASE[p] + c
                    if p == L1_MOE and c == 0:
                        at_least(pe, y_added, b + NB * p)
                    if p == L2_MOE and c % 2 == 0:
                        at_least(pe, summed, b * E + (c // 2 - 1))
                    pe.wait_ge(h_ready, k + 1)
                    to = Y if p == L1_MOE else bank[4 + c // 2 % 2]
                    starts, stops = (c == 0, False) if p == L1_MOE else (c % 2 == 0, c % 2 == 1)
                    for i in range(NT):
                        r = mm(to[:, i * P:(i + 1) * P], H1[c % NH1[p]][:, i * P:(i + 1) * P], MW2[:, c, :], start=(starts and i == 0),
                               stop=stops, skip_group_check=True)
                    r.then_inc(yc_done, 1)
                    if c == n - 1 and p == L1_MOE:
                        pe.wait_ge(rwb_ready, b + 1)
                        for i in range(NT):
                            r = mm(Y[:, i * P:(i + 1) * P], RWB[:, i * P:(i + 1) * P], MB2[:, :], start=False, stop=True, skip_group_check=True)
                        r.then_inc(y_ready, 1)
                    elif c == n - 1:
                        pe.drain().then_inc(y_ready, 1)

                def body(b):
                    first = isinstance(b, int) and b == 0
                    for c in range(n):
                        if c == 0 and not first:
                            down(b - 1, n - 2)
                        up(b, c)
                        if c == 1 and not first:
                            down(b - 1, n - 1)
                        elif c < DOWN_AT:
                            pass
                        elif c == DOWN_AT:
                            down(b, 0)
                            down(b, 1)
                        elif c > DOWN_AT:
                            down(b, c - 2)
                        if first:
                            if c == 0:
                                last_ao(L)
                            if c == 1:
                                last_y(L)
                            if c == XT_AT:
                                xt(LAYERS[L]["phase"], NB - 1, bank[7])
                            if c == LATE_LOGITS_AT:
                                logits(p, NB - 1, bank[7])
                            if p == L1_MOE and c in (LATE_T_AT, LATE_T_AT + 1):
                                gates_t(p, NB - 1, bank[7], c > LATE_T_AT)
                        elif c == XT_AT:
                            if is_last(b):
                                pe.wait_ge(prep_evac, PREP_BASE[AFTER[p]] + PREP_USES[AFTER[p]])
                            xt(p, b - 1, bank[7])
                        if is_last(b) and c in PE_START[p]:
                            prep_pe(AFTER[p], 0, PE_START[p][c])
                for_inner_blocks(pe, body)
                down(NB - 1, n - 2)
                down(NB - 1, n - 1)

            kvr(0)
            pe.wait_ge(ld_x, 48)
            for_inner_blocks(pe, layer0_pe)
            mix_y(NB - 1)
            attention_pe(0)
            moe_pe(L1_MOE)
            attention_pe(1)
            attention_pe(2)
            moe_pe(L2_MOE)
            attention_pe(3)

            def ffn_turn(b):
                pe.wait_ge(fn_ready, b + 1)
                for c in range(4):
                    if c > 1:
                        pe.wait_ge(ft_evac, b * 4 + c - 1)
                    for i in range(NT):
                        r = tr(bank[4 + c % 2][:, i * P:(i + 1) * P], HG[b % 2][:, i, c * P:(c + 1) * P], ident[:, :])
                    r.then_inc(ft_ready, 1)

            def ffn_down(b):
                at_least(pe, y_added, b + NB * LAST)
                for c in range(4):
                    pe.wait_ge(ft_evac, b * 4 + c + 1)
                    for i in range(NT):
                        r = mm(Y[:, i * P:(i + 1) * P], HT2[:, c, i * P:(i + 1) * P], FW2[:, c, :], start=(c == 0 and i == 0), stop=(c == 3),
                               skip_group_check=True)
                r.then_inc(y_ready, 1)

            def ffn_up(b):
                pe.wait_ge(xt_evac, post_index(L3_ATTN, b) + 1)
                for i in range(NT):
                    at_least(pe, fb_ready, (b - 1) * NT + i + 1)
                    mm(bank[i][:, :], blk(XT, b)[:, i * P:(i + 1) * P], FW1[:, :], start=True, stop=True).then_inc(fu_ready, 1)

            scored(3)
            pe.wait_ge(qm_used, 1)
            pe.wait_ge(tern_ready, 1)
            for b in range(NB + 1):
                if b < NB:
                    ffn_up(b)
                if b == 0:
                    last_ao(3)
                    last_y(3)
                if b == 2:
                    xt(L3_ATTN, NB - 1, bank[7])
                if b > 0:
                    ffn_turn(b - 1)
                    ffn_down(b - 1)


def _rotary(interleaved):
    freqs = np.float32(1.0) / np.float32(10000.0) ** (np.arange(0, HD, 2, dtype=np.float32) / np.float32(HD))
    angle = np.arange(T, dtype=np.float32)[None, :] * freqs[:, None].astype(np.float32)
    ch = np.arange(P) % HD
    f = ch // 2 if interleaved else ch % (HD // 2)
    sign = np.where((ch % 2 == 0) if interleaved else (ch < HD // 2), -1.0, 1.0).astype(np.float32)
    return np.stack([np.cos(angle)[f], np.sin(angle)[f] * sign[:, None]]).astype(np.float32)


def _swap(n, interleaved):
    ch = np.arange(n)
    return ch ^ 1 if interleaved else ch ^ (HD // 2)


def kernel(**inputs):
    import ml_dtypes
    import concourse.bacc as bacc
    from concourse.bass_utils import run_bass_kernel_spmd

    a = {k: np.asarray(x) for k, x in inputs.items()}
    c = np.ascontiguousarray
    bf = ml_dtypes.bfloat16
    arrays = {}
    x = a["L0_attn_x"]
    arrays["L0_attn_x"] = c(x)
    arrays["xT"] = c(x.reshape(NB * T, P).T)
    qkv = a["L2_ffn_wqkv"].T
    gq, gk, gv = qkv[:, :P], qkv[:, P:P + 32], qkv[:, P + 32:P + 64]
    l2q, l2k = a["L2_attn_wq"].T, a["L2_attn_wk"].T
    w = {"l0_k": a["L0_attn_Wk"].T, "l0_v": a["L0_attn_Wv"].T, "l0_r": a["L0_attn_Wr"].T, "l0_o": a["L0_attn_Wo"].T,
         "l1_out": a["L1_attn_W_out"].T, "l2_q": l2q, "l2_qs": l2q[:, _swap(P, True)], "l2_k": l2k,
         "l2_ks": l2k[:, _swap(P, True)], "l2_v": a["L2_attn_wv"].T, "l2_o": a["L2_attn_wo"].T,
         "g_q": gq, "g_qs": gq[:, _swap(P, False)], "g_k": gk, "g_ks": gk[:, _swap(32, False)], "g_v": gv,
         "g_o": a["L2_ffn_wo"].T, "l3_q": a["L3_attn_Wq"], "l3_k": a["L3_attn_Wk"], "l3_v": a["L3_attn_Wv"],
         "l3_o": a["L3_attn_Wo"], "l1_gate": a["L1_ffn_gate_w"].T, "l2_gate": a["L2_ffn_gate_w"].T}
    arrays["wpack"] = c(np.concatenate([w[n] for n in W_COLS], axis=1))

    def col(v):
        out = np.zeros((-(-v.size // P) * P,), np.float32)
        out[:v.size] = v.reshape(-1)
        return out.reshape(-1, P).T

    hidden = np.concatenate([a["L1_ffn_b1"].reshape(-1), a["L1_ffn_sb1"]])
    hidden3 = np.concatenate([a["L1_ffn_b3"].reshape(-1), a["L1_ffn_sb3"]])
    cols = {"decay": a["L0_attn_time_decay"], "first": a["L0_attn_time_first"], "mix": a["L0_attn_time_mix"],
            "ln1_w": a["L2_ffn_ln1_w"], "ln2_w": a["L2_ffn_ln2_w"], "bq": a["L3_attn_bq"], "bk": a["L3_attn_bk"],
            "f_ln1_g": a["L3_ffn_ln1_g"], "f_ln1_b": a["L3_ffn_ln1_b"], "f_ln2_g": a["L3_ffn_ln2_g"],
            "f_ln2_b": a["L3_ffn_ln2_b"], "m_b1": hidden, "m_b3": hidden3}
    arrays["cols"] = c(np.concatenate([col(cols[n]) for n in C_COLS], axis=1))
    rows = {"logits": a["L0_ffn_logits"], "u": a["L0_ffn_u"], "l0_b": a["L0_ffn_b"], "gate_b": a["L1_ffn_gate_b"],
            "b_out": a["L1_attn_b_out"], "bv": a["L3_attn_bv"], "bo": a["L3_attn_bo"], "f_b1": a["L3_ffn_b1"], "f_b2": a["L3_ffn_b2"]}
    arrays["rows"] = c(np.concatenate([rows[n].reshape(-1) for n in R_COLS]))
    arrays["L0_ffn_W"] = c(a["L0_ffn_W"])
    for n, k in (("l1_wq", "L1_attn_Wq"), ("l1_wk", "L1_attn_Wk"), ("l1_wv", "L1_attn_Wv")):
        arrays[n] = c(a[k].T)
    arrays["ident"] = np.eye(P, dtype=np.float32)
    arrays["identb"] = np.eye(P).astype(bf)
    arrays["maskb"] = np.where(np.arange(P)[None, :] > np.arange(P)[:, None], MASKED, 0.0).astype(bf)
    arrays["tables"] = c(np.stack([_rotary(True), _rotary(False)]))
    f1 = a["L1_ffn_w1"].shape[2]
    n1 = 13 * P

    def up(we, ws):
        out = np.zeros((P, n1), np.float32)
        out[:, :E * f1] = we.transpose(1, 0, 2).reshape(P, E * f1)
        out[:, E * f1:(E + 1) * f1] = ws
        return out

    arrays["m1_w1"], arrays["m1_w3"] = up(a["L1_ffn_w1"], a["L1_ffn_sw1"]), up(a["L1_ffn_w3"], a["L1_ffn_sw3"])
    w2 = np.zeros((n1, P), np.float32)
    w2[:E * f1] = a["L1_ffn_w2"].reshape(E * f1, P)
    w2[E * f1:(E + 1) * f1] = a["L1_ffn_sw2"]
    arrays["m1_w2"] = c(w2.reshape(13, P, P).transpose(1, 0, 2))
    arrays["m1_b2"] = c(np.concatenate([a["L1_ffn_b2"], a["L1_ffn_sb2"][None]]))
    w13 = a["L2_ffn_w13"]
    f2 = w13.shape[1] // 2
    arrays["m2_w1"] = c(w13[:, :f2].transpose(2, 0, 1).reshape(P, E * f2))
    arrays["m2_w3"] = c(w13[:, f2:].transpose(2, 0, 1).reshape(P, E * f2))
    arrays["m2_w2"] = c(a["L2_ffn_w2"].transpose(0, 2, 1).reshape(16, P, P).transpose(1, 0, 2))
    sel = np.zeros((P, 13, P), np.float32)
    for r in range(NGATE * f1):
        for part in range(PARTS):
            sel[part * NGATE + r // f1, r // P, r % P] = 1.0
    arrays["sel"] = sel.astype(bf)
    arrays["f_w1"] = c(a["L3_ffn_w1"].T)
    arrays["f_w2"] = c(a["L3_ffn_w2"].T.reshape(4, P, P).transpose(1, 0, 2))
    arrays["slopes"] = c(a["L3_attn_slopes"].reshape(H, 1))
    pad = np.zeros((P - STACK, H, T))
    arrays["qpad"] = pad.astype(bf)
    pad[ROWS_SHIFT - STACK:] = 1.0
    arrays["kpad"] = pad.astype(bf)
    pos = np.arange(T)
    kp = np.stack([pos // 256 * 256, pos % 256]).astype(bf)
    arrays["kpos"] = c(np.broadcast_to(np.tile(kp, (PARTS, 1))[:, None, :], (ALIBI, NG, T)))

    nc = bacc.Bacc("TRN2", target_bir_lowering=False, num_devices=1)
    d = {n: nc.dram_tensor("in_" + n, v.shape, mybir.dt.from_np(v.dtype), kind="ExternalInput").ap() for n, v in arrays.items()}
    d["out"] = nc.dram_tensor("out_x", (NB, T, P), F32, kind="ExternalOutput").ap()
    build(nc, d)
    r = run_bass_kernel_spmd(nc, [{"in_" + n: v for n, v in arrays.items()}], core_ids=[0])
    return r.results[0]["out_x"]
```
